# Optimizing a Trainium2 kernel written in Bass

```python
import numpy as np
import jax
import jax.numpy as jnp

def _softmax(x, axis=-1):
    return jax.nn.softmax(x, axis=axis)

def _gelu(x):
    return jax.nn.gelu(x, approximate=True)

def _silu(x):
    return jax.nn.silu(x)

def _sigmoid(x):
    return jax.nn.sigmoid(x)

def _layernorm(x, axis=-1, eps=1e-05):
    m = jnp.mean(x, axis=axis, keepdims=True)
    v = jnp.var(x, axis=axis, keepdims=True)
    return (x - m) / jnp.sqrt(v + eps)

def _scatter_add(tgt, idx, src, axis=0):
    return tgt.at[idx].add(src)

def _segment_sum(src, seg, n):
    return jax.ops.segment_sum(src, seg, n)
kernel_name = 'mk_sandwich_d1_jaxref_r8_bd52fb'

def setup_inputs(seed: int=0):
    np.random.seed(seed)
    _w = jnp.asarray

    def _L0_attn_setup():
        import jax, jax.numpy as jnp
        import numpy as np
        B, S, E, H = (2, 256, 256, 16)
        NOPE, ROPE, VD = (128, 64, 128)
        QH = NOPE + ROPE
        LORA = 64
        ROPE_THETA = 10000.0
        EPS = 1e-06

        def _rope(xp, cos, sin):
            d2 = xp.shape[-1] // 2
            x1, x2 = (xp[..., :d2], xp[..., d2:])
            return jnp.concatenate([x1 * cos - x2 * sin, x2 * cos + x1 * sin], axis=-1)
        key = jax.random.key(seed)
        ks = jax.random.split(key, 5)
        sd = lambda n: 1.0 / np.sqrt(n)
        return {'x': jax.random.normal(ks[0], (B, S, E), jnp.float32), 'wq': jax.random.normal(ks[1], (E, H * QH), jnp.float32) * sd(E), 'wkv_a': jax.random.normal(ks[2], (E, LORA + ROPE), jnp.float32) * sd(E), 'wkv_b': jax.random.normal(ks[3], (LORA, H * (NOPE + VD)), jnp.float32) * sd(LORA), 'wo': jax.random.normal(ks[4], (H * VD, E), jnp.float32) * sd(H * VD), 'kv_norm_scale': jnp.ones((LORA,), jnp.float32)}
    _L0_attn_in = _L0_attn_setup()

    def _L0_ffn_setup():
        import jax, jax.numpy as jnp
        import numpy as np
        B, S, H = (1, 128, 256)
        F = 128
        E = 16
        K = 2
        NS = 1
        ROUTE_SCALE = 1.0
        key = jax.random.key(seed)
        ks = jax.random.split(key, 8)

        def w(k, shape, fan_in):
            return jax.random.normal(k, shape, jnp.float32) * fan_in ** (-0.5)
        return {'hidden_states': jax.random.normal(ks[0], (B, S, H), jnp.float32), 'gate_w': w(ks[1], (H, E), H), 'expert_bias': jnp.zeros((E,), jnp.float32), 'shared_gate_w': w(ks[2], (H, F * NS), H), 'shared_up_w': w(ks[3], (H, F * NS), H), 'shared_down_w': w(ks[4], (F * NS, H), F * NS), 'experts_gate_up': w(ks[5], (E, H, 2 * F), H), 'experts_down': w(ks[6], (E, F, H), F)}
    _L0_ffn_in = _L0_ffn_setup()
    _d = {'L0_attn_x': _L0_attn_in['x'], 'L0_attn_wq': _L0_attn_in['wq'], 'L0_attn_wkv_a': _L0_attn_in['wkv_a'], 'L0_attn_wkv_b': _L0_attn_in['wkv_b'], 'L0_attn_wo': _L0_attn_in['wo'], 'L0_attn_kv_norm_scale': _L0_attn_in['kv_norm_scale'], 'L0_ffn_gate_w': _L0_ffn_in['gate_w'], 'L0_ffn_expert_bias': _L0_ffn_in['expert_bias'], 'L0_ffn_shared_gate_w': _L0_ffn_in['shared_gate_w'], 'L0_ffn_shared_up_w': _L0_ffn_in['shared_up_w'], 'L0_ffn_shared_down_w': _L0_ffn_in['shared_down_w'], 'L0_ffn_experts_gate_up': _L0_ffn_in['experts_gate_up'], 'L0_ffn_experts_down': _L0_ffn_in['experts_down']}
    _x0 = _d['L0_attn_x']
    _d['L0_attn_x'] = jax.random.normal(jax.random.fold_in(jax.random.key(seed), 1), (1, 2048, 256), dtype=_x0.dtype)
    del _x0
    return _d

def reference(L0_attn_x, L0_attn_wq, L0_attn_wkv_a, L0_attn_wkv_b, L0_attn_wo, L0_attn_kv_norm_scale, L0_ffn_gate_w, L0_ffn_expert_bias, L0_ffn_shared_gate_w, L0_ffn_shared_up_w, L0_ffn_shared_down_w, L0_ffn_experts_gate_up, L0_ffn_experts_down):

    def _L0_attn_ref(x, wq, wkv_a, wkv_b, wo, kv_norm_scale):
        import jax, jax.numpy as jnp
        import numpy as np
        B, S, E, H = (2, 256, 256, 16)
        NOPE, ROPE, VD = (128, 64, 128)
        QH = NOPE + ROPE
        LORA = 64
        ROPE_THETA = 10000.0
        EPS = 1e-06

        def _rope(xp, cos, sin):
            d2 = xp.shape[-1] // 2
            x1, x2 = (xp[..., :d2], xp[..., d2:])
            return jnp.concatenate([x1 * cos - x2 * sin, x2 * cos + x1 * sin], axis=-1)
        b, s, _ = x.shape
        q = (x @ wq).reshape(b, s, H, QH).transpose(0, 2, 1, 3)
        q_nope, q_pe = (q[..., :NOPE], q[..., NOPE:])
        kva = x @ wkv_a
        ckv, k_pe = (kva[..., :LORA], kva[..., LORA:])
        ckv = ckv * jax.lax.rsqrt(jnp.mean(ckv * ckv, axis=-1, keepdims=True) + EPS)
        ckv = ckv * kv_norm_scale
        kv = (ckv @ wkv_b).reshape(b, s, H, NOPE + VD).transpose(0, 2, 1, 3)
        k_nope, v = (kv[..., :NOPE], kv[..., NOPE:])
        pos = jnp.arange(s, dtype=jnp.float32)
        inv = 1.0 / ROPE_THETA ** (jnp.arange(0, ROPE, 2, dtype=jnp.float32) / ROPE)
        ang = pos[:, None] * inv
        cos, sin = (jnp.cos(ang), jnp.sin(ang))
        q_pe = _rope(q_pe, cos, sin)
        k_pe = _rope(k_pe[:, None, :, :], cos, sin)
        qs = jnp.concatenate([q_nope, q_pe], axis=-1)
        ks_ = jnp.concatenate([k_nope, jnp.broadcast_to(k_pe, (b, H, s, ROPE))], axis=-1)
        scale = QH ** (-0.5)
        scores = jnp.einsum('bhqd,bhkd->bhqk', qs, ks_) * scale
        causal = jnp.tril(jnp.ones((s, s), dtype=bool))
        scores = jnp.where(causal, scores, jnp.finfo(scores.dtype).min)
        attn = jax.nn.softmax(scores, axis=-1)
        out = jnp.einsum('bhqk,bhkd->bhqd', attn, v)
        out = out.transpose(0, 2, 1, 3).reshape(b, s, H * VD)
        return out @ wo

    def _L0_ffn_ref(hidden_states, gate_w, expert_bias, shared_gate_w, shared_up_w, shared_down_w, experts_gate_up, experts_down):
        import jax, jax.numpy as jnp
        import numpy as np
        B, S, H = (1, 128, 256)
        F = 128
        E = 16
        K = 2
        NS = 1
        ROUTE_SCALE = 1.0
        b, s, h = hidden_states.shape
        x = hidden_states.reshape(-1, h)
        T = x.shape[0]
        router_logits = (x @ gate_w).astype(jnp.float32)
        scores = jax.nn.sigmoid(router_logits)
        _, selected = jax.lax.top_k(scores + expert_bias[None, :], K)
        top_scores = jnp.take_along_axis(scores, selected, axis=1)
        top_scores = top_scores / (top_scores.sum(-1, keepdims=True) + 1e-20)
        top_scores = top_scores * ROUTE_SCALE
        shared = jax.nn.silu(x @ shared_gate_w) * (x @ shared_up_w) @ shared_down_w
        comb = jnp.zeros((T, E), jnp.float32).at[jnp.arange(T)[:, None], selected].add(top_scores)
        routed = jnp.zeros_like(x)
        for e in range(E):
            gu = x @ experts_gate_up[e]
            g, u = jnp.split(gu, 2, axis=-1)
            routed = routed + comb[:, e:e + 1] * (jax.nn.silu(g) * u @ experts_down[e])
        return (shared + routed).reshape(b, s, h)
    x = L0_attn_x
    x = x + _layernorm(_L0_attn_ref(_layernorm(x, axis=-1), L0_attn_wq, L0_attn_wkv_a, L0_attn_wkv_b, L0_attn_wo, L0_attn_kv_norm_scale), axis=-1)
    x = x + _layernorm(_L0_ffn_ref(_layernorm(x, axis=-1), L0_ffn_gate_w, L0_ffn_expert_bias, L0_ffn_shared_gate_w, L0_ffn_shared_up_w, L0_ffn_shared_down_w, L0_ffn_experts_gate_up, L0_ffn_experts_down), axis=-1)
    return x

_drawn_inputs = setup_inputs


def setup_inputs(seed=0):
    import zlib

    import numpy as np

    out = dict(_drawn_inputs(seed))
    spreads = {'L0_attn_kv_norm_scale': (1.0, 0.2), 'L0_ffn_expert_bias': (0.0, 0.1)}
    factors = {}
    for name, (base, spread) in spreads.items():
        noise = np.random.default_rng([zlib.crc32(name.encode()), seed]).standard_normal(out[name].shape)
        drawn = base * np.exp(spread * noise) if base else spread * noise
        out[name] = jnp.asarray(drawn.astype(out[name].dtype))
    for name, factor in factors.items():
        out[name] = (out[name] * factor).astype(out[name].dtype)
    return out
```

```python
from contextlib import ExitStack

import concourse.bass as bass
from concourse import mybir

F32 = mybir.dt.float32
F16 = mybir.dt.float16
BF16 = mybir.dt.bfloat16
U32 = mybir.dt.uint32
ALU = mybir.AluOpType
ACT = mybir.ActivationFunctionType
AX = mybir.AxisListType

P = 128
S, E = 2048, 256
NT = S // P
KE = E // P
H, NOPE, ROPE, VD, LORA = 16, 128, 64, 128, 64
QH = NOPE + ROPE
DK = LORA + ROPE
NP = H // 2
CQ = 512
NC = S // CQ
TC = CQ // P
NE, F = 16, 128
NX = NE + 1
SM_SCALE = float(QH) ** -0.5
LN_EPS, RMS_EPS = 1e-5, 1e-6
WS = 64.0
LAG = 2
ST_RING, MX_RING, P_RING = 4, 2, 8
NEG = -1e30

C_ID, C_COS, C_SIN = 0, P, P + NT * ROPE // 2
C_SEL = C_SIN + NT * ROPE
C_BLK = C_SEL + TC * P
C_IOTA = C_BLK + TC * P
C_END = C_IOTA + NE


def attention_moe(nc, x, wq, wkv_a, wkv_b, wo, kv_scale, gate_w, bias, sh_gate, sh_up, sh_down,
                  ex_gu, ex_down, c32_d, c16_d, out):
    with ExitStack() as ctx:
        def sb(name, shape, dt=F32):
            return ctx.enter_context(nc.sbuf_tensor(name, shape, dt))

        def sem(name):
            return ctx.enter_context(nc.semaphore(name))

        c32 = sb("c32", [P, C_END])
        c16 = sb("c16", [P, 5 * P], BF16)
        kvs = sb("kvs", [P, LORA])
        biasb = sb("biasb", [P, NE])
        xnTh = sb("xnTh", [P, KE, S], F16)
        xnTl = sb("xnTl", [P, KE, S], F16)
        WQh = sb("WQh", [P, KE, H * DK], F16)
        WQl = sb("WQl", [P, KE, H * DK], F16)
        WO = sb("WO", [P, NP, E])
        kv = sb("kv", [P, NT, DK])
        KTh = sb("KTh", [P, S], F16)
        KTl = sb("KTl", [P, S], F16)
        WEh = sb("WEh", [P, NX, KE * 2 * F + E], F16)
        WEl = sb("WEl", [P, NX, KE * 2 * F + E], F16)
        wsm = sb("wsm", [P, KE, DK + NE])
        wsmh = sb("wsmh", [P, KE, DK + NE], F16)
        wsml = sb("wsml", [P, KE, DK + NE], F16)
        st6 = sb("st6", [P, NT, 6])
        mv = sb("mv", [P, NT, 2])
        var = sb("var", [P, NT])
        std = sb("std", [P, NT])
        rstd = sb("rstd", [P, NT])
        mxp = sb("mxp", [P, 2, TC, NC])
        mrow = sb("mrow", [P, 2, TC])
        Lp = sb("Lp", [P, H, CQ // 32])
        rL = sb("rL", [P, H, TC])
        sig = sb("sig", [P, TC, NE])
        sgb = sb("sgb", [P, TC, NE])
        top8 = sb("top8", [P, TC, 8])
        idx8 = sb("idx8", [P, TC, 8], U32)
        idxf = sb("idxf", [P, TC, 8])
        pick = sb("pick", [P, 2, TC, NE])
        rsum = sb("rsum", [P, 2, TC])
        comb = sb("comb", [P, TC, NX])

        A = sb("A", [P, 8192])
        B = sb("B", [P, 4096])
        C = sb("C", [P, 4096])
        D = sb("D", [P, 4608])

        wq_raw = A[:, 0:KE * H * QH].rearrange("p (k h c) -> p k h c", k=KE, h=H)
        wT = A[:, 6144:6144 + 768].rearrange("p (r c) -> p r c", r=2)
        xn = A[:, 6912:6912 + 512].rearrange("p (r c) -> p r c", r=2)
        QTh = A[:, 0:4096].bitcast(F16)
        QTl = A[:, 4096:8192].bitcast(F16)
        xn2h = A[:, 0:512].bitcast(F16).rearrange("p (k t) -> p k t", k=KE)
        xn2l = A[:, 512:1024].bitcast(F16).rearrange("p (k t) -> p k t", k=KE)
        On = A[:, 1024:3072].rearrange("p (r c) -> p r c", r=2)
        OnT = A[:, 3072:5120].rearrange("p (r n c) -> p r n c", r=2, n=NP)
        xr = A[:, 5120:6144].rearrange("p (t e) -> p t e", t=TC)
        x1 = A[:, 6144:7168].rearrange("p (t e) -> p t e", t=TC)
        ysb = A[:, 7168:8192].rearrange("p (t e) -> p t e", t=TC)
        xs = B[:, :].rearrange("p (t e) -> p t e", t=NT)
        Pr = B[:, :].rearrange("p (r q) -> p r q", r=P_RING)
        sg = B[:, 0:512].rearrange("p (r t f) -> p r t f", r=2, t=2)
        hx = B[:, 512:1024].rearrange("p (r t f) -> p r t f", r=2, t=2)
        hh = B[:, 1024:1280].bitcast(F16).rearrange("p (r c) -> p r c", r=2)
        hl = B[:, 1280:1536].bitcast(F16).rearrange("p (r c) -> p r c", r=2)
        lnt = B[:, 2048:3072].rearrange("p (t e) -> p t e", t=TC)
        wkvb_raw = C[:, :].rearrange("p (h c) -> p h c", h=H)
        qs = C[:, 0:2048].rearrange("p (r c) -> p r c", r=4)
        ropA = C[:, 2048:2304].rearrange("p (h c) -> p h c", h=4)
        ropB = C[:, 2304:2560].rearrange("p (h c) -> p h c", h=4)
        OT = C[:, :]
        wo_raw = D[:, 0:4096].rearrange("p (h e) -> p h e", h=H)
        Pacc = D[:, 0:2048].rearrange("p (r s q) -> p r s q", r=2, s=2)
        Dm = D[:, 2048:3072].bitcast(BF16).rearrange("p (r s q) -> p r s q", r=2, s=2)
        stage = D[:, 3072:4608].rearrange("p (r c) -> p r c", r=2)
        kvt = WEl[:, 0:6, :].rearrange("p a b -> p (a b)")
        kvtA = kvt[:, 0:2048].bitcast(F32).rearrange("p (t c) -> p t c", t=NT)
        kvtB = kvt[:, 2048:4096].bitcast(F32).rearrange("p (t c) -> p t c", t=NT)

        ident = c32[:, C_ID:C_ID + P]
        cosT = c32[:, C_COS:C_SIN].rearrange("p (t c) -> p t c", t=NT)
        sinT = c32[:, C_SIN:C_SEL].rearrange("p (t c) -> p t c", t=NT)
        selL = c32[:, C_SEL:C_BLK].rearrange("p (b m) -> p b m", b=TC)
        negblk = c32[0:TC, C_BLK:C_IOTA].rearrange("p (j q) -> p j q", j=TC)
        iota = c32[:, C_IOTA:C_END]
        identb, mask_qk, mask_kq, ones4, zerob = (c16[:, i * P:(i + 1) * P] for i in range(5))

        ps = ctx.enter_context(nc.psum_tensor("ps", [P, 8, 512], F32))
        BK_O, BK_M = 6, 7

        in_const, in_x, in_wa, in_wq, in_wkvb, in_wo = map(sem, (
            "in_const", "in_x", "in_wa", "in_wq", "in_wkvb", "in_wo"))
        stats_done, var_ready, std_ready = map(sem, ("stats_done", "var_ready", "std_ready"))
        xn_ready, xt_ready, xh_done, xl_done = map(sem, ("xn_ready", "xt_ready", "xh_done", "xl_done"))
        kva_ready, kva_done = map(sem, ("kva_ready", "kva_done"))
        kfin_ready, kt_ready, kh_done, kl_done = map(sem, ("kfin_ready", "kt_ready", "kh_done", "kl_done"))
        wt_ready, wt_done, wf_ready, wfh_done, wfl_done = map(sem, (
            "wt_ready", "wt_done", "wf_ready", "wfh_done", "wfl_done"))
        small_hi, small_lo, pe_hi, pe_lo = map(sem, ("small_hi", "small_lo", "pe_hi", "pe_lo"))
        dve_seq = sem("dve_seq")
        dm_zero = sem("dm_zero")
        q_ready, q_done, rope_mul, rope_done, qt_ready, qh_done, ql_done = map(sem, (
            "q_ready", "q_done", "rope_mul", "rope_done", "qt_ready", "qh_done", "ql_done"))
        mx_ready, mx_free, m_ready, mt_ready, d_ready = map(sem, (
            "mx_ready", "mx_free", "m_ready", "mt_ready", "d_ready"))
        st_ready, exp_done, pv_done, sum_done, l_done, o_free = map(sem, (
            "st_ready", "exp_done", "pv_done", "sum_done", "l_done", "o_free"))
        raw_gu_in = [sem(f"raw_gu_in_{r}") for r in range(2)]
        raw_dn_in = [sem(f"raw_dn_in_{r}") for r in range(2)]
        shared_in, raw_hi, raw_lo = map(sem, ("shared_in", "raw_hi", "raw_lo"))
        den_ready, rl_ready, t1_ready, on_ready, t2_ready, ont_ready, mo_ready, ysb_ready = map(sem, (
            "den_ready", "rl_ready", "t1_ready", "on_ready", "t2_ready", "ont_ready", "mo_ready", "ysb_ready"))
        xr_in, xn2_ready, xt2_ready, x2h_done, x2l_done = map(sem, (
            "xr_in", "xn2_ready", "xt2_ready", "x2h_done", "x2l_done"))
        log_ready, sig_ready, comb_ready = map(sem, ("log_ready", "sig_ready", "comb_ready"))
        gu_ready, silu_done, h_ready, ht_ready, hh_done, hl_done, dn_done, y_ready, y_done = map(sem, (
            "gu_ready", "silu_done", "h_ready", "ht_ready", "hh_done", "hl_done", "dn_done", "y_ready", "y_done"))
        out_ready, out_done = map(sem, ("out_ready", "out_done"))

        CR_EXP, CR_PV, CR_SUM, CR_MX, CR_L, CR_O, CR = ST_RING, P_RING, P_RING, MX_RING, 2, 1, 2

        def units(qc):
            return 2 * TC * (qc + 1)

        def first_unit(qc):
            return sum(NP * units(q) for q in range(qc))

        STEPS = 2 * NX
        x_tiles = x.rearrange("b (t p) e -> p (b t) e", p=P)
        out_tiles = out.rearrange("b (t p) e -> p (b t) e", p=P)
        gu_d = ex_gu.rearrange("e (k p) f -> e p k f", p=P)

        block = ctx.enter_context(nc.Block())

        @block.sync
        def _(sp):
            sp.dma_start(xs[:, 0:8, :], x_tiles[:, 0:8, :]).then_inc(in_x, 16)
            sp.dma_start(xs[:, 8:16, :], x_tiles[:, 8:16, :]).then_inc(in_x, 16)
            sp.dma_start(wq_raw, wq.rearrange("(k p) (h c) -> p k h c", p=P, c=QH)).then_inc(in_wq, 16)
            sp.dma_start(wo_raw, wo.rearrange("(h p) e -> p h e", p=P)).then_inc(in_wo, 16)

            def load_expert(e, r):
                sp.wait_ge(raw_lo, e + 1)
                sp.dma_start(stage[:, r, 0:KE * 2 * F].rearrange("p (k f) -> p k f", k=KE),
                             gu_d[e]).then_inc(raw_gu_in[r], 16)
                sp.dma_start(stage[:, r, KE * 2 * F:], ex_down[e]).then_inc(raw_dn_in[r], 16)

            sp.wait_ge(wf_ready, H)
            with sp.Fori(0, NE // 2) as i:
                for r in range(2):
                    load_expert(2 * i + r, r)
            sp.wait_ge(raw_lo, NE + 1)
            for k in range(KE):
                c = k * 2 * F
                sp.dma_start(stage[:, 0, c:c + F], sh_gate[k * P:(k + 1) * P, :]).then_inc(shared_in, 16)
                sp.dma_start(stage[:, 0, c + F:c + 2 * F], sh_up[k * P:(k + 1) * P, :]).then_inc(shared_in, 16)
            sp.dma_start(stage[:, 0, KE * 2 * F:], sh_down).then_inc(shared_in, 16)

            for qc in range(NC):
                sp.wait_ge(st_ready, first_unit(qc + 1))
                sp.dma_start(xr, x_tiles[:, qc * TC:(qc + 1) * TC, :]).then_inc(xr_in, 16)
                sp.wait_ge(out_ready, qc + 1)
                sp.dma_start(out_tiles[:, qc * TC:(qc + 1) * TC, :], lnt).then_inc(out_done, 16)
            sp.wait_ge(out_done, 16 * NC)

        @block.gpsimd
        def _(pool):
            def add_up(qc, p, half):
                KT = TC * (qc + 1)
                n0 = first_unit(qc) + p * units(qc)
                pool.wait_ge(l_done, qc * NP + p + 1)
                for kt in range(1, KT):
                    c0 = max(kt - TC * qc, 0) * P
                    for s in range(2):
                        n, i = n0 + 2 * kt + s, 2 * kt + s
                        pool.wait_ge(exp_done, CR_EXP + n + 1)
                        acc = Pacc[:, half, s, :]
                        if kt == 1:
                            ins = nc.gpsimd.tensor_tensor(acc[:, c0:], Pr[:, s, c0:], Pr[:, i, c0:], ALU.add)
                            if c0:
                                ins = nc.gpsimd.tensor_copy(acc[:, 0:c0], Pr[:, s, 0:c0])
                            ins.then_inc(sum_done, 1 + 2 * s)
                        else:
                            pool.wait_ge(sum_done, CR_SUM + n - 1)
                            nc.gpsimd.tensor_tensor(acc[:, c0:], acc[:, c0:], Pr[:, i % P_RING, c0:],
                                                    ALU.add).then_inc(sum_done, 1)

            for qc in range(NC):
                with pool.Fori(0, NP // 2) as i:
                    add_up(qc, 2 * i, 0)
                    add_up(qc, 2 * i + 1, 1)

        @block.scalar
        def _(act):
            act.dma_start(c32[:, :], c32_d).then_inc(in_const, 16)
            act.dma_start(c16[:, :], c16_d.bitcast(BF16)).then_inc(in_const, 16)
            act.dma_start(wsm[:, :, 0:DK], wkv_a.rearrange("(k p) c -> p k c", p=P)).then_inc(in_wa, 16)
            act.dma_start(wsm[:, :, DK:], gate_w.rearrange("(k p) c -> p k c", p=P)).then_inc(in_wa, 16)
            act.dma_start(kvs[:, :], kv_scale.rearrange("(a c) -> a c", a=1).broadcast_to([P, LORA])).then_inc(in_wa, 16)
            act.dma_start(biasb[:, :], bias.rearrange("(a c) -> a c", a=1).broadcast_to([P, NE])).then_inc(in_wa, 16)
            act.dma_start(wkvb_raw[0:LORA], wkv_b.rearrange("c (h n) -> c h n", h=H)).then_inc(in_wkvb, 16)

            def copy(dst, src, scale=1.0):
                return nc.scalar.activation(dst, src, ACT.Copy, scale=scale)

            act.wait_ge(in_wa, 64)
            copy(wsmh[:, :, :], wsm[:, :, :], WS).then_inc(small_hi, 1)
            act.wait_ge(var_ready, 1)
            nc.scalar.activation(std[:, :], var[:, :], ACT.Sqrt).then_inc(std_ready, 1)

            for t in range(NT + 1):
                if t < NT:
                    act.wait_ge(xt_ready, t + 1)
                    copy(xnTh[:, :, t * P:(t + 1) * P],
                         ps[:, t % 2, 0:E].rearrange("p (k c) -> p k c", k=KE)).then_inc(xh_done, 1)
                if t > 0:
                    act.wait_ge(kva_ready, t)
                    copy(kv[:, t - 1, :], ps[:, 2 + (t - 1) % 2, 0:DK], 1 / WS).then_inc(kva_done, 1)
            act.wait_ge(var_ready, 2)
            nc.scalar.activation(std[:, :], var[:, :], ACT.Sqrt).then_inc(std_ready, 1)
            for g in range(NT // TC):
                act.wait_ge(kt_ready, g + 1)
                copy(KTh[:, g * CQ:(g + 1) * CQ], ps[:, g, :]).then_inc(kh_done, 1)

            act.wait_ge(in_wq, 16)
            copy(WQh[:, :, :].rearrange("p k (h c) -> p (k h) c", c=DK)[:, :, LORA:],
                 wq_raw.rearrange("p k h c -> p (k h) c")[:, :, NOPE:], WS).then_inc(pe_hi, 1)
            for h in range(H + 1):
                if h < H:
                    act.wait_ge(wt_ready, h + 1)
                    if h >= 2:
                        act.wait_ge(wf_ready, h - 1)
                    copy(wT[:, h % 2, :], ps[:, 4 + h % 2, 0:384]).then_inc(wt_done, 1)
                if h > 0:
                    g = h - 1
                    act.wait_ge(wf_ready, g + 1)
                    o = LORA * (g % 2)
                    copy(WO[o:o + LORA, g // 2, :], ps[o:o + LORA, 6 + g % 2, 128:384])
                    copy(WQh[:, :, g * DK:g * DK + LORA],
                         ps[:, 6 + g % 2, 0:128].rearrange("p (k c) -> p k c", k=KE), WS).then_inc(wfh_done, 1)

            def scores_to_probs(qc, p):
                KT = TC * (qc + 1)
                n0 = first_unit(qc) + p * units(qc)
                for i in range(2 * KT):
                    n = n0 + i
                    c0 = max(i // 2 - TC * qc, 0) * P
                    act.wait_ge(st_ready, n + 1)
                    act.wait_ge(pv_done, n + 1)
                    act.wait_ge(sum_done, n + 1)
                    nc.scalar.activation(Pr[:, i % P_RING, c0:], ps[:, i % ST_RING, c0:], ACT.Exp,
                                         scale=SM_SCALE).then_inc(exp_done, 1)
                act.wait_ge(pv_done, CR_PV + n0 + 2 * KT)
                copy(OT[:, bass.ds(p * CQ, CQ)], ps[:, BK_O, :]).then_inc(o_free, 1)
                if qc == 0:
                    for r in range(2):
                        cut_expert(p, r)

            def cut_expert(p, r):
                e = 2 * p + r
                act.wait_ge(raw_gu_in[r], (p + 1) * 16)
                act.wait_ge(raw_dn_in[r], (p + 1) * 16)
                copy(WEh[:, e, :], stage[:, r, :], WS).then_inc(raw_hi, 1)

            for qc in range(NC):
                if qc == 0:
                    act.wait_ge(pe_lo, 1)
                    act.wait_ge(wfl_done, H)
                def q_out(tile, g):
                    n = qc * NT + tile * 4 + g
                    act.wait_ge(q_ready, n + 1)
                    copy(qs[:, g, :], ps[:, g % 2, :], 1 / WS).then_inc(q_done, 1)

                def q_high(tile, g):
                    n = qc * NT + tile * 4 + g
                    act.wait_ge(qt_ready, n + 1)
                    dst = QTh.rearrange("p (h q) -> p h q", h=H)[:, 4 * g:4 * g + 4, bass.ds(tile * P, P)]
                    copy(dst, ps[:, 2 + g % 2, :].rearrange("p (h q) -> p h q", h=4)).then_inc(qh_done, 1)

                q_out(0, 0)
                with act.Fori(0, TC - 1) as i:
                    for g in range(1, 5):
                        q_out(i + g // 4, g % 4)
                        q_high(i, g - 1)
                for g in range(1, 4):
                    q_out(TC - 1, g)
                    q_high(TC - 1, g - 1)
                q_high(TC - 1, 3)

                if qc:
                    act.wait_ge(out_done, 16 * qc)
                with act.Fori(0, NP) as p:
                    scores_to_probs(qc, p)
                if qc == 0:
                    act.wait_ge(shared_in, 80)
                    copy(WEh[:, NE, :], stage[:, 0, :], WS).then_inc(raw_hi, 1)

                for j in range(TC):
                    for b in range(2):
                        act.wait_ge(t2_ready, (qc * TC + j) * 2 + b + 1)
                        copy(OnT[:, j % 2, 4 * b:4 * b + 4, :],
                             ps[:, 2 + b, :].rearrange("p (n q) -> p n q", n=4)).then_inc(ont_ready, 1)
                    act.wait_ge(mo_ready, qc * TC + j + 1)
                    copy(ysb[:, j, :], ps[:, 4 + j % 2, 0:E]).then_inc(ysb_ready, 1)
                for r in range(2):
                    act.wait_ge(var_ready, 2 + qc * 3 + r + 1)
                    nc.scalar.activation(std[:, 0:TC], var[:, 0:TC], ACT.Sqrt).then_inc(std_ready, 1)
                for k in range(KE):
                    act.wait_ge(xt2_ready, qc * KE + k + 1)
                    copy(xn2h[:, k, :], ps[:, k, :]).then_inc(x2h_done, 1)
                act.wait_ge(log_ready, qc + 1)
                nc.scalar.activation(sig[:, :, :].rearrange("p t e -> p (t e)"), ps[:, 6, 0:TC * NE],
                                     ACT.Sigmoid, scale=1 / WS).then_inc(sig_ready, 1)

                def silu(n, r):
                    act.wait_ge(gu_ready, n + 1)
                    act.wait_ge(h_ready, n + 1)
                    nc.scalar.activation(sg[:, r], ps[:, r, :].rearrange("p (t f) -> p t f", t=2)[:, :, 0:F],
                                         ACT.Silu, scale=1 / WS).then_inc(silu_done, 1)

                def h_high(n, r):
                    act.wait_ge(ht_ready, CR + n + 1)
                    act.wait_ge(dn_done, n + 1)
                    copy(hh[:, r, :], ps[:, 2 + r, 0:E]).then_inc(hh_done, 1)

                n0 = qc * STEPS
                silu(n0, 0)
                silu(n0 + 1, 1)
                h_high(n0, 0)
                with act.Fori(1, NX) as e:
                    silu(n0 + 2 * e, 0)
                    h_high(n0 + 2 * e - 1, 1)
                    silu(n0 + 2 * e + 1, 1)
                    h_high(n0 + 2 * e, 0)
                h_high(n0 + STEPS - 1, 1)
                act.wait_ge(y_ready, qc + 1)
                for b in range(2):
                    copy(ysb[:, 2 * b:2 * b + 2, :].rearrange("p t e -> p (t e)"), ps[:, 4 + b, :],
                         1 / WS).then_inc(y_done, 1)
                act.wait_ge(var_ready, 2 + qc * 3 + 3)
                nc.scalar.activation(std[:, 0:TC], var[:, 0:TC], ACT.Sqrt).then_inc(std_ready, 1)

        @block.vector
        def _(dve):
            steps = [0]

            def link(ins):
                steps[0] += 1
                ins.then_inc(dve_seq, 1)
                dve.wait_ge(dve_seq, steps[0])

            V = nc.vector

            V.memset(mxp[:, 0, 0, 0:1], 0.0).then_inc(exp_done, CR_EXP)
            V.memset(mxp[:, 0, 0, 1:2], 0.0).then_inc(pv_done, CR_PV)
            V.memset(mxp[:, 0, 0, 2:3], 0.0).then_inc(sum_done, CR_SUM)
            V.memset(mxp[:, 0, 0, 3:4], 0.0).then_inc(mx_free, CR_MX)
            V.memset(mxp[:, 0, 1, 0:1], 0.0).then_inc(l_done, CR_L)
            V.memset(mxp[:, 0, 1, 1:2], 0.0).then_inc(o_free, CR_O)
            V.memset(mxp[:, 0, 1, 2:3], 0.0).then_inc(raw_lo, 2)
            for i, two_slots in enumerate((q_done, ql_done, h_ready, ht_ready, hl_done, dn_done)):
                V.memset(mxp[:, 1, i // NC, i % NC:i % NC + 1], 0.0).then_inc(two_slots, CR)

            dve.wait_ge(small_hi, 1)
            V.scalar_tensor_tensor(out=wsml[:, :, :], in0=wsm[:, :, :], scalar=WS, in1=wsmh[:, :, :],
                                   op0=ALU.mult, op1=ALU.subtract).then_inc(small_lo, 1)

            roots = [0]

            def inv_std(n, eps, scale=1.0, src=None):
                src = mv[:, 0:n, 1] if src is None else src
                V.tensor_scalar(var[:, 0:n], src, scale, eps, ALU.mult, ALU.add).then_inc(var_ready, 1)
                roots[0] += 1
                dve.wait_ge(std_ready, roots[0])
                link(V.reciprocal(rstd[:, 0:n], std[:, 0:n]))

            def moments(src, n):
                for t in range(n):
                    ins = V.bn_stats(st6[:, t, :], src[:, t, :])
                link(ins)
                for t in range(n):
                    ins = V.bn_aggr(mv[:, t, :], st6[:, t, :])
                link(ins)

            dve.wait_ge(in_x, 32)
            moments(xs, NT)
            inv_std(NT, LN_EPS)

            def normalise(t):
                if t >= 2:
                    dve.wait_ge(xt_ready, t - 1)
                V.tensor_scalar(xn[:, t % 2, :], xs[:, t, :], mv[:, t, 0:1], rstd[:, t:t + 1],
                                ALU.subtract, ALU.mult).then_inc(xn_ready, 1)

            normalise(0)
            normalise(1)
            for t in range(NT):
                dve.wait_ge(xh_done, t + 1)
                V.tensor_tensor(xnTl[:, :, t * P:(t + 1) * P],
                                ps[:, t % 2, 0:E].rearrange("p (k c) -> p k c", k=KE),
                                xnTh[:, :, t * P:(t + 1) * P], ALU.subtract).then_inc(xl_done, 1)
                if t + 2 < NT:
                    normalise(t + 2)

            dve.wait_ge(kva_done, NT)
            dve.wait_ge(in_const, 32)
            lat, kpe = kv[:, :, 0:LORA], kv[:, :, LORA:DK]
            HR = ROPE // 2
            link(V.tensor_tensor(kvtA, lat, lat, ALU.mult))
            link(V.tensor_reduce(rsumk := mv[:, :, 0], kvtA, AX.X, ALU.add))
            inv_std(NT, RMS_EPS, 1.0 / LORA, rsumk)
            link(V.tensor_tensor(lat, lat, rstd[:, :].unsqueeze(2).broadcast_to([P, NT, LORA]), ALU.mult))
            V.tensor_tensor(lat, lat, kvs[:, :].unsqueeze(1).broadcast_to([P, NT, LORA]), ALU.mult)
            V.tensor_tensor(kvtA[:, :, 0:HR], kpe[:, :, 0:HR], cosT, ALU.mult)
            V.tensor_tensor(kvtA[:, :, HR:], kpe[:, :, HR:], cosT, ALU.mult)
            V.tensor_tensor(kvtB[:, :, 0:HR], kpe[:, :, HR:], sinT[:, :, 0:HR], ALU.mult)
            link(V.tensor_tensor(kvtB[:, :, HR:], kpe[:, :, 0:HR], sinT[:, :, HR:], ALU.mult))
            V.tensor_tensor(kpe, kvtA, kvtB, ALU.add).then_inc(kfin_ready, 1)
            for g in range(NT // TC):
                dve.wait_ge(kh_done, g + 1)
                V.tensor_tensor(KTl[:, g * CQ:(g + 1) * CQ], ps[:, g, :], KTh[:, g * CQ:(g + 1) * CQ],
                                ALU.subtract).then_inc(kl_done, 1)

            dve.wait_ge(pe_hi, 1)
            V.scalar_tensor_tensor(
                out=WQl[:, :, :].rearrange("p k (h c) -> p (k h) c", c=DK)[:, :, LORA:],
                in0=wq_raw.rearrange("p k h c -> p (k h) c")[:, :, NOPE:], scalar=WS,
                in1=WQh[:, :, :].rearrange("p k (h c) -> p (k h) c", c=DK)[:, :, LORA:],
                op0=ALU.mult, op1=ALU.subtract).then_inc(pe_lo, 1)
            for g in range(H):
                dve.wait_ge(wfh_done, g + 1)
                V.scalar_tensor_tensor(
                    out=WQl[:, :, g * DK:g * DK + LORA],
                    in0=ps[:, 6 + g % 2, 0:128].rearrange("p (k c) -> p k c", k=KE), scalar=WS,
                    in1=WQh[:, :, g * DK:g * DK + LORA],
                    op0=ALU.mult, op1=ALU.subtract).then_inc(wfl_done, 1)
            dve.wait_ge(wf_ready, H)
            V.memset(D[:, 2048:3072], 0.0).then_inc(dm_zero, 1)
            dve.wait_ge(dm_zero, 1)

            def rotate(qc, tile, g):
                n = qc * NT + tile * 4 + g
                dve.wait_ge(q_done, CR + n + 1)
                if not isinstance(n, int) or n:
                    dve.wait_ge(rope_done, n)
                pe4 = qs[:, g, :].rearrange("p (h c) -> p h c", c=DK)[:, :, LORA:]
                t = qc * TC + tile
                cosr = cosT[:, t, :].unsqueeze(1).broadcast_to([P, 4, HR])
                sinl = sinT[:, t, 0:HR].unsqueeze(1).broadcast_to([P, 4, HR])
                sinr = sinT[:, t, HR:].unsqueeze(1).broadcast_to([P, 4, HR])
                V.tensor_tensor(ropA[:, :, 0:HR], pe4[:, :, 0:HR], cosr, ALU.mult)
                V.tensor_tensor(ropA[:, :, HR:], pe4[:, :, HR:], cosr, ALU.mult)
                V.tensor_tensor(ropB[:, :, 0:HR], pe4[:, :, HR:], sinl, ALU.mult)
                V.tensor_tensor(ropB[:, :, HR:], pe4[:, :, 0:HR], sinr, ALU.mult).then_inc(rope_mul, 1)
                dve.wait_ge(rope_mul, n + 1)
                V.tensor_tensor(pe4, ropA, ropB, ALU.add).then_inc(rope_done, 1)

            def q_low(qc, tile, g):
                n = qc * NT + tile * 4 + g
                dve.wait_ge(qh_done, n + 1)
                dst = [t.rearrange("p (h q) -> p h q", h=H)[:, 4 * g:4 * g + 4, bass.ds(tile * P, P)]
                       for t in (QTh, QTl)]
                V.tensor_tensor(dst[1], ps[:, 2 + g % 2, :].rearrange("p (h q) -> p h q", h=4), dst[0],
                                ALU.subtract).then_inc(ql_done, 1)

            def maxima(qc, p):
                U = units(qc)
                n0 = first_unit(qc) + p * U

                def subtrahend(s):
                    k = (qc * NP + p) * 2 + s
                    dve.wait_ge(mt_ready, k + 1)
                    rows = ps[0:TC, BK_M, s * P:(s + 1) * P].unsqueeze(1).broadcast_to([TC, TC, P])
                    V.tensor_tensor(Dm[0:TC, p % 2, s, :].rearrange("p (j q) -> p j q", j=TC), rows, negblk,
                                    ALU.mult).then_inc(d_ready, 1)

                def row_max(s):
                    dve.wait_ge(mx_free, CR_MX + n0 + (s + 1) * U // 2)
                    V.tensor_reduce(mrow[:, s, :], mxp[:, s, :, 0:qc + 1], AX.X, ALU.max).then_inc(m_ready, 1)

                for j in range(U):
                    s, i4, kc = j // (U // 2), j % (U // 2) // (qc + 1), j % (qc + 1)
                    w = CQ if kc < qc else P * (i4 + 1)
                    dve.wait_ge(mx_ready, n0 + j + 1)
                    V.tensor_reduce(mxp[:, s, i4, kc:kc + 1], ps[:, 4 + j % MX_RING, 0:w], AX.X,
                                    ALU.max).then_inc(mx_free, 1)
                    if j == U // 2 - 1:
                        row_max(0)
                    if j == U // 2 + 2:
                        subtrahend(0)
                row_max(1)
                subtrahend(1)

            def part_sums(qc, p):
                dve.wait_ge(sum_done, CR_SUM + first_unit(qc) + (p + 1) * units(qc))
                V.tensor_reduce(Lp[:, bass.ds(2 * p, 2), :],
                                Pacc[:, p % 2].rearrange("p s (b c) -> p s b c", c=32),
                                AX.X, ALU.add, apply_transpose=True).then_inc(l_done, 1)

            def cut_expert(p, r):
                e = 2 * p + r
                dve.wait_ge(raw_hi, e + 1)
                V.scalar_tensor_tensor(out=WEl[:, e, :], in0=stage[:, r, :], scalar=WS, in1=WEh[:, e, :],
                                       op0=ALU.mult, op1=ALU.subtract).then_inc(raw_lo, 1)

            for qc in range(NC):
                rotate(qc, 0, 0)
                with dve.Fori(0, TC - 1) as i:
                    for g in range(1, 5):
                        rotate(qc, i + g // 4, g % 4)
                        q_low(qc, i, g - 1)
                for g in range(1, 4):
                    rotate(qc, TC - 1, g)
                    q_low(qc, TC - 1, g - 1)
                q_low(qc, TC - 1, 3)

                maxima(qc, 0)
                with dve.Fori(0, NP - 1) as p:
                    maxima(qc, p + 1)
                    part_sums(qc, p)
                    if qc == 0:
                        for r in range(2):
                            cut_expert(p, r)
                part_sums(qc, NP - 1)
                if qc == 0:
                    for r in range(2):
                        cut_expert(NP - 1, r)
                    dve.wait_ge(raw_hi, NX)
                    V.scalar_tensor_tensor(out=WEl[:, NE, :], in0=stage[:, 0, :], scalar=WS, in1=WEh[:, NE, :],
                                           op0=ALU.mult, op1=ALU.subtract).then_inc(raw_lo, 1)

                dve.wait_ge(den_ready, qc + 1)
                link(V.reciprocal(rL[:, :, :].rearrange("p h j -> p (h j)"), ps[:, BK_M, 0:H * TC]))
                for j in range(TC):
                    for b in range(2):
                        dve.wait_ge(t1_ready, (qc * TC + j) * 2 + b + 1)
                        if j >= 2:
                            dve.wait_ge(t2_ready, (qc * TC + j - 1) * 2)
                        V.tensor_tensor(On[:, j % 2, 512 * b:512 * b + 512].rearrange("p (h c) -> p h c", c=LORA),
                                        ps[:, b, :].rearrange("p (h c) -> p h c", c=LORA),
                                        rL[:, 8 * b:8 * b + 8, j:j + 1].broadcast_to([P, 8, LORA]),
                                        ALU.mult).then_inc(on_ready, 1)

                def layer_norm(src, dst, done=None):
                    moments(src, TC)
                    inv_std(TC, LN_EPS)
                    for j in range(TC):
                        ins = V.tensor_scalar(dst[:, j, :], src[:, j, :], mv[:, j, 0:1], rstd[:, j:j + 1],
                                              ALU.subtract, ALU.mult)
                    if done is None:
                        link(ins)
                    else:
                        ins.then_inc(done, 1)

                dve.wait_ge(ysb_ready, (qc + 1) * TC)
                layer_norm(ysb, lnt)
                dve.wait_ge(xr_in, 16 * (qc + 1))
                link(V.tensor_tensor(x1, xr, lnt, ALU.add))
                layer_norm(x1, lnt, xn2_ready)
                for k in range(KE):
                    dve.wait_ge(x2h_done, qc * KE + k + 1)
                    V.tensor_tensor(xn2l[:, k, :], ps[:, k, :], xn2h[:, k, :], ALU.subtract).then_inc(x2l_done, 1)

                dve.wait_ge(sig_ready, qc + 1)
                link(V.tensor_tensor(sgb[:, :, :], sig[:, :, :],
                                     biasb[:, :].unsqueeze(1).broadcast_to([P, TC, NE]), ALU.add))
                for j in range(TC):
                    ins = V.max(top8[:, j, :], sgb[:, j, :])
                link(ins)
                for j in range(TC):
                    ins = V.max_index(idx8[:, j, :], top8[:, j, :], sgb[:, j, :])
                link(ins)
                link(V.tensor_copy(idxf[:, :, :], idx8[:, :, :]))
                iota4 = iota.unsqueeze(1).broadcast_to([P, TC, NE])
                V.tensor_tensor(pick[:, 0], iota4, idxf[:, :, 0:1].broadcast_to([P, TC, NE]), ALU.is_equal)
                link(V.tensor_tensor(pick[:, 1], iota4, idxf[:, :, 1:2].broadcast_to([P, TC, NE]), ALU.is_equal))
                link(V.tensor_tensor(pick[:, 0], pick[:, 0], pick[:, 1], ALU.add))
                link(V.tensor_tensor(pick[:, 0], pick[:, 0], sig[:, :, :], ALU.mult))
                link(V.tensor_reduce(rsum[:, 0, :], pick[:, 0], AX.X, ALU.add))
                link(V.tensor_scalar(rsum[:, 0, :], rsum[:, 0, :], 1e-20, None, ALU.add))
                link(V.reciprocal(rsum[:, 1, :], rsum[:, 0, :]))
                V.memset(comb[:, :, NE:NX], 1 / WS)
                V.scalar_tensor_tensor(out=comb[:, :, 0:NE], in0=pick[:, 0], scalar=1 / WS,
                                       in1=rsum[:, 1, :].unsqueeze(2).broadcast_to([P, TC, NE]),
                                       op0=ALU.mult, op1=ALU.mult).then_inc(comb_ready, 1)
                dve.wait_ge(comb_ready, qc + 1)

                def product(n, r, e):
                    dve.wait_ge(silu_done, n + 1)
                    dve.wait_ge(ht_ready, n + 1)
                    for t in range(2):
                        ins = V.scalar_tensor_tensor(
                            out=hx[:, r, t, :], in0=ps[:, r, 256 * t + F:256 * t + 2 * F],
                            scalar=comb[:, 2 * r + t, bass.ds(e, 1)], in1=sg[:, r, t, :],
                            op0=ALU.mult, op1=ALU.mult)
                    ins.then_inc(h_ready, 1)

                def h_low(n, r):
                    dve.wait_ge(hh_done, n + 1)
                    V.tensor_tensor(hl[:, r, :], ps[:, 2 + r, 0:E], hh[:, r, :], ALU.subtract).then_inc(hl_done, 1)

                n0 = qc * STEPS
                product(n0, 0, 0)
                product(n0 + 1, 1, 0)
                h_low(n0, 0)
                with dve.Fori(1, NX) as e:
                    product(n0 + 2 * e, 0, e)
                    h_low(n0 + 2 * e - 1, 1)
                    product(n0 + 2 * e + 1, 1, e)
                    h_low(n0 + 2 * e, 0)
                h_low(n0 + STEPS - 1, 1)

                dve.wait_ge(y_done, 2 * (qc + 1))
                layer_norm(ysb, lnt)
                V.tensor_tensor(lnt, lnt, x1, ALU.add).then_inc(out_ready, 1)

        @block.tensor
        def _(pe):
            T = nc.tensor

            def three(dst, ah, al, bh, bl, first=True, last=True):
                T.matmul(dst, ah, bh, start=first, stop=False)
                T.matmul(dst, ah, bl, start=False, stop=False)
                return T.matmul(dst, al, bh, start=False, stop=last)

            pe.wait_ge(in_const, 32)
            pe.wait_ge(small_lo, 1)
            for t in range(NT + 1):
                if t < NT:
                    pe.wait_ge(xn_ready, t + 1)
                    if t >= 2:
                        pe.wait_ge(xl_done, t - 1)
                    for k in range(KE):
                        ins = T.transpose(ps[:, t % 2, k * P:(k + 1) * P], xn[:, t % 2, k * P:(k + 1) * P], ident)
                    ins.then_inc(xt_ready, 1)
                if t > 0:
                    u = t - 1
                    pe.wait_ge(xl_done, u + 1)
                    if u >= 2:
                        pe.wait_ge(kva_done, u - 1)
                    for k in range(KE):
                        tok = slice(u * P, (u + 1) * P)
                        ins = three(ps[:, 2 + u % 2, 0:DK], xnTh[:, k, tok], xnTl[:, k, tok],
                                    wsmh[:, k, 0:DK], wsml[:, k, 0:DK], k == 0, k == KE - 1)
                    ins.then_inc(kva_ready, 1)
            pe.wait_ge(kfin_ready, 1)
            for t in range(NT):
                ins = T.transpose(ps[:, t // TC, t % TC * P:(t % TC + 1) * P], kv[:, t, :], ident)
                if t % TC == TC - 1:
                    ins.then_inc(kt_ready, 1)

            pe.wait_ge(in_wq, 16)
            pe.wait_ge(in_wkvb, 16)
            pe.wait_ge(in_wo, 16)
            for h in range(H + 1):
                if h < H:
                    if h >= 2:
                        pe.wait_ge(wt_done, h - 1)
                    b = 4 + h % 2
                    for k in range(KE):
                        T.transpose(ps[:, b, k * P:(k + 1) * P], wq_raw[:, k, h, 0:NOPE], ident)
                    for v in range(2):
                        ins = T.transpose(ps[:, b, 256 + v * LORA:256 + (v + 1) * LORA],
                                          wkvb_raw[0:LORA, h, v * NOPE:(v + 1) * NOPE], ident[0:LORA, 0:LORA])
                    ins.then_inc(wt_ready, 1)
                if h > 0:
                    g = h - 1
                    pe.wait_ge(wt_done, g + 1)
                    if g >= 2:
                        pe.wait_ge(wfl_done, g - 1)
                    b, w, o = 6 + g % 2, wT[:, g % 2, :], LORA * (g % 2)
                    for k in range(KE):
                        T.matmul(ps[:, b, k * LORA:(k + 1) * LORA], w[:, k * P:(k + 1) * P],
                                 w[:, 256:256 + LORA], start=True, stop=True)
                    T.matmul(ps[o:o + LORA, b, 128:384], w[:, 256 + LORA:384], wo_raw[:, g, :],
                             start=True, stop=True).then_inc(wf_ready, 1)

            for qc in range(NC):
                def project(tile, g):
                    n = qc * NT + tile * 4 + g
                    pe.wait_ge(q_done, n + 1)
                    tok = bass.ds((qc * TC + tile) * P, P)
                    for k in range(KE):
                        cols = slice(g * 512, (g + 1) * 512)
                        ins = three(ps[:, g % 2, :], xnTh[:, k, tok], xnTl[:, k, tok],
                                    WQh[:, k, cols], WQl[:, k, cols], k == 0, k == KE - 1)
                    ins.then_inc(q_ready, 1)

                def turn(tile, g):
                    n = qc * NT + tile * 4 + g
                    pe.wait_ge(rope_done, n + 1)
                    pe.wait_ge(ql_done, n + 1)
                    for h in range(4):
                        ins = T.transpose(ps[:, 2 + g % 2, h * P:(h + 1) * P], qs[:, g, h * P:(h + 1) * P], ident)
                    ins.then_inc(qt_ready, 1)

                if qc == 0:
                    pe.wait_ge(kl_done, NT // TC)
                    pe.wait_ge(pe_lo, 1)
                    pe.wait_ge(wfl_done, H)
                else:
                    pe.wait_ge(y_done, 2 * qc)
                project(0, 0)
                with pe.Fori(0, TC - 1) as i:
                    for g in range(1, 5):
                        project(i + g // 4, g % 4)
                        turn(i, g - 1)
                for g in range(1, 4):
                    project(TC - 1, g)
                    turn(TC - 1, g - 1)
                turn(TC - 1, 3)

                KT, U = TC * (qc + 1), units(qc)

                def max_unit(p, j):
                    s, i4, kc = j // (U // 2), j % (U // 2) // (qc + 1), j % (qc + 1)
                    w = CQ if kc < qc else P * (i4 + 1)
                    b = 4 + j % MX_RING
                    pe.wait_ge(mx_free, first_unit(qc) + p * U + j + 1)
                    ins = T.matmul(ps[:, b, 0:w], QTh[:, bass.ds((2 * p + s) * CQ + i4 * P, P)],
                                   KTh[:, kc * CQ:kc * CQ + w], start=True, stop=(kc < qc))
                    if kc == qc:
                        ins = T.matmul(ps[:, b, w - P:w], identb, mask_qk, start=False, stop=True)
                    ins.then_inc(mx_ready, 1)

                def turn_max(p, s):
                    k = (qc * NP + p) * 2 + s
                    pe.wait_ge(m_ready, k + 1)
                    if qc or s or not isinstance(p, int) or p:
                        pe.wait_ge(d_ready, k)
                    T.transpose(ps[0:TC, BK_M, s * P:(s + 1) * P], mrow[:, s, :], ident).then_inc(mt_ready, 1)

                def score_unit(p, i):
                    kt, s = i // 2, i % 2
                    j = kt - TC * qc
                    c0 = max(j, 0) * P
                    dst = ps[:, i % ST_RING, c0:]
                    q = bass.ds((2 * p + s) * CQ + c0, CQ - c0)
                    keys = slice(kt * P, (kt + 1) * P)
                    if i < 2:
                        pe.wait_ge(d_ready, (qc * NP + p) * 2 + s + 1)
                    pe.wait_ge(exp_done, first_unit(qc) + p * U + i + 1)
                    three(dst, KTh[:, keys], KTl[:, keys], QTh[:, q], QTl[:, q], True, False)
                    ins = T.matmul(dst, ones4, Dm[:, p % 2, s, c0:], start=False, stop=(j < 0))
                    if j >= 0:
                        ins = T.matmul(ps[:, i % ST_RING, c0:c0 + P], identb, mask_kq, start=False, stop=True)
                    ins.then_inc(st_ready, 1)

                def values(p, kt):
                    c0 = max(kt - TC * qc, 0) * P
                    if kt == 0:
                        pe.wait_ge(o_free, qc * NP + p + 1)
                    for s in range(2):
                        i = 2 * kt + s
                        pe.wait_ge(exp_done, CR_EXP + first_unit(qc) + p * U + i + 1)
                        T.matmul(ps[LORA * s:LORA * (s + 1), BK_O, c0:], kv[:, kt, 0:LORA],
                                 Pr[:, i % P_RING, c0:], start=(kt == 0), stop=(kt == KT - 1)).then_inc(pv_done, 1)

                def pair(p, ahead):
                    j, turned = 0, False
                    for kt in range(KT):
                        score_unit(p, 2 * kt)
                        score_unit(p, 2 * kt + 1)
                        if ahead:
                            for _ in range(3):
                                if j < U:
                                    max_unit(p + 1, j)
                                    j += 1
                            if j >= U // 2 + 2 and not turned:
                                turn_max(p + 1, 0)
                                turned = True
                        if kt >= LAG:
                            values(p, kt - LAG)
                    if ahead:
                        turn_max(p + 1, 1)
                    for kt in range(KT - LAG, KT):
                        values(p, kt)

                pe.wait_ge(ql_done, CR + (qc + 1) * NT)
                for j in range(U):
                    max_unit(0, j)
                    if j == U // 2 + 2:
                        turn_max(0, 0)
                turn_max(0, 1)
                with pe.Fori(0, NP - 1) as p:
                    pair(p, True)
                pair(NP - 1, False)

                pe.wait_ge(l_done, CR_L + (qc + 1) * NP)
                parts = Lp[:, :, :].rearrange("p h (j b) -> p h j b", b=4)
                for b in range(4):
                    ins = T.matmul(ps[:, BK_M, 0:H * TC], selL[:, b, :], parts[:, :, :, b],
                                   start=(b == 0), stop=(b == 3))
                ins.then_inc(den_ready, 1)
                pe.wait_ge(o_free, CR_O + (qc + 1) * NP)

                def turn_out(j):
                    for b in range(2):
                        if j:
                            pe.wait_ge(on_ready, (qc * TC + j - 1) * 2 + b + 1)
                        for n in range(4):
                            o = (4 * b + n) * CQ + j * P
                            ins = T.transpose(ps[:, b, n * P:(n + 1) * P], OT[:, o:o + P], ident)
                        ins.then_inc(t1_ready, 1)

                turn_out(0)
                for j in range(TC):
                    for b in range(2):
                        pe.wait_ge(on_ready, (qc * TC + j) * 2 + b + 1)
                        if qc or j:
                            pe.wait_ge(ont_ready, (qc * TC + j - 1) * 2 + b + 1)
                        for n in range(4):
                            ins = T.transpose(ps[:, 2 + b, n * P:(n + 1) * P],
                                              On[:, j % 2, (4 * b + n) * P:(4 * b + n + 1) * P], ident)
                        ins.then_inc(t2_ready, 1)
                    if j + 1 < TC:
                        turn_out(j + 1)
                    pe.wait_ge(ont_ready, (qc * TC + j + 1) * 2)
                    if j >= 2:
                        pe.wait_ge(ysb_ready, qc * TC + j - 1)
                    for n in range(NP):
                        ins = T.matmul(ps[:, 4 + j % 2, 0:E], OnT[:, j % 2, n, :], WO[:, n, :],
                                       start=(n == 0), stop=(n == NP - 1))
                    ins.then_inc(mo_ready, 1)

                pe.wait_ge(xn2_ready, qc + 1)
                for k in range(KE):
                    for j in range(TC):
                        ins = T.transpose(ps[:, k, j * P:(j + 1) * P], lnt[:, j, k * P:(k + 1) * P], ident)
                    ins.then_inc(xt2_ready, 1)
                pe.wait_ge(x2l_done, (qc + 1) * KE)
                for j in range(TC):
                    for k in range(KE):
                        tok = slice(j * P, (j + 1) * P)
                        ins = three(ps[:, 6, j * NE:(j + 1) * NE], xn2h[:, k, tok], xn2l[:, k, tok],
                                    wsmh[:, k, DK:], wsml[:, k, DK:], k == 0, k == KE - 1)
                ins.then_inc(log_ready, 1)

                def gate_up(n, r, e):
                    pe.wait_ge(h_ready, n + 1)
                    for t in range(2):
                        tok = slice((2 * r + t) * P, (2 * r + t + 1) * P)
                        for k in range(KE):
                            w = slice(k * 2 * F, (k + 1) * 2 * F)
                            ins = three(ps[:, r, 256 * t:256 * (t + 1)], xn2h[:, k, tok], xn2l[:, k, tok],
                                        WEh[:, e, w], WEl[:, e, w], k == 0, k == KE - 1)
                    ins.then_inc(gu_ready, 1)

                def turn_h(n, r):
                    pe.wait_ge(h_ready, CR + n + 1)
                    pe.wait_ge(hl_done, n + 1)
                    for t in range(2):
                        ins = T.transpose(ps[:, 2 + r, t * P:(t + 1) * P], hx[:, r, t, :], ident)
                    ins.then_inc(ht_ready, 1)

                def down(n, r, e):
                    pe.wait_ge(hl_done, CR + n + 1)
                    w = slice(KE * 2 * F, KE * 2 * F + E)
                    for t in range(2):
                        dst = ps[:, 4 + r, t * E:(t + 1) * E]
                        tok = slice(t * P, (t + 1) * P)
                        T.matmul(dst, hh[:, r, tok], WEh[:, e, w], start=False, stop=False)
                        T.matmul(dst, hh[:, r, tok], WEl[:, e, w], start=False, stop=False)
                        ins = T.matmul(dst, hl[:, r, tok], WEh[:, e, w], start=False, stop=False)
                    ins.then_inc(dn_done, 1)

                pe.wait_ge(ysb_ready, (qc + 1) * TC)
                pe.wait_ge(raw_lo, 2 + NX)
                for b in range(2):
                    T.matmul(ps[:, 4 + b, :], zerob, c16[:, 0:512], start=True, stop=False)
                n0 = qc * STEPS
                gate_up(n0, 0, 0)
                gate_up(n0 + 1, 1, 0)
                turn_h(n0, 0)
                with pe.Fori(1, NX) as e:
                    gate_up(n0 + 2 * e, 0, e)
                    turn_h(n0 + 2 * e - 1, 1)
                    down(n0 + 2 * e - 2, 0, e - 1)
                    gate_up(n0 + 2 * e + 1, 1, e)
                    turn_h(n0 + 2 * e, 0)
                    down(n0 + 2 * e - 1, 1, e - 1)
                turn_h(n0 + STEPS - 1, 1)
                down(n0 + STEPS - 2, 0, NE)
                down(n0 + STEPS - 1, 1, NE)
                for b in range(2):
                    ins = T.matmul(ps[:, 4 + b, :], zerob, c16[:, 0:512], start=False, stop=True)
                ins.then_inc(y_ready, 1)


def constants():
    import numpy as np

    c = np.zeros((P, C_END), np.float32)
    c[:, C_ID:C_ID + P] = np.eye(P)
    pos = np.arange(S, dtype=np.float32)
    inv = np.float32(1.0) / np.float32(10000.0) ** (np.arange(0, ROPE, 2, dtype=np.float32) / np.float32(ROPE))
    ang = pos[:, None] * inv.astype(np.float32)
    cos, sin = np.cos(ang).astype(np.float32), np.sin(ang).astype(np.float32)
    c[:, C_COS:C_SIN] = cos.reshape(NT, P, ROPE // 2).transpose(1, 0, 2).reshape(P, -1)
    c[:, C_SIN:C_SEL] = np.concatenate([-sin, sin], 1).reshape(NT, P, ROPE).transpose(1, 0, 2).reshape(P, -1)
    sel = np.zeros((P, TC, P), np.float32)
    for b in range(TC):
        for a in range(4):
            sel[32 * a + np.arange(32), b, 32 * b + np.arange(32)] = 1
    c[:, C_SEL:C_BLK] = sel.reshape(P, -1)
    blk = np.zeros((P, TC, P), np.float32)
    for j in range(TC):
        blk[j, j] = -1
    c[:, C_BLK:C_IOTA] = blk.reshape(P, -1)
    c[:, C_IOTA:C_END] = np.arange(NE)
    row, col = np.arange(P)[:, None], np.arange(P)[None]
    ones4 = np.broadcast_to(row < TC, (P, P))
    b16 = np.concatenate([row == col, (col > row) * NEG, (col < row) * NEG, ones4, np.zeros((P, P))], 1)
    return c, (b16.astype(np.float32).view(np.uint32) >> 16).astype(np.uint16)


_INS = ['L0_attn_x', 'L0_attn_wq', 'L0_attn_wkv_a', 'L0_attn_wkv_b', 'L0_attn_wo', 'L0_attn_kv_norm_scale',
        'L0_ffn_gate_w', 'L0_ffn_expert_bias', 'L0_ffn_shared_gate_w', 'L0_ffn_shared_up_w',
        'L0_ffn_shared_down_w', 'L0_ffn_experts_gate_up', 'L0_ffn_experts_down']


def kernel(**inputs):
    import numpy as _np
    import concourse.bacc as _bacc
    from concourse import mybir as _mybir
    from concourse.bass_utils import run_bass_kernel_spmd as _run

    nc = _bacc.Bacc("TRN2", target_bir_lowering=False, num_devices=1)
    arrays, args = {}, []
    given = {name: _np.ascontiguousarray(inputs[name]) for name in _INS}
    given["table_f32"], given["table_bf16"] = constants()
    for name, a in given.items():
        arrays[f"in_{name}"] = a
        args.append(nc.dram_tensor(f"in_{name}", a.shape, _mybir.dt.from_np(a.dtype), kind="ExternalInput").ap())
    args.append(nc.dram_tensor("out_0", (1, S, E), F32, kind="ExternalOutput").ap())
    attention_moe(nc, *args)
    r = _run(nc, [arrays], core_ids=[0])
    return r.results[0]["out_0"]
```

```python
from contextlib import ExitStack

import concourse.bass as bass
from concourse import mybir

F32 = mybir.dt.float32
F16 = mybir.dt.float16
BF16 = mybir.dt.bfloat16
U32 = mybir.dt.uint32
ALU = mybir.AluOpType
ACT = mybir.ActivationFunctionType
AX = mybir.AxisListType

P = 128
S, E = 2048, 256
NT = S // P
KE = E // P
H, NOPE, ROPE, VD, LORA = 16, 128, 64, 128, 64
QH = NOPE + ROPE
DK = LORA + ROPE
NP = H // 2
CQ = 512
NC = S // CQ
TC = CQ // P
NE, F = 16, 128
NX = NE + 1
TOPK = 2
MT = (TOPK * S + NE * (P - 1)) // P + 1
GT = NT + MT
XR = 4
SM_SCALE = float(QH) ** -0.5
LN_EPS, RMS_EPS = 1e-5, 1e-6
WS = 64.0
LAG = 2
ST_RING, MX_RING, P_RING = 4, 2, 8
NEG = -1e30

C_ID, C_COS, C_SIN = 0, P, P + NT * ROPE // 2
C_SEL = C_SIN + NT * ROPE
C_BLK = C_SEL + TC * P
C_IOTA = C_BLK
C_TOK = C_IOTA + NE
C_ROW = C_TOK + NT
C_TILE = C_ROW + 2
C_END = C_TILE + MT


def attention_moe(nc, x, wq, wkv_a, wkv_b, wo, kv_scale, gate_w, bias, sh_gate, sh_up, sh_down,
                  ex_gu, ex_down, c32_d, c16_d, out):
    with ExitStack() as ctx:
        def sb(name, shape, dt=F32):
            return ctx.enter_context(nc.sbuf_tensor(name, shape, dt))

        def sem(name):
            return ctx.enter_context(nc.semaphore(name))

        c32 = sb("c32", [P, C_END])
        c16 = sb("c16", [P, (7 + TC) * P], BF16)
        kvs = sb("kvs", [P, LORA])
        biasb = sb("biasb", [P, NE])
        xnTh = sb("xnTh", [P, KE, S], F16)
        xnTl = sb("xnTl", [P, KE, S], F16)
        WQh = sb("WQh", [P, KE, H * DK], F16)
        WQl = sb("WQl", [P, KE, H * DK], F16)
        WO = sb("WO", [P, NP, E])
        kv = sb("kv", [P, NT, DK])
        KTh = sb("KTh", [P, S], F16)
        KTl = sb("KTl", [P, S], F16)
        WEh = sb("WEh", [P, NX, KE * 2 * F + E], F16)
        WEl = sb("WEl", [P, NX, KE * 2 * F + E], F16)
        wsmh = sb("wsmh", [P, KE, DK + NE], F16)
        wsml = sb("wsml", [P, KE, DK + NE], F16)
        st6 = sb("st6", [P, NT, 6])
        mv = sb("mv", [P, NT, 2])
        var = sb("var", [P, NT])
        std = sb("std", [P, NT])
        rstd = sb("rstd", [P, NT])
        mxp = sb("mxp", [P, 2, TC, NC])
        mrow = sb("mrow", [P, 2, TC])
        Lp = sb("Lp", [P, H, CQ // 32])
        rL = sb("rL", [P, H, TC])
        sig = sb("sig", [P, TC, NE])
        sgb = sb("sgb", [P, TC, NE])
        top8 = sb("top8", [P, TC, 8])
        idx8 = sb("idx8", [P, TC, 8], U32)
        idxf = sb("idxf", [P, TC, 8])
        pick = sb("pick", [P, TOPK, NT, NE], BF16)
        pickb = sb("pickb", [P, TC, NE], BF16)
        share = sb("share", [P, NT, TOPK])
        rsum = sb("rsum", [P, 2, TC])
        counts = sb("counts", [P, 2, NE])
        place = sb("place", [P, TC, NE])
        where = sb("where", [P, NT, TOPK])
        where_i = sb("where_i", [P, NT, TOPK], U32)
        res_i = sb("res_i", [P, NT, TOPK], U32)
        tok_i = sb("tok_i", [P, MT], U32)
        expert_i = sb("expert_i", [P, GT], U32)

        A = sb("A", [P, 8192])
        B = sb("B", [P, 4096])
        C = sb("C", [P, 4096])
        D = sb("D", [P, 4608])

        wq_raw = A[:, 0:KE * H * QH].rearrange("p (k h c) -> p k h c", k=KE, h=H)
        wT = A[:, 6144:6144 + 768].rearrange("p (r c) -> p r c", r=2)
        xn = A[:, 6912:6912 + 512].rearrange("p (r c) -> p r c", r=2)
        QTh = A[:, 0:4096].bitcast(F16)
        QTl = A[:, 4096:8192].bitcast(F16)
        xn2h = A[:, 0:512].bitcast(F16).rearrange("p (k t) -> p k t", k=KE)
        xn2l = A[:, 512:1024].bitcast(F16).rearrange("p (k t) -> p k t", k=KE)
        On = A[:, 1024:3072].rearrange("p (r c) -> p r c", r=2)
        OnT = A[:, 3072:5120].rearrange("p (r n c) -> p r n c", r=2, n=NP)
        xr = A[:, 5120:6144].rearrange("p (t e) -> p t e", t=TC)
        x1 = A[:, 6144:7168].rearrange("p (t e) -> p t e", t=TC)
        ysb = A[:, 7168:8192].rearrange("p (t e) -> p t e", t=TC)
        xs = B[:, :].rearrange("p (t e) -> p t e", t=NT)
        Pr = B[:, :].rearrange("p (r q) -> p r q", r=P_RING)
        xg = B[:, 0:1024].rearrange("p (r e) -> p r e", r=XR)
        yo = B[:, 1024:2048].rearrange("p (r e) -> p r e", r=XR)
        sg = B[:, 3072:3328].rearrange("p (r f) -> p r f", r=2)
        hx = B[:, 3328:3584].rearrange("p (r f) -> p r f", r=2)
        hh = B[:, 3584:3712].bitcast(F16).rearrange("p (r c) -> p r c", r=2)
        hl = B[:, 3712:3840].bitcast(F16).rearrange("p (r c) -> p r c", r=2)
        xgh = C[:, 0:256].bitcast(F16).rearrange("p (r k c) -> p r k c", r=2, k=KE)
        xgl = C[:, 256:512].bitcast(F16).rearrange("p (r k c) -> p r k c", r=2, k=KE)
        scr = C[:, 1024:4096]
        lnc = C[:, 1024:2048].rearrange("p (t e) -> p t e", t=TC)
        parts4 = A[:, :].rearrange("p (r w t e) -> p r w t e", r=2, w=4, t=TC)
        mapf = D[:, 0:2 * P].rearrange("p (k c) -> p k c", k=2)
        sel_t = D[:, 512:512 + 2 * MT].rearrange("p (k m) -> p k m", k=2)
        lnt = B[:, 2048:3072].rearrange("p (t e) -> p t e", t=TC)
        wkvb_raw = C[:, :].rearrange("p (h c) -> p h c", h=H)
        qs = C[:, 0:2048].rearrange("p (r c) -> p r c", r=4)
        ropA = C[:, 2048:2560].rearrange("p (r h c) -> p r h c", r=2, h=4)
        ropB = C[:, 2560:3072].rearrange("p (r h c) -> p r h c", r=2, h=4)
        OT = C[:, :]
        wo_raw = D[:, 0:4096].rearrange("p (h e) -> p h e", h=H)
        Pacc = D[:, 0:2048].rearrange("p (r s q) -> p r s q", r=2, s=2)
        Dm = D[:, 2048:3072].bitcast(BF16).rearrange("p (r s q) -> p r s q", r=2, s=2)
        stage = D[:, 3072:4608].rearrange("p (r c) -> p r c", r=2)
        kvt = WEl[:, 0:6, :].rearrange("p a b -> p (a b)")
        wsm = WEl[:, 8, 0:2 * KE * (DK + NE)].bitcast(F32).rearrange("p (k c) -> p k c", k=KE)
        kvtA = kvt[:, 0:2048].bitcast(F32).rearrange("p (t c) -> p t c", t=NT)
        kvtB = kvt[:, 2048:4096].bitcast(F32).rearrange("p (t c) -> p t c", t=NT)

        ident = c32[:, C_ID:C_ID + P]
        cosT = c32[:, C_COS:C_SIN].rearrange("p (t c) -> p t c", t=NT)
        sinT = c32[:, C_SIN:C_SEL].rearrange("p (t c) -> p t c", t=NT)
        selL = c32[:, C_SEL:C_BLK].rearrange("p (b m) -> p b m", b=TC)
        negblk = c16[0:TC, 7 * P:11 * P].rearrange("p (j q) -> p j q", j=TC)
        iota = c32[:, C_IOTA:C_TOK]
        token = c32[:, C_TOK:C_ROW]
        row_id = c32[:, C_ROW:C_TILE]
        tile_id = c32[:, C_TILE:C_END]
        identb, mask_qk, mask_kq, ones4, zerob, before, onesb = (c16[:, i * P:(i + 1) * P] for i in range(7))

        xn2_d = nc.dram_tensor("xn2_rows", (S, E), F32, kind="Internal").ap()
        x1_d = nc.dram_tensor("x1_rows", (S, E), F32, kind="Internal").ap()
        res_d = nc.dram_tensor("results", (GT * P, E), F32, kind="Internal").ap()
        map_d = nc.dram_tensor("token_map", (NE * S, 1), F32, kind="Internal").ap()

        ps = ctx.enter_context(nc.psum_tensor("ps", [P, 8, 512], F32))
        BK_O, BK_M = 6, 7

        in_const, in_x, in_wa, in_wq, in_wkvb, in_wo = map(sem, (
            "in_const", "in_x", "in_wa", "in_wq", "in_wkvb", "in_wo"))
        stats_done, var_ready, std_ready = map(sem, ("stats_done", "var_ready", "std_ready"))
        xn_ready, xt_ready, xh_done, xl_done = map(sem, ("xn_ready", "xt_ready", "xh_done", "xl_done"))
        kva_ready, kva_done = map(sem, ("kva_ready", "kva_done"))
        kfin_ready, kt_ready, kh_done, kl_done = map(sem, ("kfin_ready", "kt_ready", "kh_done", "kl_done"))
        wt_ready, wt_done, wf_ready, wfh_done, wfl_done = map(sem, (
            "wt_ready", "wt_done", "wf_ready", "wfh_done", "wfl_done"))
        small_hi, small_lo, pe_hi, pe_lo = map(sem, ("small_hi", "small_lo", "pe_hi", "pe_lo"))
        dve_seq = sem("dve_seq")
        dm_zero = sem("dm_zero")
        q_ready, q_done, cos_done, sin_done, rope_done, qt_ready, qh_done, ql_done = map(sem, (
            "q_ready", "q_done", "cos_done", "sin_done", "rope_done", "qt_ready", "qh_done", "ql_done"))
        mx_ready, mx_free, m_ready, mt_ready, d_ready = map(sem, (
            "mx_ready", "mx_free", "m_ready", "mt_ready", "d_ready"))
        st_ready, exp_done, pv_done, sum_done, l_done, o_free = map(sem, (
            "st_ready", "exp_done", "pv_done", "sum_done", "l_done", "o_free"))
        raw_gu_in = [sem(f"raw_gu_in_{r}") for r in range(2)]
        raw_dn_in = [sem(f"raw_dn_in_{r}") for r in range(2)]
        shared_in, raw_hi, raw_lo = map(sem, ("shared_in", "raw_hi", "raw_lo"))
        den_ready, rl_ready, t1_ready, on_ready, t2_ready, ont_ready, mo_ready, ysb_ready = map(sem, (
            "den_ready", "rl_ready", "t1_ready", "on_ready", "t2_ready", "ont_ready", "mo_ready", "ysb_ready"))
        xr_in, xn2_ready, xt2_ready, x2h_done, x2l_done = map(sem, (
            "xr_in", "xn2_ready", "xt2_ready", "x2h_done", "x2l_done"))
        log_ready, sig_ready, pickb_ready, rank_ready, where_ready = map(sem, (
            "log_ready", "sig_ready", "pickb_ready", "rank_ready", "where_ready"))
        map_zero, map_in, map_back, rows_out = map(sem, ("map_zero", "map_in", "map_back", "rows_out"))
        sel_ready, tok_ready, tok_done, res_ready = map(sem, ("sel_ready", "tok_ready", "tok_done", "res_ready"))
        row_in = [sem(f"row_in_{r}") for r in range(XR)]
        xg_in = [sem(f"xg_in_{r}") for r in range(XR)]
        res_out = [sem(f"res_out_{r}") for r in range(XR)]
        ex_ready, exh_done, exl_done, gu_ready, silu_done, h_ready, ht_ready, hh_done, hl_done, dn_done, yo_ready = map(
            sem, ("ex_ready", "exh_done", "exl_done", "gu_ready", "silu_done", "h_ready", "ht_ready", "hh_done",
                  "hl_done", "dn_done", "yo_ready"))
        own_in = [sem(f"own_in_{r}") for r in range(2)]
        got_in = [sem(f"got_in_{r}") for r in range(2)]
        out_ready, out_done = map(sem, ("out_ready", "out_done"))

        CR_EXP, CR_PV, CR_SUM, CR_MX, CR_L, CR_O, CR = ST_RING, P_RING, P_RING, MX_RING, 2, 1, 2

        def units(qc):
            return 2 * TC * (qc + 1)

        HR = ROPE // 2

        def pe_of(g):
            return qs[:, g, :].rearrange("p (h c) -> p h c", c=DK)[:, :, LORA:]

        def first_unit(qc):
            return sum(NP * units(q) for q in range(qc))

        x_tiles = x.rearrange("b (t p) e -> p (b t) e", p=P)
        out_tiles = out.rearrange("b (t p) e -> p (b t) e", p=P)
        xn2_tiles = xn2_d.rearrange("(t p) e -> p t e", p=P)
        x1_tiles = x1_d.rearrange("(t p) e -> p t e", p=P)
        res_tiles = res_d.rearrange("(t p) e -> p t e", p=P)
        gu_d = ex_gu.rearrange("e (k p) f -> e p k f", p=P)

        block = ctx.enter_context(nc.Block())

        @block.sync
        def _(sp):
            sp.dma_start(xs[:, 0:8, :], x_tiles[:, 0:8, :]).then_inc(in_x, 16)
            sp.dma_start(xs[:, 8:16, :], x_tiles[:, 8:16, :]).then_inc(in_x, 16)
            sp.dma_start(wq_raw, wq.rearrange("(k p) (h c) -> p k h c", p=P, c=QH)).then_inc(in_wq, 16)
            sp.dma_start(wo_raw, wo.rearrange("(h p) e -> p h e", p=P)).then_inc(in_wo, 16)

            sp.wait_ge(in_const, 32)
            sp.dma_start(map_d.rearrange("(p b c) o -> p b (c o)", p=P, c=P // 2),
                         zerob.bitcast(F32).unsqueeze(1).broadcast_to([P, NE * S // P // (P // 2), P // 2])
                         ).then_inc(map_zero, 16)

            sp.wait_ge(wf_ready, H)
            for k in range(KE):
                c = k * 2 * F
                sp.dma_start(stage[:, 0, c:c + F], sh_gate[k * P:(k + 1) * P, :]).then_inc(shared_in, 16)
                sp.dma_start(stage[:, 0, c + F:c + 2 * F], sh_up[k * P:(k + 1) * P, :]).then_inc(shared_in, 16)
            sp.dma_start(stage[:, 0, KE * 2 * F:], sh_down).then_inc(shared_in, 16)

            def load_expert(e, r):
                sp.wait_ge(raw_lo, e + 2)
                slot = 1 - r
                sp.dma_start(stage[:, slot, 0:KE * 2 * F].rearrange("p (k f) -> p k f", k=KE),
                             gu_d[e]).then_inc(raw_gu_in[slot], 16)
                sp.dma_start(stage[:, slot, KE * 2 * F:], ex_down[e]).then_inc(raw_dn_in[slot], 16)

            for qc in range(NC):
                tiles = slice(qc * TC, (qc + 1) * TC)
                if qc == NC - 1:
                    with sp.Fori(0, NE // 2) as i:
                        for r in range(2):
                            load_expert(2 * i + r, r)
                sp.wait_ge(st_ready, first_unit(qc + 1))
                sp.dma_start(xr, x_tiles[:, tiles, :]).then_inc(xr_in, 16)
                sp.wait_ge(xn2_ready, qc + 1)
                sp.dma_start(xn2_tiles[:, tiles, :], lnt).then_inc(rows_out, 16)
                sp.dma_start(x1_tiles[:, tiles, :], x1).then_inc(rows_out, 16)

            def load_own(n):
                if n >= XR:
                    sp.wait_ge(ex_ready, n - XR + 1)
                sp.dma_start(xg[:, n % XR, :], xn2_tiles[:, n, :]).then_inc(row_in[n % XR], 16)

            def store(n, r):
                sp.wait_ge(yo_ready, CR + n + 1)
                sp.dma_start(res_tiles[:, n, :], yo[:, r, :]).then_inc(res_out[r], 16)

            sp.wait_ge(rows_out, 32 * NC)
            for n in range(XR):
                load_own(n)
            for n in range(XR, NT):
                load_own(n)
                if n - XR - 3 >= 0:
                    store(n - XR - 3, (n - XR - 3) % XR)
                if n == NT - 2:
                    sp.wait_ge(map_in, 16 * NT * TOPK)
                    sp.dma_start(mapf, map_d.rearrange("(k r c) o -> r k (c o)", k=2, c=P)).then_inc(map_back, 16)
            for n in range(NT - XR - 3, NT - XR):
                store(n, n % XR)
            with sp.Fori(NT // XR - 1, GT // XR) as a:
                for r in range(XR):
                    store(XR * a + r, r)

            for g in range(NC):
                tiles = slice(g * TC, (g + 1) * TC)
                if g == 0:
                    for r in range(XR):
                        sp.wait_ge(res_out[r], 16 + 16 * (GT // XR))
                if g >= 2:
                    sp.wait_ge(out_done, 16 * (g - 1))
                sp.dma_start(parts4[:, g % 2, 0], res_tiles[:, tiles, :]).then_inc(own_in[g % 2], 16)
                sp.dma_start(parts4[:, g % 2, 1], x1_tiles[:, tiles, :]).then_inc(own_in[g % 2], 16)
                if g:
                    sp.wait_ge(out_ready, g)
                    sp.dma_start(out_tiles[:, (g - 1) * TC:g * TC, :], parts4[:, (g - 1) % 2, 0]).then_inc(out_done, 16)
            sp.wait_ge(out_ready, NC)
            sp.dma_start(out_tiles[:, (NC - 1) * TC:, :], parts4[:, (NC - 1) % 2, 0]).then_inc(out_done, 16)
            sp.wait_ge(out_done, 16 * NC)

        @block.gpsimd
        def _(pool):
            def add_up(qc, p, half):
                KT = TC * (qc + 1)
                n0 = first_unit(qc) + p * units(qc)
                pool.wait_ge(l_done, qc * NP + p + 1)
                for kt in range(1, KT):
                    c0 = max(kt - TC * qc, 0) * P
                    for s in range(2):
                        n, i = n0 + 2 * kt + s, 2 * kt + s
                        pool.wait_ge(exp_done, CR_EXP + n + 1)
                        acc = Pacc[:, half, s, :]
                        if kt == 1:
                            ins = nc.gpsimd.tensor_tensor(acc[:, c0:], Pr[:, s, c0:], Pr[:, i, c0:], ALU.add)
                            if c0:
                                ins = nc.gpsimd.tensor_copy(acc[:, 0:c0], Pr[:, s, 0:c0])
                            ins.then_inc(sum_done, 1 + 2 * s)
                        else:
                            pool.wait_ge(sum_done, CR_SUM + n - 1)
                            nc.gpsimd.tensor_tensor(acc[:, c0:], acc[:, c0:], Pr[:, i % P_RING, c0:],
                                                    ALU.add).then_inc(sum_done, 1)

            def sines(qc, tile, g):
                n = qc * NT + tile * 4 + g
                pool.wait_ge(q_done, CR + n + 1)
                if n >= 2:
                    pool.wait_ge(rope_done, n - 1)
                for dst, src in ((slice(0, HR), slice(HR, ROPE)), (slice(HR, ROPE), slice(0, HR))):
                    sine = sinT[:, qc * TC + tile, dst].unsqueeze(1).broadcast_to([P, 4, HR])
                    ins = nc.gpsimd.tensor_tensor(ropB[:, g % 2, :, dst], pe_of(g)[:, :, src], sine, ALU.mult)
                ins.then_inc(sin_done, 1)

            def gather(dst, rows, index, done):
                nc.gpsimd.indirect_dma_start(
                    out=dst, out_offset=None, in_=rows,
                    in_offset=bass.IndirectOffsetOnAxis(ap=index, axis=0)).then_inc(done, 16)

            pool.wait_ge(in_const, 32)
            for qc in range(NC):
                for tile in range(TC):
                    for g in range(4):
                        sines(qc, tile, g)
                with pool.Fori(0, NP // 2) as i:
                    add_up(qc, 2 * i, 0)
                    add_up(qc, 2 * i + 1, 1)
                if qc == 0:
                    pool.wait_ge(map_zero, 16)
                pool.wait_ge(where_ready, qc + 1)
                for t in range(qc * TC, (qc + 1) * TC):
                    for k in range(TOPK):
                        nc.gpsimd.indirect_dma_start(
                            out=map_d, out_offset=bass.IndirectOffsetOnAxis(ap=where_i[:, t, k:k + 1], axis=0),
                            in_=token[:, t:t + 1], in_offset=None).then_inc(map_in, 16)
            pool.wait_ge(tok_ready, 1)
            for n in range(NT, GT):
                pool.wait_ge(ex_ready, n - XR + 1)
                gather(xg[:, n % XR, :], xn2_d, tok_i[:, n - NT:n - NT + 1], xg_in[n % XR])
            pool.wait_ge(res_ready, 1)
            for r in range(XR):
                pool.wait_ge(res_out[r], 16 + 16 * (GT // XR))
            for g in range(NC):
                if g >= 2:
                    pool.wait_ge(out_ready, g - 1)
                for j in range(TC):
                    for k in range(TOPK):
                        gather(parts4[:, g % 2, 2 + k, j], res_d, res_i[:, g * TC + j, k:k + 1], got_in[g % 2])

        @block.scalar
        def _(act):
            act.dma_start(c32[:, :], c32_d).then_inc(in_const, 16)
            act.dma_start(c16[:, :], c16_d.bitcast(BF16)).then_inc(in_const, 16)
            act.dma_start(wsm[:, :, 0:DK], wkv_a.rearrange("(k p) c -> p k c", p=P)).then_inc(in_wa, 16)
            act.dma_start(wsm[:, :, DK:], gate_w.rearrange("(k p) c -> p k c", p=P)).then_inc(in_wa, 16)
            act.dma_start(kvs[:, :], kv_scale.rearrange("(a c) -> a c", a=1).broadcast_to([P, LORA])).then_inc(in_wa, 16)
            act.dma_start(biasb[:, :], bias.rearrange("(a c) -> a c", a=1).broadcast_to([P, NE])).then_inc(in_wa, 16)
            act.dma_start(wkvb_raw[0:LORA], wkv_b.rearrange("c (h n) -> c h n", h=H)).then_inc(in_wkvb, 16)

            def copy(dst, src, scale=1.0):
                return nc.scalar.activation(dst, src, ACT.Copy, scale=scale)

            act.wait_ge(in_wa, 64)
            copy(wsmh[:, :, :], wsm[:, :, :], WS).then_inc(small_hi, 1)
            act.wait_ge(var_ready, 1)
            nc.scalar.activation(std[:, :], var[:, :], ACT.Sqrt).then_inc(std_ready, 1)

            for t in range(NT + 1):
                if t < NT:
                    act.wait_ge(xt_ready, t + 1)
                    copy(xnTh[:, :, t * P:(t + 1) * P],
                         ps[:, t % 2, 0:E].rearrange("p (k c) -> p k c", k=KE)).then_inc(xh_done, 1)
                if t > 0:
                    act.wait_ge(kva_ready, t)
                    copy(kv[:, t - 1, :], ps[:, 2 + (t - 1) % 2, 0:DK], 1 / WS).then_inc(kva_done, 1)
            act.wait_ge(var_ready, 2)
            nc.scalar.activation(std[:, :], var[:, :], ACT.Sqrt).then_inc(std_ready, 1)
            for g in range(NT // TC):
                act.wait_ge(kt_ready, g + 1)
                copy(KTh[:, g * CQ:(g + 1) * CQ], ps[:, g, :]).then_inc(kh_done, 1)

            act.wait_ge(in_wq, 16)
            copy(WQh[:, :, :].rearrange("p k (h c) -> p (k h) c", c=DK)[:, :, LORA:],
                 wq_raw.rearrange("p k h c -> p (k h) c")[:, :, NOPE:], WS).then_inc(pe_hi, 1)
            for h in range(H + 1):
                if h < H:
                    act.wait_ge(wt_ready, h + 1)
                    if h >= 2:
                        act.wait_ge(wf_ready, h - 1)
                    copy(wT[:, h % 2, :], ps[:, 4 + h % 2, 0:384]).then_inc(wt_done, 1)
                if h > 0:
                    g = h - 1
                    act.wait_ge(wf_ready, g + 1)
                    o = LORA * (g % 2)
                    copy(WO[o:o + LORA, g // 2, :], ps[o:o + LORA, 6 + g % 2, 128:384])
                    copy(WQh[:, :, g * DK:g * DK + LORA],
                         ps[:, 6 + g % 2, 0:128].rearrange("p (k c) -> p k c", k=KE), WS).then_inc(wfh_done, 1)

            def scores_to_probs(qc, p):
                KT = TC * (qc + 1)
                n0 = first_unit(qc) + p * units(qc)
                cuts = (KT, KT + 6)
                for i in range(2 * KT):
                    n = n0 + i
                    c0 = max(i // 2 - TC * qc, 0) * P
                    act.wait_ge(st_ready, n + 1)
                    act.wait_ge(pv_done, n + 1)
                    act.wait_ge(sum_done, n + 1)
                    nc.scalar.activation(Pr[:, i % P_RING, c0:], ps[:, i % ST_RING, c0:], ACT.Exp,
                                         scale=SM_SCALE).then_inc(exp_done, 1)
                    if qc == NC - 1 and i in cuts:
                        cut_expert(p, cuts.index(i))
                act.wait_ge(pv_done, CR_PV + n0 + 2 * KT)
                copy(OT[:, bass.ds(p * CQ, CQ)], ps[:, BK_O, :]).then_inc(o_free, 1)

            def cut_expert(p, r):
                act.wait_ge(raw_gu_in[1 - r], (p + 1) * 16)
                act.wait_ge(raw_dn_in[1 - r], (p + 1) * 16)
                copy(WEh[:, 2 * p + r, :], stage[:, 1 - r, :], WS).then_inc(raw_hi, 1)

            for qc in range(NC):
                if qc == 0:
                    act.wait_ge(pe_lo, 1)
                    act.wait_ge(wfl_done, H)
                def q_out(tile, g):
                    n = qc * NT + tile * 4 + g
                    act.wait_ge(q_ready, n + 1)
                    copy(qs[:, g, :], ps[:, g % 2, :], 1 / WS).then_inc(q_done, 1)

                def q_high(tile, g):
                    n = qc * NT + tile * 4 + g
                    act.wait_ge(qt_ready, n + 1)
                    dst = QTh.rearrange("p (h q) -> p h q", h=H)[:, 4 * g:4 * g + 4, bass.ds(tile * P, P)]
                    copy(dst, ps[:, 2 + g % 2, :].rearrange("p (h q) -> p h q", h=4)).then_inc(qh_done, 1)

                if qc:
                    act.wait_ge(rows_out, 32 * qc)
                q_out(0, 0)
                q_out(0, 1)
                with act.Fori(0, TC - 1) as i:
                    for g in range(2, 6):
                        q_out(i + g // 4, g % 4)
                        q_high(i, g - 2)
                for g in range(2, 4):
                    q_out(TC - 1, g)
                    q_high(TC - 1, g - 2)
                for g in range(2, 4):
                    q_high(TC - 1, g)

                if qc:
                    act.wait_ge(rows_out, 32 * qc)
                if qc == NC - 1:
                    act.wait_ge(shared_in, 80)
                    copy(WEh[:, NE, :], stage[:, 0, :], WS).then_inc(raw_hi, 1)
                with act.Fori(0, NP) as p:
                    scores_to_probs(qc, p)
                for j in range(TC):
                    for b in range(2):
                        act.wait_ge(t2_ready, (qc * TC + j) * 2 + b + 1)
                        copy(OnT[:, j % 2, 4 * b:4 * b + 4, :],
                             ps[:, 2 + b, :].rearrange("p (n q) -> p n q", n=4)).then_inc(ont_ready, 1)
                    act.wait_ge(mo_ready, qc * TC + j + 1)
                    copy(ysb[:, j, :], ps[:, 4 + j % 2, 0:E]).then_inc(ysb_ready, 1)
                for r in range(2):
                    act.wait_ge(var_ready, 2 + qc * 2 + r + 1)
                    nc.scalar.activation(std[:, 0:TC], var[:, 0:TC], ACT.Sqrt).then_inc(std_ready, 1)
                for k in range(KE):
                    act.wait_ge(xt2_ready, qc * KE + k + 1)
                    copy(xn2h[:, k, :], ps[:, k, :]).then_inc(x2h_done, 1)
                act.wait_ge(log_ready, qc + 1)
                nc.scalar.activation(sig[:, :, :].rearrange("p t e -> p (t e)"), ps[:, 6, 0:TC * NE],
                                     ACT.Sigmoid, scale=1 / WS).then_inc(sig_ready, 1)

            def x_high(n, r):
                act.wait_ge(ex_ready, n + 1)
                act.wait_ge(gu_ready, n + 1)
                copy(xgh[:, r], ps[:, r, 0:E].rearrange("p (k c) -> p k c", k=KE)).then_inc(exh_done, 1)

            def silu(n, r):
                act.wait_ge(gu_ready, CR + n + 1)
                act.wait_ge(h_ready, n + 1)
                nc.scalar.activation(sg[:, r], ps[:, 2 + r, 0:F], ACT.Silu, scale=1 / WS).then_inc(silu_done, 1)

            def h_high(n, r):
                act.wait_ge(ht_ready, CR + n + 1)
                act.wait_ge(dn_done, n + 1)
                copy(hh[:, r], ps[:, 4 + r, 0:P]).then_inc(hh_done, 1)

            def step(n, r, k=None):
                if k is None or k < GT:
                    x_high(n, r % 2)
                if k is None or 0 <= k - 1 < GT:
                    silu(n - 1, (r - 1) % 2)
                if k is None or 0 <= k - 2 < GT:
                    h_high(n - 2, r % 2)

            for k in range(XR):
                step(k, k, k)
            with act.Fori(1, GT // XR) as a:
                for r in range(XR):
                    step(XR * a + r, r)
            for k in range(GT, GT + 2):
                step(k, k, k)
            for g in range(NC):
                act.wait_ge(var_ready, 2 + 2 * NC + g + 1)
                nc.scalar.activation(std[:, 0:TC], var[:, 0:TC], ACT.Sqrt).then_inc(std_ready, 1)

        @block.vector
        def _(dve):
            steps = [0]

            def link(ins):
                steps[0] += 1
                ins.then_inc(dve_seq, 1)
                dve.wait_ge(dve_seq, steps[0])

            V = nc.vector

            V.memset(mxp[:, 0, 0, 0:1], 0.0).then_inc(exp_done, CR_EXP)
            V.memset(mxp[:, 0, 0, 1:2], 0.0).then_inc(pv_done, CR_PV)
            V.memset(mxp[:, 0, 0, 2:3], 0.0).then_inc(sum_done, CR_SUM)
            V.memset(mxp[:, 0, 0, 3:4], 0.0).then_inc(mx_free, CR_MX)
            V.memset(mxp[:, 0, 1, 0:1], 0.0).then_inc(l_done, CR_L)
            V.memset(mxp[:, 0, 1, 1:2], 0.0).then_inc(o_free, CR_O)
            V.memset(mxp[:, 0, 1, 2:3], 0.0).then_inc(raw_lo, 2)
            for i, two_slots in enumerate((q_done, ql_done, exl_done, gu_ready, h_ready, ht_ready, hl_done, dn_done,
                                           yo_ready)):
                V.memset(mxp[:, 1, i // NC, i % NC:i % NC + 1], 0.0).then_inc(two_slots, CR)
            for r in range(XR):
                V.memset(mxp[:, 0, 2, r:r + 1], 0.0).then_inc(res_out[r], 16)
            link(V.memset(counts[:, 0, :], 0.0))
            V.memset(expert_i[:, 0:NT], NE)

            dve.wait_ge(small_hi, 1)
            V.scalar_tensor_tensor(out=wsml[:, :, :], in0=wsm[:, :, :], scalar=WS, in1=wsmh[:, :, :],
                                   op0=ALU.mult, op1=ALU.subtract).then_inc(small_lo, 1)

            roots = [0]

            def inv_std(n, eps, scale=1.0, src=None):
                src = mv[:, 0:n, 1] if src is None else src
                V.tensor_scalar(var[:, 0:n], src, scale, eps, ALU.mult, ALU.add).then_inc(var_ready, 1)
                roots[0] += 1
                dve.wait_ge(std_ready, roots[0])
                link(V.reciprocal(rstd[:, 0:n], std[:, 0:n]))

            def moments(src, n):
                for t in range(n):
                    ins = V.bn_stats(st6[:, t, :], src[:, t, :])
                link(ins)
                for t in range(n):
                    ins = V.bn_aggr(mv[:, t, :], st6[:, t, :])
                link(ins)

            dve.wait_ge(in_x, 32)
            moments(xs, NT)
            inv_std(NT, LN_EPS)

            def normalise(t):
                if t >= 2:
                    dve.wait_ge(xt_ready, t - 1)
                V.tensor_scalar(xn[:, t % 2, :], xs[:, t, :], mv[:, t, 0:1], rstd[:, t:t + 1],
                                ALU.subtract, ALU.mult).then_inc(xn_ready, 1)

            normalise(0)
            normalise(1)
            for t in range(NT):
                dve.wait_ge(xh_done, t + 1)
                V.tensor_tensor(xnTl[:, :, t * P:(t + 1) * P],
                                ps[:, t % 2, 0:E].rearrange("p (k c) -> p k c", k=KE),
                                xnTh[:, :, t * P:(t + 1) * P], ALU.subtract).then_inc(xl_done, 1)
                if t + 2 < NT:
                    normalise(t + 2)

            dve.wait_ge(kva_done, NT)
            dve.wait_ge(in_const, 32)
            lat, kpe = kv[:, :, 0:LORA], kv[:, :, LORA:DK]
            link(V.tensor_tensor(kvtA, lat, lat, ALU.mult))
            link(V.tensor_reduce(rsumk := mv[:, :, 0], kvtA, AX.X, ALU.add))
            inv_std(NT, RMS_EPS, 1.0 / LORA, rsumk)
            link(V.tensor_tensor(lat, lat, rstd[:, :].unsqueeze(2).broadcast_to([P, NT, LORA]), ALU.mult))
            V.tensor_tensor(lat, lat, kvs[:, :].unsqueeze(1).broadcast_to([P, NT, LORA]), ALU.mult)
            V.tensor_tensor(kvtA[:, :, 0:HR], kpe[:, :, 0:HR], cosT, ALU.mult)
            V.tensor_tensor(kvtA[:, :, HR:], kpe[:, :, HR:], cosT, ALU.mult)
            V.tensor_tensor(kvtB[:, :, 0:HR], kpe[:, :, HR:], sinT[:, :, 0:HR], ALU.mult)
            link(V.tensor_tensor(kvtB[:, :, HR:], kpe[:, :, 0:HR], sinT[:, :, HR:], ALU.mult))
            V.tensor_tensor(kpe, kvtA, kvtB, ALU.add).then_inc(kfin_ready, 1)
            for g in range(NT // TC):
                dve.wait_ge(kh_done, g + 1)
                V.tensor_tensor(KTl[:, g * CQ:(g + 1) * CQ], ps[:, g, :], KTh[:, g * CQ:(g + 1) * CQ],
                                ALU.subtract).then_inc(kl_done, 1)

            dve.wait_ge(pe_hi, 1)
            V.scalar_tensor_tensor(
                out=WQl[:, :, :].rearrange("p k (h c) -> p (k h) c", c=DK)[:, :, LORA:],
                in0=wq_raw.rearrange("p k h c -> p (k h) c")[:, :, NOPE:], scalar=WS,
                in1=WQh[:, :, :].rearrange("p k (h c) -> p (k h) c", c=DK)[:, :, LORA:],
                op0=ALU.mult, op1=ALU.subtract).then_inc(pe_lo, 1)
            for g in range(H):
                dve.wait_ge(wfh_done, g + 1)
                V.scalar_tensor_tensor(
                    out=WQl[:, :, g * DK:g * DK + LORA],
                    in0=ps[:, 6 + g % 2, 0:128].rearrange("p (k c) -> p k c", k=KE), scalar=WS,
                    in1=WQh[:, :, g * DK:g * DK + LORA],
                    op0=ALU.mult, op1=ALU.subtract).then_inc(wfl_done, 1)
            dve.wait_ge(wf_ready, H)
            V.memset(D[:, 2048:3072], 0.0).then_inc(dm_zero, 1)
            dve.wait_ge(dm_zero, 1)

            def cosines(qc, tile, g):
                n = qc * NT + tile * 4 + g
                dve.wait_ge(q_done, CR + n + 1)
                if not isinstance(n, int) or n >= 2:
                    dve.wait_ge(rope_done, n - 1)
                halves = [P, 4, 2, HR]
                V.tensor_tensor(ropA[:, g % 2].rearrange("p h (x c) -> p h x c", x=2),
                                pe_of(g).rearrange("p h (x c) -> p h x c", x=2),
                                cosT[:, qc * TC + tile, :].unsqueeze(1).unsqueeze(1).broadcast_to(halves),
                                ALU.mult).then_inc(cos_done, 1)

            def rotate(qc, tile, g):
                n = qc * NT + tile * 4 + g
                dve.wait_ge(cos_done, n + 1)
                dve.wait_ge(sin_done, n + 1)
                V.tensor_tensor(pe_of(g), ropA[:, g % 2], ropB[:, g % 2], ALU.add).then_inc(rope_done, 1)

            def q_low(qc, tile, g):
                n = qc * NT + tile * 4 + g
                dve.wait_ge(qh_done, n + 1)
                dst = [t.rearrange("p (h q) -> p h q", h=H)[:, 4 * g:4 * g + 4, bass.ds(tile * P, P)]
                       for t in (QTh, QTl)]
                V.tensor_tensor(dst[1], ps[:, 2 + g % 2, :].rearrange("p (h q) -> p h q", h=4), dst[0],
                                ALU.subtract).then_inc(ql_done, 1)

            def maxima(qc, p, sums=None):
                U = units(qc)
                n0 = first_unit(qc) + p * U

                def subtrahend(s):
                    k = (qc * NP + p) * 2 + s
                    dve.wait_ge(mt_ready, k + 1)
                    rows = ps[0:TC, BK_M, s * P:(s + 1) * P].unsqueeze(1).broadcast_to([TC, TC, P])
                    V.tensor_tensor(Dm[0:TC, p % 2, s, :].rearrange("p (j q) -> p j q", j=TC), rows, negblk,
                                    ALU.mult).then_inc(d_ready, 1)

                def row_max(s):
                    dve.wait_ge(mx_free, CR_MX + n0 + (s + 1) * U // 2)
                    V.tensor_reduce(mrow[:, s, :], mxp[:, s, :, 0:qc + 1], AX.X, ALU.max).then_inc(m_ready, 1)

                for j in range(U):
                    s, i4, kc = j // (U // 2), j % (U // 2) // (qc + 1), j % (qc + 1)
                    w = CQ if kc < qc else P * (i4 + 1)
                    dve.wait_ge(mx_ready, n0 + j + 1)
                    V.tensor_reduce(mxp[:, s, i4, kc:kc + 1], ps[:, 4 + j % MX_RING, 0:w], AX.X,
                                    ALU.max).then_inc(mx_free, 1)
                    if j == U // 2 - 1:
                        row_max(0)
                    if j == U // 2 + 2:
                        subtrahend(0)
                    if j == U // 4 + 1 and sums is not None:
                        part_sums(qc, sums)
                row_max(1)
                subtrahend(1)

            def part_sums(qc, p):
                dve.wait_ge(sum_done, CR_SUM + first_unit(qc) + (p + 1) * units(qc))
                V.tensor_reduce(Lp[:, bass.ds(2 * p, 2), :],
                                Pacc[:, p % 2].rearrange("p s (b c) -> p s b c", c=32),
                                AX.X, ALU.add, apply_transpose=True).then_inc(l_done, 1)

            def cut_expert(p, r):
                e = 2 * p + r
                dve.wait_ge(raw_hi, e + 2)
                V.scalar_tensor_tensor(out=WEl[:, e, :], in0=stage[:, 1 - r, :], scalar=WS, in1=WEh[:, e, :],
                                       op0=ALU.mult, op1=ALU.subtract).then_inc(raw_lo, 1)

            def layer_norm(src, dst, done=None):
                moments(src, TC)
                inv_std(TC, LN_EPS)
                for j in range(TC):
                    ins = V.tensor_scalar(dst[:, j, :], src[:, j, :], mv[:, j, 0:1], rstd[:, j:j + 1],
                                          ALU.subtract, ALU.mult)
                if done is None:
                    link(ins)
                else:
                    ins.then_inc(done, 1)

            scr_p = C[:, 512:640].rearrange("p (k t e) -> p k t e", k=TOPK, t=TC)
            scr_c = C[:, 640:704].rearrange("p (t e) -> p t e", t=TC)
            scr_s = C[:, 704:720]

            for qc in range(NC):
                for g in range(2):
                    cosines(qc, 0, g)
                    rotate(qc, 0, g)
                with dve.Fori(0, TC - 1) as i:
                    for g in range(2, 6):
                        cosines(qc, i + g // 4, g % 4)
                        q_low(qc, i, g - 2)
                        rotate(qc, i + g // 4, g % 4)
                for g in range(2, 4):
                    cosines(qc, TC - 1, g)
                    q_low(qc, TC - 1, g - 2)
                    rotate(qc, TC - 1, g)
                for g in range(2, 4):
                    q_low(qc, TC - 1, g)

                maxima(qc, 0)
                maxima(qc, 1)
                if qc == NC - 1:
                    dve.wait_ge(raw_hi, 1)
                    V.scalar_tensor_tensor(out=WEl[:, NE, :], in0=stage[:, 0, :], scalar=WS, in1=WEh[:, NE, :],
                                           op0=ALU.mult, op1=ALU.subtract).then_inc(raw_lo, 1)
                    for r in range(2):
                        cut_expert(0, r)
                with dve.Fori(1, NP - 1) as p:
                    maxima(qc, p + 1, sums=p - 1)
                    if qc == NC - 1:
                        for r in range(2):
                            cut_expert(p, r)
                if qc == NC - 1:
                    for r in range(2):
                        cut_expert(NP - 1, r)
                part_sums(qc, NP - 2)
                part_sums(qc, NP - 1)
                dve.wait_ge(den_ready, qc + 1)
                link(V.reciprocal(rL[:, :, :].rearrange("p h j -> p (h j)"), ps[:, BK_M, 0:H * TC]))
                for j in range(TC):
                    for b in range(2):
                        dve.wait_ge(t1_ready, (qc * TC + j) * 2 + b + 1)
                        if j >= 2:
                            dve.wait_ge(t2_ready, (qc * TC + j - 1) * 2)
                        V.tensor_tensor(On[:, j % 2, 512 * b:512 * b + 512].rearrange("p (h c) -> p h c", c=LORA),
                                        ps[:, b, :].rearrange("p (h c) -> p h c", c=LORA),
                                        rL[:, 8 * b:8 * b + 8, j:j + 1].broadcast_to([P, 8, LORA]),
                                        ALU.mult).then_inc(on_ready, 1)

                dve.wait_ge(ysb_ready, (qc + 1) * TC)
                layer_norm(ysb, lnt)
                dve.wait_ge(xr_in, 16 * (qc + 1))
                link(V.tensor_tensor(x1, xr, lnt, ALU.add))
                layer_norm(x1, lnt, xn2_ready)
                for k in range(KE):
                    dve.wait_ge(x2h_done, qc * KE + k + 1)
                    V.tensor_tensor(xn2l[:, k, :], ps[:, k, :], xn2h[:, k, :], ALU.subtract).then_inc(x2l_done, 1)

                dve.wait_ge(sig_ready, qc + 1)
                link(V.tensor_tensor(sgb[:, :, :], sig[:, :, :],
                                     biasb[:, :].unsqueeze(1).broadcast_to([P, TC, NE]), ALU.add))
                for j in range(TC):
                    ins = V.max(top8[:, j, :], sgb[:, j, :])
                link(ins)
                for j in range(TC):
                    ins = V.max_index(idx8[:, j, :], top8[:, j, :], sgb[:, j, :])
                link(ins)
                link(V.tensor_copy(idxf[:, :, :], idx8[:, :, :]))
                iota4 = iota.unsqueeze(1).broadcast_to([P, TC, NE])
                tiles = slice(qc * TC, (qc + 1) * TC)
                for k in range(TOPK):
                    ins = V.tensor_tensor(pick[:, k, tiles, :], iota4,
                                          idxf[:, :, k:k + 1].broadcast_to([P, TC, NE]), ALU.is_equal)
                link(ins)
                V.tensor_tensor(pickb[:, :, :], pick[:, 0, tiles, :], pick[:, 1, tiles, :], ALU.add).then_inc(pickb_ready, 1)
                for k in range(TOPK):
                    ins = V.tensor_tensor(scr_p[:, k], pick[:, k, tiles, :], sig[:, :, :], ALU.mult)
                link(ins)
                for k in range(TOPK):
                    ins = V.tensor_reduce(share[:, tiles, k], scr_p[:, k], AX.X, ALU.add)
                link(ins)
                link(V.tensor_tensor(rsum[:, 0, :], share[:, tiles, 0], share[:, tiles, 1], ALU.add))
                link(V.tensor_scalar(rsum[:, 0, :], rsum[:, 0, :], 1e-20, None, ALU.add))
                link(V.reciprocal(rsum[:, 1, :], rsum[:, 0, :]))
                link(V.tensor_tensor(share[:, tiles, :], share[:, tiles, :],
                                     rsum[:, 1, :].unsqueeze(2).broadcast_to([P, TC, TOPK]), ALU.mult))

                dve.wait_ge(rank_ready, qc + 1)
                rank = ps[:, 6, 64:64 + 2 * TC * NE].rearrange("p (w t e) -> p w t e", w=2, t=TC)
                for j in range(TC):
                    V.tensor_tensor(place[:, j, :], rank[:, 0, j, :], counts[:, j % 2, :], ALU.add)
                    link(V.tensor_tensor(counts[:, (j + 1) % 2, :], rank[:, 1, j, :], counts[:, j % 2, :], ALU.add))
                V.tensor_scalar(scr_s[:, :], iota, float(S), None, ALU.mult)
                link(V.tensor_copy(scr_c[:, :], place[:, :, :]))
                link(V.tensor_tensor(place[:, :, :], scr_c[:, :], scr_s[:, :].unsqueeze(1).broadcast_to([P, TC, NE]),
                                     ALU.add))
                for k in range(TOPK):
                    ins = V.tensor_tensor(scr_p[:, k], pick[:, k, tiles, :], place[:, :, :], ALU.mult)
                link(ins)
                for k in range(TOPK):
                    ins = V.tensor_reduce(where[:, tiles, k], scr_p[:, k], AX.X, ALU.add)
                link(ins)
                V.tensor_copy(where_i[:, tiles, :], where[:, tiles, :]).then_inc(where_ready, 1)

            link(V.tensor_scalar(scr_s[:, :], iota, float(P), None, ALU.mult))
            more = scr[:, 0:NE * NT].rearrange("p (e j) -> p e j", e=NE)
            link(V.tensor_tensor(more, counts[:, 0, :].unsqueeze(2).broadcast_to([P, NE, NT]),
                                 scr_s[:, :].unsqueeze(1).broadcast_to([P, NE, NT]), ALU.is_gt))
            n_tiles, ends = scr[:, 256:256 + NE], [scr[:, 288 + 16 * i:304 + 16 * i] for i in range(2)]
            link(V.tensor_reduce(n_tiles, more, AX.X, ALU.add))
            link(V.tensor_copy(ends[0], n_tiles))
            a, d = 0, 1
            while d < NE:
                V.tensor_copy(ends[1 - a][:, 0:d], ends[a][:, 0:d])
                link(V.tensor_tensor(ends[1 - a][:, d:], ends[a][:, d:], ends[a][:, 0:NE - d], ALU.add))
                a, d = 1 - a, 2 * d
            end = ends[a]
            done = scr[:, 512:512 + MT * NE].rearrange("p (m e) -> p m e", e=NE)
            link(V.tensor_tensor(done, end.unsqueeze(1).broadcast_to([P, MT, NE]),
                                 tile_id.unsqueeze(2).broadcast_to([P, MT, NE]), ALU.is_le))
            which, col = scr[:, 1536:1536 + MT], scr[:, 1600:1600 + MT]
            link(V.tensor_reduce(which, done, AX.X, ALU.add))
            link(V.tensor_tensor(done, done, n_tiles.unsqueeze(1).broadcast_to([P, MT, NE]), ALU.mult))
            link(V.tensor_reduce(col, done, AX.X, ALU.add))
            link(V.tensor_tensor(col, tile_id, col, ALU.subtract))
            link(V.scalar_tensor_tensor(out=col, in0=which, scalar=float(NT), in1=col, op0=ALU.mult, op1=ALU.add))
            link(V.tensor_scalar(col, col, float(NE * NT - 1), None, ALU.min))
            V.tensor_scalar(expert_i[:, NT:], which, float(NE - 1), None, ALU.min)
            for k in range(2):
                ins = V.tensor_scalar(sel_t[:, k, :], col, row_id[:, k:k + 1], None, ALU.is_equal)
            ins.then_inc(sel_ready, 1)
            V.tensor_tensor(scr[:, 320:336], end, n_tiles, ALU.subtract)
            link(V.tensor_scalar(scr[:, 336:352], iota, -float(S), float(NT * P), ALU.mult, ALU.add))
            link(V.scalar_tensor_tensor(out=scr[:, 352:368], in0=scr[:, 320:336], scalar=float(P),
                                        in1=scr[:, 336:352], op0=ALU.mult, op1=ALU.add))
            shift = scr[:, 1792:1792 + TOPK * NT * NE].rearrange("p (k t e) -> p k t e", k=TOPK, t=NT)
            for k in range(TOPK):
                ins = V.tensor_tensor(shift[:, k], pick[:, k], scr[:, 352:368].unsqueeze(1).broadcast_to([P, NT, NE]),
                                      ALU.mult)
            link(ins)
            moved = scr[:, 1700:1700 + NT * TOPK].rearrange("p (t k) -> p t k", k=TOPK)
            for k in range(TOPK):
                ins = V.tensor_reduce(moved[:, :, k], shift[:, k], AX.X, ALU.add)
            link(ins)
            V.tensor_tensor(res_i[:, :, :], moved, where[:, :, :], ALU.add).then_inc(res_ready, 1)

            def x_low(n, r):
                dve.wait_ge(exh_done, n + 1)
                V.tensor_tensor(xgl[:, r], ps[:, r, 0:E].rearrange("p (k c) -> p k c", k=KE), xgh[:, r],
                                ALU.subtract).then_inc(exl_done, 1)

            def product(n, r):
                dve.wait_ge(silu_done, n + 1)
                dve.wait_ge(ht_ready, n + 1)
                V.scalar_tensor_tensor(out=hx[:, r], in0=ps[:, 2 + r, F:2 * F], scalar=1 / WS, in1=sg[:, r],
                                       op0=ALU.mult, op1=ALU.mult).then_inc(h_ready, 1)

            def h_low(n, r):
                dve.wait_ge(hh_done, n + 1)
                V.tensor_tensor(hl[:, r], ps[:, 4 + r, 0:P], hh[:, r], ALU.subtract).then_inc(hl_done, 1)

            def result(n, r, turn):
                dve.wait_ge(dn_done, CR + n + 1)
                dve.wait_ge(res_out[r], 16 * (turn + 1))
                V.tensor_scalar(yo[:, r, :], ps[:, 6 + r % 2, 0:E], 1 / WS, None, ALU.mult).then_inc(yo_ready, 1)

            def step(n, r, a, k=None):
                if k is None or k < GT:
                    x_low(n, r % 2)
                if k is None or 0 <= k - 1 < GT:
                    product(n - 1, (r - 1) % 2)
                if k is None or 0 <= k - 2 < GT:
                    h_low(n - 2, r % 2)
                if k is None or 0 <= k - 3 < GT:
                    result(n - 3, (r - 3) % XR, a - (r < 3))

            dve.wait_ge(rows_out, 32 * NC)
            for k in range(XR):
                step(k, k, 0, k)
            with dve.Fori(1, NT // XR) as a:
                for r in range(XR):
                    step(XR * a + r, r, a)
            dve.wait_ge(tok_done, 1)
            V.tensor_copy(tok_i[:, :], ps[:, 7, 256:256 + MT]).then_inc(tok_ready, 1)
            with dve.Fori(NT // XR, GT // XR) as a:
                for r in range(XR):
                    step(XR * a + r, r, a)
            for k in range(GT, GT + 3):
                step(k, k % XR, GT // XR, k)

            for g in range(NC):
                b = g % 2
                dve.wait_ge(own_in[b], 32 * (g // 2 + 1))
                dve.wait_ge(got_in[b], 16 * TC * TOPK * (g // 2 + 1))
                acc = parts4[:, b, 0]
                for k in range(TOPK):
                    for j in range(TC):
                        ins = V.scalar_tensor_tensor(out=acc[:, j], in0=parts4[:, b, 2 + k, j],
                                                     scalar=share[:, g * TC + j, k:k + 1], in1=acc[:, j],
                                                     op0=ALU.mult, op1=ALU.add)
                    link(ins)
                layer_norm(acc, lnc)
                V.tensor_tensor(acc, lnc, parts4[:, b, 1], ALU.add).then_inc(out_ready, 1)

        @block.tensor
        def _(pe):
            T = nc.tensor

            def three(dst, ah, al, bh, bl, first=True, last=True):
                T.matmul(dst, ah, bh, start=first, stop=False)
                T.matmul(dst, ah, bl, start=False, stop=False)
                return T.matmul(dst, al, bh, start=False, stop=last)

            pe.wait_ge(in_const, 32)
            pe.wait_ge(small_lo, 1)
            for t in range(NT + 1):
                if t < NT:
                    pe.wait_ge(xn_ready, t + 1)
                    if t >= 2:
                        pe.wait_ge(xl_done, t - 1)
                    for k in range(KE):
                        ins = T.transpose(ps[:, t % 2, k * P:(k + 1) * P], xn[:, t % 2, k * P:(k + 1) * P], ident)
                    ins.then_inc(xt_ready, 1)
                if t > 0:
                    u = t - 1
                    pe.wait_ge(xl_done, u + 1)
                    if u >= 2:
                        pe.wait_ge(kva_done, u - 1)
                    for k in range(KE):
                        tok = slice(u * P, (u + 1) * P)
                        ins = three(ps[:, 2 + u % 2, 0:DK], xnTh[:, k, tok], xnTl[:, k, tok],
                                    wsmh[:, k, 0:DK], wsml[:, k, 0:DK], k == 0, k == KE - 1)
                    ins.then_inc(kva_ready, 1)
            pe.wait_ge(kfin_ready, 1)
            for t in range(NT):
                ins = T.transpose(ps[:, t // TC, t % TC * P:(t % TC + 1) * P], kv[:, t, :], ident)
                if t % TC == TC - 1:
                    ins.then_inc(kt_ready, 1)

            pe.wait_ge(in_wq, 16)
            pe.wait_ge(in_wkvb, 16)
            pe.wait_ge(in_wo, 16)
            for h in range(H + 1):
                if h < H:
                    if h >= 2:
                        pe.wait_ge(wt_done, h - 1)
                    b = 4 + h % 2
                    for k in range(KE):
                        T.transpose(ps[:, b, k * P:(k + 1) * P], wq_raw[:, k, h, 0:NOPE], ident)
                    for v in range(2):
                        ins = T.transpose(ps[:, b, 256 + v * LORA:256 + (v + 1) * LORA],
                                          wkvb_raw[0:LORA, h, v * NOPE:(v + 1) * NOPE], ident[0:LORA, 0:LORA])
                    ins.then_inc(wt_ready, 1)
                if h > 0:
                    g = h - 1
                    pe.wait_ge(wt_done, g + 1)
                    if g >= 2:
                        pe.wait_ge(wfl_done, g - 1)
                    b, w, o = 6 + g % 2, wT[:, g % 2, :], LORA * (g % 2)
                    for k in range(KE):
                        T.matmul(ps[:, b, k * LORA:(k + 1) * LORA], w[:, k * P:(k + 1) * P],
                                 w[:, 256:256 + LORA], start=True, stop=True)
                    T.matmul(ps[o:o + LORA, b, 128:384], w[:, 256 + LORA:384], wo_raw[:, g, :],
                             start=True, stop=True).then_inc(wf_ready, 1)

            for qc in range(NC):
                def project(tile, g):
                    n = qc * NT + tile * 4 + g
                    pe.wait_ge(q_done, n + 1)
                    tok = bass.ds((qc * TC + tile) * P, P)
                    for k in range(KE):
                        cols = slice(g * 512, (g + 1) * 512)
                        ins = three(ps[:, g % 2, :], xnTh[:, k, tok], xnTl[:, k, tok],
                                    WQh[:, k, cols], WQl[:, k, cols], k == 0, k == KE - 1)
                    ins.then_inc(q_ready, 1)

                def turn(tile, g):
                    n = qc * NT + tile * 4 + g
                    pe.wait_ge(rope_done, n + 1)
                    pe.wait_ge(ql_done, n + 1)
                    for h in range(4):
                        ins = T.transpose(ps[:, 2 + g % 2, h * P:(h + 1) * P], qs[:, g, h * P:(h + 1) * P], ident)
                    ins.then_inc(qt_ready, 1)

                if qc == 0:
                    pe.wait_ge(kl_done, NT // TC)
                    pe.wait_ge(pe_lo, 1)
                    pe.wait_ge(wfl_done, H)
                else:
                    pe.wait_ge(where_ready, qc)
                project(0, 0)
                project(0, 1)
                with pe.Fori(0, TC - 1) as i:
                    for g in range(2, 6):
                        project(i + g // 4, g % 4)
                        turn(i, g - 2)
                for g in range(2, 4):
                    project(TC - 1, g)
                    turn(TC - 1, g - 2)
                for g in range(2, 4):
                    turn(TC - 1, g)

                KT, U = TC * (qc + 1), units(qc)

                def max_unit(p, j):
                    s, i4, kc = j // (U // 2), j % (U // 2) // (qc + 1), j % (qc + 1)
                    w = CQ if kc < qc else P * (i4 + 1)
                    b = 4 + j % MX_RING
                    pe.wait_ge(mx_free, first_unit(qc) + p * U + j + 1)
                    ins = T.matmul(ps[:, b, 0:w], QTh[:, bass.ds((2 * p + s) * CQ + i4 * P, P)],
                                   KTh[:, kc * CQ:kc * CQ + w], start=True, stop=(kc < qc))
                    if kc == qc:
                        ins = T.matmul(ps[:, b, w - P:w], identb, mask_qk, start=False, stop=True)
                    ins.then_inc(mx_ready, 1)

                def turn_max(p, s):
                    k = (qc * NP + p) * 2 + s
                    pe.wait_ge(m_ready, k + 1)
                    if qc or s or not isinstance(p, int) or p:
                        pe.wait_ge(d_ready, k)
                    T.transpose(ps[0:TC, BK_M, s * P:(s + 1) * P], mrow[:, s, :], ident).then_inc(mt_ready, 1)

                def score_unit(p, i):
                    kt, s = i // 2, i % 2
                    j = kt - TC * qc
                    c0 = max(j, 0) * P
                    dst = ps[:, i % ST_RING, c0:]
                    q = bass.ds((2 * p + s) * CQ + c0, CQ - c0)
                    keys = slice(kt * P, (kt + 1) * P)
                    if i < 2:
                        pe.wait_ge(d_ready, (qc * NP + p) * 2 + s + 1)
                    pe.wait_ge(exp_done, first_unit(qc) + p * U + i + 1)
                    three(dst, KTh[:, keys], KTl[:, keys], QTh[:, q], QTl[:, q], True, False)
                    ins = T.matmul(dst, ones4, Dm[:, p % 2, s, c0:], start=False, stop=(j < 0))
                    if j >= 0:
                        ins = T.matmul(ps[:, i % ST_RING, c0:c0 + P], identb, mask_kq, start=False, stop=True)
                    ins.then_inc(st_ready, 1)

                def values(p, kt):
                    c0 = max(kt - TC * qc, 0) * P
                    if kt == 0:
                        pe.wait_ge(o_free, qc * NP + p + 1)
                    for s in range(2):
                        i = 2 * kt + s
                        pe.wait_ge(exp_done, CR_EXP + first_unit(qc) + p * U + i + 1)
                        T.matmul(ps[LORA * s:LORA * (s + 1), BK_O, c0:], kv[:, kt, 0:LORA],
                                 Pr[:, i % P_RING, c0:], start=(kt == 0), stop=(kt == KT - 1)).then_inc(pv_done, 1)

                def pair(p, ahead):
                    slot = 0

                    def between():
                        nonlocal slot
                        if ahead:
                            if slot < U:
                                max_unit(p + 1, slot)
                            if slot == U // 2 + 2:
                                turn_max(p + 1, 0)
                            if slot == U + 1:
                                turn_max(p + 1, 1)
                            slot += 1

                    for kt in range(KT):
                        score_unit(p, 2 * kt)
                        between()
                        score_unit(p, 2 * kt + 1)
                        between()
                        if kt >= LAG:
                            values(p, kt - LAG)
                        between()
                    for kt in range(KT - LAG, KT):
                        values(p, kt)

                pe.wait_ge(ql_done, CR + (qc + 1) * NT)
                for j in range(U):
                    max_unit(0, j)
                    if j == U // 2 + 2:
                        turn_max(0, 0)
                turn_max(0, 1)
                with pe.Fori(0, NP - 1) as p:
                    pair(p, True)
                pair(NP - 1, False)

                pe.wait_ge(l_done, CR_L + (qc + 1) * NP)
                parts = Lp[:, :, :].rearrange("p h (j b) -> p h j b", b=4)
                for b in range(4):
                    ins = T.matmul(ps[:, BK_M, 0:H * TC], selL[:, b, :], parts[:, :, :, b],
                                   start=(b == 0), stop=(b == 3))
                ins.then_inc(den_ready, 1)
                pe.wait_ge(o_free, CR_O + (qc + 1) * NP)

                def turn_out(j):
                    for b in range(2):
                        if j:
                            pe.wait_ge(on_ready, (qc * TC + j - 1) * 2 + b + 1)
                        for n in range(4):
                            o = (4 * b + n) * CQ + j * P
                            ins = T.transpose(ps[:, b, n * P:(n + 1) * P], OT[:, o:o + P], ident)
                        ins.then_inc(t1_ready, 1)

                turn_out(0)
                for j in range(TC):
                    for b in range(2):
                        pe.wait_ge(on_ready, (qc * TC + j) * 2 + b + 1)
                        if qc or j:
                            pe.wait_ge(ont_ready, (qc * TC + j - 1) * 2 + b + 1)
                        for n in range(4):
                            ins = T.transpose(ps[:, 2 + b, n * P:(n + 1) * P],
                                              On[:, j % 2, (4 * b + n) * P:(4 * b + n + 1) * P], ident)
                        ins.then_inc(t2_ready, 1)
                    if j + 1 < TC:
                        turn_out(j + 1)
                    pe.wait_ge(ont_ready, (qc * TC + j + 1) * 2)
                    if j >= 2:
                        pe.wait_ge(ysb_ready, qc * TC + j - 1)
                    for n in range(NP):
                        ins = T.matmul(ps[:, 4 + j % 2, 0:E], OnT[:, j % 2, n, :], WO[:, n, :],
                                       start=(n == 0), stop=(n == NP - 1))
                    ins.then_inc(mo_ready, 1)

                pe.wait_ge(xn2_ready, qc + 1)
                for k in range(KE):
                    for j in range(TC):
                        ins = T.transpose(ps[:, k, j * P:(j + 1) * P], lnt[:, j, k * P:(k + 1) * P], ident)
                    ins.then_inc(xt2_ready, 1)
                pe.wait_ge(x2l_done, (qc + 1) * KE)
                for j in range(TC):
                    for k in range(KE):
                        tok = slice(j * P, (j + 1) * P)
                        ins = three(ps[:, 6, j * NE:(j + 1) * NE], xn2h[:, k, tok], xn2l[:, k, tok],
                                    wsmh[:, k, DK:], wsml[:, k, DK:], k == 0, k == KE - 1)
                ins.then_inc(log_ready, 1)

                pe.wait_ge(pickb_ready, qc + 1)
                pk = pickb[:, :, :].rearrange("p t e -> p (t e)")
                T.matmul(ps[:, 6, 64:64 + TC * NE], before, pk, start=True, stop=True)
                T.matmul(ps[:, 6, 64 + TC * NE:64 + 2 * TC * NE], onesb, pk, start=True, stop=True).then_inc(rank_ready, 1)

            def turn_x(n, r, a, gathered):
                if gathered:
                    pe.wait_ge(xg_in[r], 16 * (a + 1 - NT // XR))
                else:
                    pe.wait_ge(row_in[r], 16 * (a + 1))
                pe.wait_ge(exl_done, n + 1)
                for k in range(KE):
                    ins = T.transpose(ps[:, r % 2, k * P:(k + 1) * P], xg[:, r, k * P:(k + 1) * P], ident)
                ins.then_inc(ex_ready, 1)

            def experts_of(a, tiles=2 * XR):
                return nc.values_load_multi_w_load_instructions(
                    expert_i[0:1, bass.ds((a - 1) * XR, tiles)], engines=[mybir.EngineType.PE],
                    min_val=0, max_val=NE,
                    skip_runtime_bounds_check_because="they are made as the least of a count and NE - 1")[1]

            def gate_up(n, r, e):
                pe.wait_ge(exl_done, CR + n + 1)
                pe.wait_ge(h_ready, n + 1)
                for k in range(KE):
                    w = slice(k * 2 * F, (k + 1) * 2 * F)
                    ins = three(ps[:, 2 + r, 0:2 * F], xgh[:, r, k], xgl[:, r, k], WEh[:, e, w], WEl[:, e, w],
                                k == 0, k == KE - 1)
                ins.then_inc(gu_ready, 1)

            def turn_h(n, r):
                pe.wait_ge(h_ready, CR + n + 1)
                pe.wait_ge(hl_done, n + 1)
                T.transpose(ps[:, 4 + r, 0:P], hx[:, r], ident).then_inc(ht_ready, 1)

            def down(n, r, e):
                pe.wait_ge(hl_done, CR + n + 1)
                pe.wait_ge(yo_ready, n + 1)
                w = slice(KE * 2 * F, KE * 2 * F + E)
                three(ps[:, 6 + r, 0:E], hh[:, r], hl[:, r], WEh[:, e, w], WEl[:, e, w]).then_inc(dn_done, 1)

            def step(n, r, a, experts, k=None, gathered=False):
                if k is None or k < GT:
                    turn_x(n, r, a, gathered)
                if k is None or 0 <= k - 1 < GT:
                    gate_up(n - 1, (r - 1) % 2, experts[XR + r - 1])
                if k is None or 0 <= k - 2 < GT:
                    turn_h(n - 2, r % 2)
                if k is None or 0 <= k - 3 < GT:
                    down(n - 3, (r - 3) % 2, experts[XR + r - 3])

            pe.wait_ge(raw_lo, 2 + NX)
            pe.wait_ge(where_ready, NC)
            shared = [NE] * 2 * XR
            for k in range(XR):
                step(k, k, 0, shared, k)
            with pe.Fori(1, NT // XR) as a:
                for r in range(XR):
                    step(XR * a + r, r, a, shared)
            pe.wait_ge(sel_ready, 1)
            pe.wait_ge(map_back, 16)
            pe.wait_ge(yo_ready, CR + NT - 3)
            for k in range(2):
                ins = T.matmul(ps[:, 7, 256:256 + MT], mapf[:, k, :], sel_t[:, k, :], start=(k == 0), stop=(k == 1))
            ins.then_inc(tok_done, 1)
            pe.wait_ge(tok_ready, 1)
            with pe.Fori(NT // XR, GT // XR) as a:
                experts = experts_of(a)
                for r in range(XR):
                    step(XR * a + r, r, a, experts, gathered=True)
            experts = experts_of(GT // XR, XR)
            for k in range(GT, GT + 3):
                step(k, k % XR, GT // XR, experts, k)


def constants():
    import numpy as np

    c = np.zeros((P, C_END), np.float32)
    c[:, C_ID:C_ID + P] = np.eye(P)
    pos = np.arange(S, dtype=np.float32)
    inv = np.float32(1.0) / np.float32(10000.0) ** (np.arange(0, ROPE, 2, dtype=np.float32) / np.float32(ROPE))
    ang = pos[:, None] * inv.astype(np.float32)
    cos, sin = np.cos(ang).astype(np.float32), np.sin(ang).astype(np.float32)
    c[:, C_COS:C_SIN] = cos.reshape(NT, P, ROPE // 2).transpose(1, 0, 2).reshape(P, -1)
    c[:, C_SIN:C_SEL] = np.concatenate([-sin, sin], 1).reshape(NT, P, ROPE).transpose(1, 0, 2).reshape(P, -1)
    sel = np.zeros((P, TC, P), np.float32)
    for b in range(TC):
        for a in range(4):
            sel[32 * a + np.arange(32), b, 32 * b + np.arange(32)] = 1
    c[:, C_SEL:C_BLK] = sel.reshape(P, -1)
    blk = np.zeros((P, TC, P), np.float32)
    for j in range(TC):
        blk[j, j] = -1
    c[:, C_IOTA:C_TOK] = np.arange(NE)
    c[:, C_TOK:C_ROW] = np.arange(P)[:, None] + P * np.arange(NT)
    c[:, C_ROW:C_TILE] = np.arange(P)[:, None] + P * np.arange(2)
    c[:, C_TILE:C_END] = np.arange(MT)
    row, col = np.arange(P)[:, None], np.arange(P)[None]
    ones4 = np.broadcast_to(row < TC, (P, P))
    b16 = np.concatenate([row == col, (col > row) * NEG, (col < row) * NEG, ones4, np.zeros((P, P)), row < col,
                          np.ones((P, P)), blk.reshape(P, -1)], 1)
    return c, (b16.astype(np.float32).view(np.uint32) >> 16).astype(np.uint16)


_INS = ['L0_attn_x', 'L0_attn_wq', 'L0_attn_wkv_a', 'L0_attn_wkv_b', 'L0_attn_wo', 'L0_attn_kv_norm_scale',
        'L0_ffn_gate_w', 'L0_ffn_expert_bias', 'L0_ffn_shared_gate_w', 'L0_ffn_shared_up_w',
        'L0_ffn_shared_down_w', 'L0_ffn_experts_gate_up', 'L0_ffn_experts_down']


def kernel(**inputs):
    import numpy as _np
    import concourse.bacc as _bacc
    from concourse import mybir as _mybir
    from concourse.bass_utils import run_bass_kernel_spmd as _run

    nc = _bacc.Bacc("TRN2", target_bir_lowering=False, num_devices=1)
    arrays, args = {}, []
    given = {name: _np.ascontiguousarray(inputs[name]) for name in _INS}
    given["table_f32"], given["table_bf16"] = constants()
    for name, a in given.items():
        arrays[f"in_{name}"] = a
        args.append(nc.dram_tensor(f"in_{name}", a.shape, _mybir.dt.from_np(a.dtype), kind="ExternalInput").ap())
    args.append(nc.dram_tensor("out_0", (1, S, E), F32, kind="ExternalOutput").ap())
    attention_moe(nc, *args)
    r = _run(nc, [arrays], core_ids=[0])
    return r.results[0]["out_0"]
```

```python
from contextlib import ExitStack

import concourse.bass as bass
from concourse import mybir

F32 = mybir.dt.float32
F16 = mybir.dt.float16
BF16 = mybir.dt.bfloat16
U32 = mybir.dt.uint32
ALU = mybir.AluOpType
ACT = mybir.ActivationFunctionType
AX = mybir.AxisListType

P = 128
S, E = 2048, 256
NT = S // P
KE = E // P
H, NOPE, ROPE, VD, LORA = 16, 128, 64, 128, 64
QH = NOPE + ROPE
DK = LORA + ROPE
NP = H // 2
CQ = 512
NC = S // CQ
TC = CQ // P
HG = 4
QG = TC * H // HG
NE, F = 16, 128
NX = NE + 1
TOPK = 2
SHIFT_FROM = 2
MT = (TOPK * S + NE * (P - 1)) // P + 1
GT = NT + MT
XR = 4
SM_SCALE = float(QH) ** -0.5
LN_EPS, RMS_EPS = 1e-5, 1e-6
WS = 64.0
RAW = KE * 2 * F + E
LAG = 2
ST_RING, MX_RING, P_RING = 4, 2, 8
KT_AFTER, PE_AFTER = 7, 12
NEG = -1e30

OUT_PARTS = [(g, j, j + TC // 2) for g in range(NC) for j in (0, TC // 2)]

C_ID, C_COS, C_SIN = 0, P, P + NT * ROPE // 2
C_SEL = C_SIN + NT * ROPE
C_BLK = C_SEL + TC * P
C_IOTA = C_BLK
C_TOK = C_IOTA + NE
C_ROW = C_TOK + NT
C_TILE = C_ROW + 2
C_END = C_TILE + MT


def attention_moe(nc, x, wq, wkv_a, wkv_b, wo, kv_scale, gate_w, bias, sh_gate, sh_up, sh_down,
                  ex_gu, ex_down, c32_d, c16_d, out):
    with ExitStack() as ctx:
        def sb(name, shape, dt=F32):
            return ctx.enter_context(nc.sbuf_tensor(name, shape, dt))

        def sem(name):
            return ctx.enter_context(nc.semaphore(name))

        c32 = sb("c32", [P, C_END])
        c16 = sb("c16", [P, (7 + TC) * P], BF16)
        kvs = sb("kvs", [P, LORA])
        biasb = sb("biasb", [P, NE])
        xnTh = sb("xnTh", [P, KE, S], F16)
        xnTl = sb("xnTl", [P, KE, S], F16)
        WQh = sb("WQh", [P, KE, H * DK], F16)
        WQl = sb("WQl", [P, KE, H * DK], F16)
        WO = sb("WO", [P, NP, E])
        kv = sb("kv", [P, NT, DK])
        KTh = sb("KTh", [P, S], F16)
        KTl = sb("KTl", [P, S], F16)
        WEh = sb("WEh", [P, NX, KE * 2 * F + E], F16)
        WEl = sb("WEl", [P, NX, KE * 2 * F + E], F16)
        wsmh = sb("wsmh", [P, KE, DK + NE], F16)
        wsml = sb("wsml", [P, KE, DK + NE], F16)
        st6 = sb("st6", [P, NT, 6])
        mv = sb("mv", [P, NT, 2])
        var = sb("var", [P, NT])
        std = sb("std", [P, NT])
        rstd = sb("rstd", [P, NT])
        shiftb = sb("shiftb", [P, NT])
        mxp = sb("mxp", [P, 2, TC, NC])
        mrow = sb("mrow", [P, 2, TC])
        Lp = sb("Lp", [P, H, CQ // 32])
        rL = sb("rL", [P, H, TC])
        sig = sb("sig", [P, TC, NE])
        sgb = sb("sgb", [P, TC, NE])
        top8 = sb("top8", [P, TC, 8])
        idx8 = sb("idx8", [P, TC, 8], U32)
        idxf = sb("idxf", [P, TC, 8])
        pick = sb("pick", [P, TOPK, NT, NE], BF16)
        pickb = sb("pickb", [P, TC, NE], BF16)
        share = sb("share", [P, NT, TOPK])
        rsum = sb("rsum", [P, 2, TC])
        counts = sb("counts", [P, 2, NE])
        place = sb("place", [P, TC, NE])
        where = sb("where", [P, NT, TOPK])
        where_i = sb("where_i", [P, NT, TOPK], U32)
        res_i = sb("res_i", [P, NT, TOPK], U32)
        tok_i = sb("tok_i", [P, MT], U32)
        expert_i = sb("expert_i", [P, GT], U32)

        A = sb("A", [P, 8192])
        B = sb("B", [P, 4096])
        C = sb("C", [P, 4096])
        D = sb("D", [P, 4096])

        wq_raw = A[:, 0:KE * H * QH].rearrange("p (k h c) -> p k h c", k=KE, h=H)
        wT = A[:, 6144:6144 + 768].rearrange("p (r c) -> p r c", r=2)
        xn = A[:, 6912:6912 + 512].rearrange("p (r c) -> p r c", r=2)
        QTh = A[:, 0:4096].bitcast(F16)
        QTl = A[:, 4096:8192].bitcast(F16)
        On = A[:, 1024:3072].rearrange("p (r c) -> p r c", r=2)
        OnT = A[:, 3072:5120].rearrange("p (r n c) -> p r n c", r=2, n=NP)
        xs = B[:, :].rearrange("p (t e) -> p t e", t=NT)
        Pr = B[:, :].rearrange("p (r q) -> p r q", r=P_RING)
        xg = B[:, 0:1024].rearrange("p (r e) -> p r e", r=XR)
        yo = B[:, 1024:2048].rearrange("p (r e) -> p r e", r=XR)
        sg = B[:, 3072:3328].rearrange("p (r f) -> p r f", r=2)
        hx = B[:, 3328:3584].rearrange("p (r f) -> p r f", r=2)
        hh = B[:, 3584:3712].bitcast(F16).rearrange("p (r c) -> p r c", r=2)
        hl = B[:, 3712:3840].bitcast(F16).rearrange("p (r c) -> p r c", r=2)
        xgh = C[:, 0:256].bitcast(F16).rearrange("p (r k c) -> p r k c", r=2, k=KE)
        xgl = C[:, 256:512].bitcast(F16).rearrange("p (r k c) -> p r k c", r=2, k=KE)
        scr = C[:, 1024:4096]
        mapf = D[:, 0:2 * P].rearrange("p (k c) -> p k c", k=2)
        sel_t = D[:, 512:512 + 2 * MT].rearrange("p (k m) -> p k m", k=2)
        xr, ysb, lnt, x1 = (B[:, i * TC * E:(i + 1) * TC * E].rearrange("p (t e) -> p t e", t=TC) for i in range(4))
        xn2h, xn2l = (D[:, i * CQ:(i + 1) * CQ].bitcast(F16).rearrange("p (k t) -> p k t", k=KE) for i in range(2))
        wkvb_raw = C[:, :].rearrange("p (h c) -> p h c", h=H)
        qs = C[:, 0:2048].rearrange("p (r c) -> p r c", r=4)
        ropA = C[:, 2048:2560].rearrange("p (r h c) -> p r h c", r=2, h=HG)
        ropB = C[:, 2560:3072].rearrange("p (r h c) -> p r h c", r=2, h=HG)
        OT = C[:, :]
        wo_raw = D[:, 0:4096].rearrange("p (h e) -> p h e", h=H)
        Pacc = D[:, 0:2048].rearrange("p (r s q) -> p r s q", r=2, s=2)
        Dm = D[:, 2048:3072].bitcast(BF16).rearrange("p (r s q) -> p r s q", r=2, s=2)
        minus_m = D[:, 3072:4096].rearrange("p (r q) -> p r q", r=2)
        stage = xnTl[:, :, :].rearrange("p k s -> p (k s)").bitcast(F32)[:, 0:2 * RAW].rearrange("p (r c) -> p r c", r=2)
        kvt = WEl[:, 0:6, :].rearrange("p a b -> p (a b)")
        wsm = WEl[:, 8, 0:2 * KE * (DK + NE)].bitcast(F32).rearrange("p (k c) -> p k c", k=KE)
        kvtA = kvt[:, 0:2048].bitcast(F32).rearrange("p (t c) -> p t c", t=NT)
        kvtB = kvt[:, 2048:4096].bitcast(F32).rearrange("p (t c) -> p t c", t=NT)

        ident = c32[:, C_ID:C_ID + P]
        cosT = c32[:, C_COS:C_SIN].rearrange("p (t c) -> p t c", t=NT)
        sinT = c32[:, C_SIN:C_SEL].rearrange("p (t c) -> p t c", t=NT)
        selL = c32[:, C_SEL:C_BLK].rearrange("p (b m) -> p b m", b=TC)
        negblk = c16[0:TC, 7 * P:11 * P].rearrange("p (j q) -> p j q", j=TC)
        iota = c32[:, C_IOTA:C_TOK]
        token = c32[:, C_TOK:C_ROW]
        row_id = c32[:, C_ROW:C_TILE]
        tile_id = c32[:, C_TILE:C_END]
        identb, mask_qk, mask_kq, ones4, zerob, before, onesb = (c16[:, i * P:(i + 1) * P] for i in range(7))

        xn2_d = nc.dram_tensor("xn2_rows", (S, E), F32, kind="Internal").ap()
        x1_d = nc.dram_tensor("x1_rows", (S, E), F32, kind="Internal").ap()
        res_d = nc.dram_tensor("results", (GT * P, E), F32, kind="Internal").ap()
        map_d = nc.dram_tensor("token_map", (NE * S, 1), F32, kind="Internal").ap()

        ps = ctx.enter_context(nc.psum_tensor("ps", [P, 8, 512], F32))
        BK_O, BK_M = 6, 7

        in_const, in_wa, in_wq, in_wkvb, in_wo = map(sem, ("in_const", "in_wa", "in_wq", "in_wkvb", "in_wo"))
        in_x = [sem(f"in_x_{g}") for g in range(NC)]
        var_ready, std_ready = map(sem, ("var_ready", "std_ready"))
        xn_ready, xt_ready, xh_done, xl_done = map(sem, ("xn_ready", "xt_ready", "xh_done", "xl_done"))
        kva_ready, kva_done = map(sem, ("kva_ready", "kva_done"))
        kfin_ready, kt_ready, kh_done, kl_done = map(sem, ("kfin_ready", "kt_ready", "kh_done", "kl_done"))
        wt_ready, wt_done, wf_ready, wfh_done, wfl_done = map(sem, (
            "wt_ready", "wt_done", "wf_ready", "wfh_done", "wfl_done"))
        small_hi, small_lo, pe_hi, pe_lo = map(sem, ("small_hi", "small_lo", "pe_hi", "pe_lo"))
        dve_seq = sem("dve_seq")
        dm_zero = sem("dm_zero")
        q_ready, q_done, cos_done, sin_done, rope_done, qt_ready, qh_done, ql_done = map(sem, (
            "q_ready", "q_done", "cos_done", "sin_done", "rope_done", "qt_ready", "qh_done", "ql_done"))
        mx_ready, mx_free, m_ready, mt_ready, d_ready = map(sem, (
            "mx_ready", "mx_free", "m_ready", "mt_ready", "d_ready"))
        wide_ready, wide_done, shifted = map(sem, ("wide_ready", "wide_done", "shifted"))
        st_ready, exp_done, pv_done, sum_done, l_done, o_free = map(sem, (
            "st_ready", "exp_done", "pv_done", "sum_done", "l_done", "o_free"))
        raw_gu_in = [sem(f"raw_gu_in_{r}") for r in range(2)]
        raw_dn_in = [sem(f"raw_dn_in_{r}") for r in range(2)]
        shared_in, raw_hi, raw_lo = map(sem, ("shared_in", "raw_hi", "raw_lo"))
        den_ready, t1_ready, on_ready, t2_ready, ont_ready, mo_ready, ysb_ready = map(sem, (
            "den_ready", "t1_ready", "on_ready", "t2_ready", "ont_ready", "mo_ready", "ysb_ready"))
        xr_in, xn2_ready, xt2_ready, x2h_done, x2l_done = map(sem, (
            "xr_in", "xn2_ready", "xt2_ready", "x2h_done", "x2l_done"))
        log_ready, sig_ready, pickb_ready, rank_ready, where_ready = map(sem, (
            "log_ready", "sig_ready", "pickb_ready", "rank_ready", "where_ready"))
        map_zero, map_in, map_back, rows_out = map(sem, ("map_zero", "map_in", "map_back", "rows_out"))
        sel_ready, tok_ready, tok_done, res_ready = map(sem, ("sel_ready", "tok_ready", "tok_done", "res_ready"))
        row_in = [sem(f"row_in_{r}") for r in range(XR)]
        xg_in = [sem(f"xg_in_{r}") for r in range(XR)]
        res_out = [sem(f"res_out_{r}") for r in range(XR)]
        ex_ready, exh_done, exl_done, gu_ready, silu_done, h_ready, ht_ready, hh_done, hl_done, dn_done, yo_ready = map(
            sem, ("ex_ready", "exh_done", "exl_done", "gu_ready", "silu_done", "h_ready", "ht_ready", "hh_done",
                  "hl_done", "dn_done", "yo_ready"))
        own_in = [sem(f"own_in_{g}") for g in range(NC)]
        got_in = [sem(f"got_in_{k}") for k in range(len(OUT_PARTS))]
        shift_ready, normed, out_ready, out_done = map(sem, ("shift_ready", "normed", "out_ready", "out_done"))

        CR_EXP, CR_PV, CR_SUM, CR_MX, CR_L, CR_O, CR = ST_RING, P_RING, P_RING, MX_RING, 2, 1, 2

        def units(qc):
            return 2 * TC * (qc + 1)

        def spread_slots(qc):
            return (units(qc) + 3, units(qc) + 5) if qc >= SHIFT_FROM else ()

        def shifts(qc, p):
            return (first_unit(qc) - first_unit(SHIFT_FROM)) // 2 + p * (units(qc) // 2)

        def spreads(qc, p):
            return 2 * ((qc - SHIFT_FROM) * NP + p)

        HR = ROPE // 2

        def pe_of(g):
            return qs[:, g, :].rearrange("p (h c) -> p h c", c=DK)[:, :, LORA:]

        def first_unit(qc):
            return sum(NP * units(q) for q in range(qc))

        x_tiles = x.rearrange("b (t p) e -> p (b t) e", p=P)
        out_tiles = out.rearrange("b (t p) e -> p (b t) e", p=P)
        xn2_tiles = xn2_d.rearrange("(t p) e -> p t e", p=P)
        x1_tiles = x1_d.rearrange("(t p) e -> p t e", p=P)
        res_tiles = res_d.rearrange("(t p) e -> p t e", p=P)
        gu_d = ex_gu.rearrange("e (k p) f -> e p k f", p=P)

        def parts_of(g, w):
            if g < 2:
                mem, k = A, 4 * g + w
            else:
                mem, k = ((WQh, WQl), (xnTh, xnTl))[g - 2][w // 2][:, :, :].rearrange("p k c -> p (k c)").bitcast(F32), w % 2
            return mem[:, k * TC * E:(k + 1) * TC * E].rearrange("p (t e) -> p t e", t=TC)

        block = ctx.enter_context(nc.Block())

        @block.sync
        def _(sp):
            for g in range(NC):
                tiles = slice(g * TC, (g + 1) * TC)
                sp.dma_start(xs[:, tiles, :], x_tiles[:, tiles, :]).then_inc(in_x[g], 16)
            sp.dma_start(wq_raw, wq.rearrange("(k p) (h c) -> p k h c", p=P, c=QH)).then_inc(in_wq, 16)
            sp.dma_start(wo_raw, wo.rearrange("(h p) e -> p h e", p=P)).then_inc(in_wo, 16)

            sp.wait_ge(in_const, 32)
            sp.dma_start(map_d.rearrange("(p b c) o -> p b (c o)", p=P, c=P // 2),
                         zerob.bitcast(F32).unsqueeze(1).broadcast_to([P, NE * S // P // (P // 2), P // 2])
                         ).then_inc(map_zero, 16)

            def load_expert(e, r):
                sp.wait_ge(raw_lo, e + 2)
                slot = 1 - r
                sp.dma_start(stage[:, slot, 0:KE * 2 * F].rearrange("p (k f) -> p k f", k=KE),
                             gu_d[e]).then_inc(raw_gu_in[slot], 16)
                sp.dma_start(stage[:, slot, KE * 2 * F:], ex_down[e]).then_inc(raw_dn_in[slot], 16)

            for qc in range(NC):
                tiles = slice(qc * TC, (qc + 1) * TC)
                if qc == NC - 1:
                    sp.wait_ge(q_ready, NC * QG)
                    for k in range(KE):
                        c = k * 2 * F
                        sp.dma_start(stage[:, 0, c:c + F], sh_gate[k * P:(k + 1) * P, :]).then_inc(shared_in, 16)
                        sp.dma_start(stage[:, 0, c + F:c + 2 * F], sh_up[k * P:(k + 1) * P, :]).then_inc(shared_in, 16)
                    sp.dma_start(stage[:, 0, KE * 2 * F:], sh_down).then_inc(shared_in, 16)
                    with sp.Fori(0, NE // 2) as i:
                        for r in range(2):
                            load_expert(2 * i + r, r)
                sp.wait_ge(pv_done, CR_PV + first_unit(qc + 1))
                sp.wait_ge(sum_done, CR_SUM + first_unit(qc + 1))
                sp.dma_start(xr, x_tiles[:, tiles, :]).then_inc(xr_in, 16)
                sp.wait_ge(xn2_ready, (qc + 1) * TC)
                sp.dma_start(xn2_tiles[:, tiles, :], lnt).then_inc(rows_out, 16)
                sp.dma_start(x1_tiles[:, tiles, :], x1).then_inc(rows_out, 16)

            def load_own(n):
                if n >= XR:
                    sp.wait_ge(ex_ready, n - XR + 1)
                sp.dma_start(xg[:, n % XR, :], xn2_tiles[:, n, :]).then_inc(row_in[n % XR], 16)

            def store(n, r):
                sp.wait_ge(yo_ready, CR + n + 1)
                sp.dma_start(res_tiles[:, n, :], yo[:, r, :]).then_inc(res_out[r], 16)

            sp.wait_ge(rows_out, 32 * NC)
            for n in range(XR):
                load_own(n)
            for n in range(XR, NT):
                load_own(n)
                if n - XR - 3 >= 0:
                    store(n - XR - 3, (n - XR - 3) % XR)
                if n == NT - XR - 2:
                    sp.wait_ge(map_in, 16 * NT * TOPK)
                    sp.dma_start(mapf, map_d.rearrange("(k r c) o -> r k (c o)", k=2, c=P)).then_inc(map_back, 16)
            for n in range(NT - XR - 3, NT - XR):
                store(n, n % XR)
            for n in range(NT - XR, NT):
                store(n, n % XR)
            turns = MT // XR // NC
            for g in range(NC):
                tiles = slice(g * TC, (g + 1) * TC)
                a0 = NT // XR + turns * g
                for r in range(XR):
                    store(XR * a0 + r, r)
                if g == 0:
                    for r in range(XR):
                        sp.wait_ge(res_out[r], 16 + 16 * (NT // XR))
                sp.dma_start(parts_of(g, 0), res_tiles[:, tiles, :]).then_inc(own_in[g], 16)
                with sp.Fori(a0 + 1, a0 + turns) as a:
                    for r in range(XR):
                        store(XR * a + r, r)
                sp.dma_start(parts_of(g, 1), x1_tiles[:, tiles, :]).then_inc(own_in[g], 16)
            for g in range(NC):
                sp.wait_ge(out_ready, 2 * (g + 1))
                sp.dma_start(out_tiles[:, g * TC:(g + 1) * TC, :], parts_of(g, 0)).then_inc(out_done, 16)
            sp.wait_ge(out_done, 16 * NC)

        @block.gpsimd
        def _(pool):
            def add_up(qc, p, half):
                KT = TC * (qc + 1)
                n0 = first_unit(qc) + p * units(qc)
                pool.wait_ge(l_done, qc * NP + p + 1)
                for kt in range(1, KT):
                    c0 = max(kt - TC * qc, 0) * P
                    for s in range(2):
                        n, i = n0 + 2 * kt + s, 2 * kt + s
                        pool.wait_ge(exp_done, CR_EXP + n + 1)
                        acc = Pacc[:, half, s, :]
                        if kt == 1:
                            ins = nc.gpsimd.tensor_tensor(acc[:, c0:], Pr[:, s, c0:], Pr[:, i, c0:], ALU.add)
                            if c0:
                                ins = nc.gpsimd.tensor_copy(acc[:, 0:c0], Pr[:, s, 0:c0])
                            ins.then_inc(sum_done, 1 + 2 * s)
                        else:
                            pool.wait_ge(sum_done, CR_SUM + n - 1)
                            nc.gpsimd.tensor_tensor(acc[:, c0:], acc[:, c0:], Pr[:, i % P_RING, c0:],
                                                    ALU.add).then_inc(sum_done, 1)

            def rotate(qc, tile, g):
                n = qc * QG + tile * HG + g
                pool.wait_ge(q_done, CR + n + 1)
                for dst, src in ((slice(0, HR), slice(HR, ROPE)), (slice(HR, ROPE), slice(0, HR))):
                    sine = sinT[:, qc * TC + tile, dst].unsqueeze(1).broadcast_to([P, HG, HR])
                    ins = nc.gpsimd.tensor_tensor(ropB[:, g % 2, :, dst], pe_of(g)[:, :, src], sine, ALU.mult)
                ins.then_inc(sin_done, 1)
                pool.wait_ge(sin_done, n + 1)
                pool.wait_ge(cos_done, n + 1)
                nc.gpsimd.tensor_tensor(pe_of(g), ropA[:, g % 2], ropB[:, g % 2], ALU.add).then_inc(rope_done, 1)

            def gather(dst, rows, index, done):
                nc.gpsimd.indirect_dma_start(
                    out=dst, out_offset=None, in_=rows,
                    in_offset=bass.IndirectOffsetOnAxis(ap=index, axis=0)).then_inc(done, 16)

            pool.wait_ge(in_const, 32)
            def scatter(qc, t, k):
                if t == qc * TC and k == 0:
                    if qc == 0:
                        pool.wait_ge(map_zero, 16)
                    pool.wait_ge(where_ready, qc + 1)
                nc.gpsimd.indirect_dma_start(
                    out=map_d, out_offset=bass.IndirectOffsetOnAxis(ap=where_i[:, t, k:k + 1], axis=0),
                    in_=token[:, t:t + 1], in_offset=None).then_inc(map_in, 16)

            for qc in range(NC):
                for tile in range(TC):
                    for g in range(HG):
                        rotate(qc, tile, g)
                if qc:
                    for k in range(TOPK):
                        for j in range(TC):
                            scatter(qc - 1, (qc - 1) * TC + j, k)
                with pool.Fori(0, NP // 2) as i:
                    add_up(qc, 2 * i, 0)
                    add_up(qc, 2 * i + 1, 1)
            for k in range(TOPK):
                for j in range(TC):
                    scatter(NC - 1, (NC - 1) * TC + j, k)
            pool.wait_ge(tok_ready, 1)
            for n in range(NT, GT):
                pool.wait_ge(ex_ready, n - XR + 1)
                gather(xg[:, n % XR, :], xn2_d, tok_i[:, n - NT:n - NT + 1], xg_in[n % XR])
            pool.wait_ge(res_ready, 1)
            for r in range(XR):
                pool.wait_ge(res_out[r], 16 + 16 * (GT // XR))
            for (g, first, n), got in zip(OUT_PARTS, got_in):
                for j in range(first, n):
                    for k in range(TOPK):
                        gather(parts_of(g, 2 + k)[:, j], res_d, res_i[:, g * TC + j, k:k + 1], got)

        @block.scalar
        def _(act):
            act.dma_start(wsm[:, :, 0:DK], wkv_a.rearrange("(k p) c -> p k c", p=P)).then_inc(in_wa, 16)
            act.dma_start(wsm[:, :, DK:], gate_w.rearrange("(k p) c -> p k c", p=P)).then_inc(in_wa, 16)
            act.dma_start(kvs[:, :], kv_scale.rearrange("(a c) -> a c", a=1).broadcast_to([P, LORA])).then_inc(in_wa, 16)
            act.dma_start(biasb[:, :], bias.rearrange("(a c) -> a c", a=1).broadcast_to([P, NE])).then_inc(in_wa, 16)
            act.dma_start(c32[:, :], c32_d).then_inc(in_const, 16)
            act.dma_start(c16[:, :], c16_d.bitcast(BF16)).then_inc(in_const, 16)
            act.dma_start(wkvb_raw[0:LORA], wkv_b.rearrange("c (h n) -> c h n", h=H)).then_inc(in_wkvb, 16)

            def copy(dst, src, scale=1.0):
                return nc.scalar.activation(dst, src, ACT.Copy, scale=scale)

            act.wait_ge(in_wa, 64)
            copy(wsmh[:, :, :], wsm[:, :, :], WS).then_inc(small_hi, 1)
            act.wait_ge(var_ready, 1)
            nc.scalar.activation(std[:, :], var[:, :], ACT.Sqrt).then_inc(std_ready, 1)

            for t in range(NT + 1):
                if t < NT:
                    act.wait_ge(xt_ready, t + 1)
                    copy(xnTh[:, :, t * P:(t + 1) * P],
                         ps[:, t % 2, 0:E].rearrange("p (k c) -> p k c", k=KE)).then_inc(xh_done, 1)
                if t > 0:
                    act.wait_ge(kva_ready, t)
                    copy(kv[:, t - 1, :], ps[:, 2 + (t - 1) % 2, 0:DK], 1 / WS).then_inc(kva_done, 1)
            for h in range(H + 1):
                if h < H:
                    act.wait_ge(wt_ready, h + 1)
                    if h >= 2:
                        act.wait_ge(wf_ready, h - 1)
                    copy(wT[:, h % 2, :], ps[:, 4 + h % 2, 0:384]).then_inc(wt_done, 1)
                if h > 0:
                    g = h - 1
                    act.wait_ge(wf_ready, g + 1)
                    o = LORA * (g % 2)
                    copy(WO[o:o + LORA, g // 2, :], ps[o:o + LORA, 6 + g % 2, 128:384])
                    copy(WQh[:, :, g * DK:g * DK + LORA],
                         ps[:, 6 + g % 2, 0:128].rearrange("p (k c) -> p k c", k=KE), WS).then_inc(wfh_done, 1)
                    if g == 1:
                        act.wait_ge(var_ready, 2)
                        nc.scalar.activation(std[:, :], var[:, :], ACT.Sqrt).then_inc(std_ready, 1)
                    if KT_AFTER < g <= KT_AFTER + NT // TC:
                        b = g - KT_AFTER - 1
                        act.wait_ge(kt_ready, b + 1)
                        copy(KTh[:, b * CQ:(b + 1) * CQ], ps[:, b, :]).then_inc(kh_done, 1)
                    if g == PE_AFTER:
                        act.wait_ge(in_wq, 16)
                        copy(WQh[:, :, :].rearrange("p k (h c) -> p (k h) c", c=DK)[:, :, LORA:],
                             wq_raw.rearrange("p k h c -> p (k h) c")[:, :, NOPE:], WS).then_inc(pe_hi, 1)

            def scores_to_probs(qc, p):
                KT = TC * (qc + 1)
                n0 = first_unit(qc) + p * units(qc)
                cuts = (KT, KT + 6)
                for i in range(2 * KT):
                    n = n0 + i
                    c0 = max(i // 2 - TC * qc, 0) * P
                    if i % 2 == 0 or qc < SHIFT_FROM:
                        act.wait_ge(st_ready, n + 1)
                    else:
                        act.wait_ge(shifted, shifts(qc, p) + i // 2 + 1)
                    act.wait_ge(pv_done, n + 1)
                    act.wait_ge(sum_done, n + 1)
                    nc.scalar.activation(Pr[:, i % P_RING, c0:], ps[:, i % ST_RING, c0:], ACT.Exp,
                                         scale=SM_SCALE).then_inc(exp_done, 1)
                    if qc == NC - 1 and i in cuts:
                        cut_expert(p, cuts.index(i))
                act.wait_ge(pv_done, CR_PV + n0 + 2 * KT)
                copy(OT[:, bass.ds(p * CQ, CQ)], ps[:, BK_O, :]).then_inc(o_free, 1)

            def cut_expert(p, r):
                act.wait_ge(raw_gu_in[1 - r], (p + 1) * 16)
                act.wait_ge(raw_dn_in[1 - r], (p + 1) * 16)
                copy(WEh[:, 2 * p + r, :], stage[:, 1 - r, :], WS).then_inc(raw_hi, 1)

            def root(qc, j, r):
                act.wait_ge(var_ready, 2 + (qc * TC + j) * 2 + r + 1)
                nc.scalar.activation(std[:, j:j + 1], var[:, j:j + 1], ACT.Sqrt).then_inc(std_ready, 1)

            def xn2_high(qc):
                for k in range(KE):
                    act.wait_ge(xt2_ready, qc * KE + k + 1)
                    copy(xn2h[:, k, :], ps[:, 4 + k, :]).then_inc(x2h_done, 1)

            def sigmoids(qc):
                act.wait_ge(log_ready, qc + 1)
                nc.scalar.activation(sig[:, :, :].rearrange("p t e -> p (t e)"), ps[:, 6, 0:TC * NE],
                                     ACT.Sigmoid, scale=1 / WS).then_inc(sig_ready, 1)

            for qc in range(NC):
                if qc == 0:
                    act.wait_ge(pe_lo, 1)
                    act.wait_ge(wfl_done, H)
                def q_out(tile, g):
                    n = qc * QG + tile * HG + g
                    act.wait_ge(q_ready, n + 1)
                    copy(qs[:, g, :], ps[:, g % 2, :], 1 / WS).then_inc(q_done, 1)

                def q_high(tile, g):
                    n = qc * QG + tile * HG + g
                    act.wait_ge(qt_ready, n + 1)
                    dst = QTh.rearrange("p (h q) -> p h q", h=H)[:, 4 * g:4 * g + 4, bass.ds(tile * P, P)]
                    copy(dst, ps[:, 2 + g % 2, :].rearrange("p (h q) -> p h q", h=HG)).then_inc(qh_done, 1)

                for k in range(QG + 2):
                    if k < QG:
                        q_out(k // HG, k % HG)
                    if k >= 2:
                        q_high((k - 2) // HG, (k - 2) % HG)
                    if qc and k == 0:
                        root(qc - 1, TC - 1, 1)
                    if qc and k == 2:
                        xn2_high(qc - 1)
                    if qc and k == 5:
                        sigmoids(qc - 1)

                if qc:
                    act.wait_ge(rows_out, 32 * qc)
                if qc == NC - 1:
                    act.wait_ge(shared_in, 80)
                    copy(WEh[:, NE, :], stage[:, 0, :], WS).then_inc(raw_hi, 1)
                with act.Fori(0, NP) as p:
                    scores_to_probs(qc, p)
                def turned(j):
                    for b in range(2):
                        act.wait_ge(t2_ready, (qc * TC + j) * 2 + b + 1)
                        copy(OnT[:, j % 2, 4 * b:4 * b + 4, :],
                             ps[:, 2 + b, :].rearrange("p (n q) -> p n q", n=4)).then_inc(ont_ready, 1)

                turned(0)
                for j in range(TC):
                    if j + 1 < TC:
                        turned(j + 1)
                    if j:
                        root(qc, j - 1, 1)
                    act.wait_ge(mo_ready, qc * TC + j + 1)
                    copy(ysb[:, j, :], ps[:, 4 + j % 2, 0:E]).then_inc(ysb_ready, 1)
                    root(qc, j, 0)
            root(NC - 1, TC - 1, 1)
            xn2_high(NC - 1)
            sigmoids(NC - 1)

            def x_high(n, r):
                act.wait_ge(ex_ready, n + 1)
                act.wait_ge(gu_ready, n + 1)
                copy(xgh[:, r], ps[:, r, 0:E].rearrange("p (k c) -> p k c", k=KE)).then_inc(exh_done, 1)

            def silu(n, r):
                act.wait_ge(gu_ready, CR + n + 1)
                act.wait_ge(h_ready, n + 1)
                nc.scalar.activation(sg[:, r], ps[:, 2 + r, 0:F], ACT.Silu, scale=1 / WS).then_inc(silu_done, 1)

            def h_high(n, r):
                act.wait_ge(ht_ready, CR + n + 1)
                act.wait_ge(dn_done, n + 1)
                copy(hh[:, r], ps[:, 4 + r, 0:P]).then_inc(hh_done, 1)

            def result(n, r, turn):
                act.wait_ge(dn_done, CR + n + 1)
                act.wait_ge(res_out[r], 16 * (turn + 1))
                copy(yo[:, r, :], ps[:, 6 + r % 2, 0:E], 1 / WS).then_inc(yo_ready, 1)

            def step(n, r, a, k=None):
                if k is None or k < GT:
                    x_high(n, r % 2)
                if k is None or 0 <= k - 1 < GT:
                    silu(n - 1, (r - 1) % 2)
                if k is None or 0 <= k - 2 < GT:
                    h_high(n - 2, r % 2)
                if k is None or 0 <= k - 3 < GT:
                    result(n - 3, (r - 3) % XR, a - (r < 3))

            act.wait_ge(rows_out, 32 * NC)
            for k in range(XR):
                step(k, k, 0, k)
            with act.Fori(1, GT // XR) as a:
                for r in range(XR):
                    step(XR * a + r, r, a)
            for k in range(GT, GT + 3):
                step(k, k % XR, GT // XR, k)

            def last_norm(k, g, first, n):
                tiles = slice(g * TC + first, g * TC + n)
                act.wait_ge(var_ready, 2 + 2 * NT + k + 1)
                nc.scalar.activation(std[:, tiles], var[:, tiles], ACT.Sqrt).then_inc(std_ready, 1)
                act.wait_ge(shift_ready, k + 1)
                for j in range(first, n):
                    t, acc = g * TC + j, parts_of(g, 0)[:, j]
                    ins = nc.scalar.activation(acc, acc, ACT.Identity, bias=shiftb[:, t:t + 1], scale=rstd[:, t:t + 1])
                ins.then_inc(normed, 1)

            for k, (g, first, n) in enumerate(OUT_PARTS):
                last_norm(k, g, first, n)

        @block.vector
        def _(dve):
            steps = [0]

            def link(ins):
                steps[0] += 1
                ins.then_inc(dve_seq, 1)
                dve.wait_ge(dve_seq, steps[0])

            V = nc.vector

            V.memset(mxp[:, 0, 0, 0:1], 0.0).then_inc(exp_done, CR_EXP)
            V.memset(mxp[:, 0, 0, 1:2], 0.0).then_inc(pv_done, CR_PV)
            V.memset(mxp[:, 0, 0, 2:3], 0.0).then_inc(sum_done, CR_SUM)
            V.memset(mxp[:, 0, 0, 3:4], 0.0).then_inc(mx_free, CR_MX)
            V.memset(mxp[:, 0, 1, 0:1], 0.0).then_inc(l_done, CR_L)
            V.memset(mxp[:, 0, 1, 1:2], 0.0).then_inc(o_free, CR_O)
            V.memset(mxp[:, 0, 1, 2:3], 0.0).then_inc(raw_lo, 2)
            for i, two_slots in enumerate((q_done, ql_done, exl_done, gu_ready, h_ready, ht_ready, hl_done, dn_done,
                                           yo_ready)):
                V.memset(mxp[:, 1, i // NC, i % NC:i % NC + 1], 0.0).then_inc(two_slots, CR)
            for r in range(XR):
                V.memset(mxp[:, 0, 2, r:r + 1], 0.0).then_inc(res_out[r], 16)
            link(V.memset(counts[:, 0, :], 0.0))
            V.memset(expert_i[:, 0:NT], NE)

            dve.wait_ge(small_hi, 1)
            V.scalar_tensor_tensor(out=wsml[:, :, :], in0=wsm[:, :, :], scalar=WS, in1=wsmh[:, :, :],
                                   op0=ALU.mult, op1=ALU.subtract).then_inc(small_lo, 1)

            roots = [0]

            def inv_std(n, eps, scale=1.0, src=None, first=0):
                src = mv[:, first:n, 1] if src is None else src
                V.tensor_scalar(var[:, first:n], src, scale, eps, ALU.mult, ALU.add).then_inc(var_ready, 1)
                roots[0] += 1
                dve.wait_ge(std_ready, roots[0])
                link(V.reciprocal(rstd[:, first:n], std[:, first:n]))

            def moments(src, n, first=0):
                for t in range(first, n):
                    ins = V.bn_stats(st6[:, t, :], src[:, t, :])
                link(ins)
                for t in range(first, n):
                    ins = V.bn_aggr(mv[:, t, :], st6[:, t, :])
                link(ins)

            for g in range(NC):
                dve.wait_ge(in_x[g], 16)
                moments(xs, (g + 1) * TC, first=g * TC)
            inv_std(NT, LN_EPS)

            def normalise(t):
                if t >= 2:
                    dve.wait_ge(xt_ready, t - 1)
                V.tensor_scalar(xn[:, t % 2, :], xs[:, t, :], mv[:, t, 0:1], rstd[:, t:t + 1],
                                ALU.subtract, ALU.mult).then_inc(xn_ready, 1)

            normalise(0)
            normalise(1)
            for t in range(NT):
                dve.wait_ge(xh_done, t + 1)
                V.tensor_tensor(xnTl[:, :, t * P:(t + 1) * P],
                                ps[:, t % 2, 0:E].rearrange("p (k c) -> p k c", k=KE),
                                xnTh[:, :, t * P:(t + 1) * P], ALU.subtract).then_inc(xl_done, 1)
                if t + 2 < NT:
                    normalise(t + 2)

            dve.wait_ge(kva_done, NT)
            dve.wait_ge(in_const, 32)
            lat, kpe = kv[:, :, 0:LORA], kv[:, :, LORA:DK]
            def latents(g):
                if g == 0:
                    link(V.tensor_tensor(kvtA, lat, lat, ALU.mult))
                    link(V.tensor_reduce(mv[:, :, 0], kvtA, AX.X, ALU.add))
                if g == 1:
                    inv_std(NT, RMS_EPS, 1.0 / LORA, mv[:, :, 0])
                if g == 2:
                    link(V.tensor_tensor(lat, lat, rstd[:, :].unsqueeze(2).broadcast_to([P, NT, LORA]), ALU.mult))
                if g == 3:
                    V.tensor_tensor(lat, lat, kvs[:, :].unsqueeze(1).broadcast_to([P, NT, LORA]), ALU.mult)
                    V.tensor_tensor(kvtA[:, :, 0:HR], kpe[:, :, 0:HR], cosT, ALU.mult)
                if g == 4:
                    V.tensor_tensor(kvtA[:, :, HR:], kpe[:, :, HR:], cosT, ALU.mult)
                    V.tensor_tensor(kvtB[:, :, 0:HR], kpe[:, :, HR:], sinT[:, :, 0:HR], ALU.mult)
                if g == 5:
                    link(V.tensor_tensor(kvtB[:, :, HR:], kpe[:, :, 0:HR], sinT[:, :, HR:], ALU.mult))
                    V.tensor_tensor(kpe, kvtA, kvtB, ALU.add).then_inc(kfin_ready, 1)

            for g in range(H):
                dve.wait_ge(wfh_done, g + 1)
                V.scalar_tensor_tensor(
                    out=WQl[:, :, g * DK:g * DK + LORA],
                    in0=ps[:, 6 + g % 2, 0:128].rearrange("p (k c) -> p k c", k=KE), scalar=WS,
                    in1=WQh[:, :, g * DK:g * DK + LORA],
                    op0=ALU.mult, op1=ALU.subtract).then_inc(wfl_done, 1)
                latents(g)
                if KT_AFTER < g <= KT_AFTER + NT // TC:
                    b = g - KT_AFTER - 1
                    dve.wait_ge(kh_done, b + 1)
                    V.tensor_tensor(KTl[:, b * CQ:(b + 1) * CQ], ps[:, b, :], KTh[:, b * CQ:(b + 1) * CQ],
                                    ALU.subtract).then_inc(kl_done, 1)
                if g == PE_AFTER:
                    dve.wait_ge(pe_hi, 1)
                    V.scalar_tensor_tensor(
                        out=WQl[:, :, :].rearrange("p k (h c) -> p (k h) c", c=DK)[:, :, LORA:],
                        in0=wq_raw.rearrange("p k h c -> p (k h) c")[:, :, NOPE:], scalar=WS,
                        in1=WQh[:, :, :].rearrange("p k (h c) -> p (k h) c", c=DK)[:, :, LORA:],
                        op0=ALU.mult, op1=ALU.subtract).then_inc(pe_lo, 1)
            dve.wait_ge(wf_ready, H)
            V.memset(D[:, 2048:3072], 0.0).then_inc(dm_zero, 1)
            dve.wait_ge(dm_zero, 1)

            def cosines(qc, tile, g):
                n = qc * QG + tile * HG + g
                dve.wait_ge(q_done, CR + n + 1)
                if not isinstance(n, int) or n >= 2:
                    dve.wait_ge(rope_done, n - 1)
                halves = [P, HG, 2, HR]
                V.tensor_tensor(ropA[:, g % 2].rearrange("p h (x c) -> p h x c", x=2),
                                pe_of(g).rearrange("p h (x c) -> p h x c", x=2),
                                cosT[:, qc * TC + tile, :].unsqueeze(1).unsqueeze(1).broadcast_to(halves),
                                ALU.mult).then_inc(cos_done, 1)

            def q_low(qc, tile, g):
                n = qc * QG + tile * HG + g
                dve.wait_ge(qh_done, n + 1)
                dst = [t.rearrange("p (h q) -> p h q", h=H)[:, 4 * g:4 * g + 4, bass.ds(tile * P, P)]
                       for t in (QTh, QTl)]
                V.tensor_tensor(dst[1], ps[:, 2 + g % 2, :].rearrange("p (h q) -> p h q", h=HG), dst[0],
                                ALU.subtract).then_inc(ql_done, 1)

            def subtrahend(qc, p, s):
                k = (qc * NP + p) * 2 + s
                dve.wait_ge(mt_ready, k + 1)
                rows = ps[0:TC, BK_M, s * P:(s + 1) * P].unsqueeze(1).broadcast_to([TC, TC, P])
                V.tensor_tensor(Dm[0:TC, p % 2, s, :].rearrange("p (j q) -> p j q", j=TC), rows, negblk,
                                ALU.mult).then_inc(d_ready, 1)

            def maxima(qc, p, j):
                U = units(qc)
                n0 = first_unit(qc) + p * U
                s, i4, kc = j // (U // 2), j % (U // 2) // (qc + 1), j % (qc + 1)
                w = CQ if kc < qc else P * (i4 + 1)
                dve.wait_ge(mx_ready, n0 + j + 1)
                V.tensor_reduce(mxp[:, s, i4, kc:kc + 1], ps[:, 4 + j % MX_RING, 0:w], AX.X,
                                ALU.max).then_inc(mx_free, 1)
                if j % (U // 2) == U // 2 - 1:
                    dve.wait_ge(mx_free, CR_MX + n0 + (s + 1) * U // 2)
                    V.tensor_reduce(mrow[:, s, :], mxp[:, s, :, 0:qc + 1], AX.X, ALU.max).then_inc(m_ready, 1)

            def widen(qc, p, h):
                dve.wait_ge(wide_ready, spreads(qc, p) + h + 1)
                V.tensor_copy(minus_m[:, p % 2, h * CQ // 2:(h + 1) * CQ // 2],
                              ps[:, BK_M, CQ // 2:]).then_inc(wide_done, 1)

            def shift(qc, p, kt):
                c0 = max(kt - TC * qc, 0) * P
                i = 2 * kt + 1
                if kt == 0:
                    dve.wait_ge(wide_done, spreads(qc, p + 1))
                dve.wait_ge(st_ready, first_unit(qc) + p * units(qc) + i + 1)
                V.tensor_tensor(ps[:, i % ST_RING, c0:], ps[:, i % ST_RING, c0:], minus_m[:, p % 2, c0:],
                                ALU.add).then_inc(shifted, 1)

            def pair(qc, p, ahead=True, sums=None):
                KT, U = TC * (qc + 1), units(qc)
                slot = 0

                def between():
                    nonlocal slot
                    if ahead:
                        if slot < U:
                            maxima(qc, p + 1, slot)
                        if slot == U // 2 + 2:
                            subtrahend(qc, p + 1, 0)
                        if slot == U + 1:
                            subtrahend(qc, p + 1, 1)
                        if slot in spread_slots(qc):
                            widen(qc, p + 1, spread_slots(qc).index(slot))
                    if slot == U // 4 + 1 and sums is not None:
                        part_sums(qc, sums)
                    slot += 1

                for kt in range(KT):
                    between()
                    if qc >= SHIFT_FROM:
                        shift(qc, p, kt)
                    between()
                    between()
                    if qc == NC - 1 and kt in (KT - 6, KT - 3):
                        cut_expert(p, int(kt == KT - 3))

            def part_sums(qc, p):
                dve.wait_ge(sum_done, CR_SUM + first_unit(qc) + (p + 1) * units(qc))
                V.tensor_reduce(Lp[:, bass.ds(2 * p, 2), :],
                                Pacc[:, p % 2].rearrange("p s (b c) -> p s b c", c=32),
                                AX.X, ALU.add, apply_transpose=True).then_inc(l_done, 1)

            def cut_expert(p, r):
                e = 2 * p + r
                dve.wait_ge(raw_hi, e + 2)
                V.scalar_tensor_tensor(out=WEl[:, e, :], in0=stage[:, 1 - r, :], scalar=WS, in1=WEh[:, e, :],
                                       op0=ALU.mult, op1=ALU.subtract).then_inc(raw_lo, 1)

            def layer_norm(src, dst, done=None, first=0, n=TC):
                moments(src, n, first)
                inv_std(n, LN_EPS, first=first)
                for j in range(first, n):
                    ins = V.tensor_scalar(dst[:, j, :], src[:, j, :], mv[:, j, 0:1], rstd[:, j:j + 1],
                                          ALU.subtract, ALU.mult)
                if done is None:
                    link(ins)
                else:
                    ins.then_inc(done, 1)

            scr_p = C[:, 3584:3712].rearrange("p (k t e) -> p k t e", k=TOPK, t=TC)
            scr_c = C[:, 3712:3776].rearrange("p (t e) -> p t e", t=TC)
            scr_s = C[:, 3776:3792]

            def normalised(qc, j):
                for b in range(2):
                    dve.wait_ge(t1_ready, (qc * TC + j) * 2 + b + 1)
                    if j >= 2:
                        dve.wait_ge(t2_ready, (qc * TC + j - 1) * 2)
                    V.tensor_tensor(On[:, j % 2, 512 * b:512 * b + 512].rearrange("p (h c) -> p h c", c=LORA),
                                    ps[:, b, :].rearrange("p (h c) -> p h c", c=LORA),
                                    rL[:, 8 * b:8 * b + 8, j:j + 1].broadcast_to([P, 8, LORA]),
                                    ALU.mult).then_inc(on_ready, 1)

            def first_norm(qc, j):
                dve.wait_ge(ysb_ready, qc * TC + j + 1)
                layer_norm(ysb, lnt, first=j, n=j + 1)
                dve.wait_ge(xr_in, 16 * (qc + 1))
                link(V.tensor_tensor(x1[:, j, :], xr[:, j, :], lnt[:, j, :], ALU.add))

            def second_norm(qc, j):
                layer_norm(x1, lnt, xn2_ready, first=j, n=j + 1)

            def xn2_low(qc):
                for k in range(KE):
                    dve.wait_ge(x2h_done, qc * KE + k + 1)
                    V.tensor_tensor(xn2l[:, k, :], ps[:, 4 + k, :], xn2h[:, k, :], ALU.subtract).then_inc(x2l_done, 1)

            def choose(qc):
                tiles = slice(qc * TC, (qc + 1) * TC)
                dve.wait_ge(sig_ready, qc + 1)
                link(V.tensor_tensor(sgb[:, :, :], sig[:, :, :],
                                     biasb[:, :].unsqueeze(1).broadcast_to([P, TC, NE]), ALU.add))
                for j in range(TC):
                    ins = V.max(top8[:, j, :], sgb[:, j, :])
                link(ins)
                for j in range(TC):
                    ins = V.max_index(idx8[:, j, :], top8[:, j, :], sgb[:, j, :])
                link(ins)
                link(V.tensor_copy(idxf[:, :, :], idx8[:, :, :]))
                iota4 = iota.unsqueeze(1).broadcast_to([P, TC, NE])
                for k in range(TOPK):
                    ins = V.tensor_tensor(pick[:, k, tiles, :], iota4,
                                          idxf[:, :, k:k + 1].broadcast_to([P, TC, NE]), ALU.is_equal)
                link(ins)
                V.tensor_tensor(pickb[:, :, :], pick[:, 0, tiles, :], pick[:, 1, tiles, :], ALU.add).then_inc(pickb_ready, 1)

            def shares(qc):
                tiles = slice(qc * TC, (qc + 1) * TC)
                for k in range(TOPK):
                    ins = V.tensor_tensor(scr_p[:, k], pick[:, k, tiles, :], sig[:, :, :], ALU.mult)
                link(ins)
                for k in range(TOPK):
                    ins = V.tensor_reduce(share[:, tiles, k], scr_p[:, k], AX.X, ALU.add)
                link(ins)
                link(V.tensor_tensor(rsum[:, 0, :], share[:, tiles, 0], share[:, tiles, 1], ALU.add))
                link(V.tensor_scalar(rsum[:, 0, :], rsum[:, 0, :], 1e-20, None, ALU.add))
                link(V.reciprocal(rsum[:, 1, :], rsum[:, 0, :]))
                link(V.tensor_tensor(share[:, tiles, :], share[:, tiles, :],
                                     rsum[:, 1, :].unsqueeze(2).broadcast_to([P, TC, TOPK]), ALU.mult))

            def places(qc):
                tiles = slice(qc * TC, (qc + 1) * TC)
                dve.wait_ge(rank_ready, qc + 1)
                rank = ps[:, 6, 64:64 + 2 * TC * NE].rearrange("p (w t e) -> p w t e", w=2, t=TC)
                for j in range(TC):
                    V.tensor_tensor(place[:, j, :], rank[:, 0, j, :], counts[:, j % 2, :], ALU.add)
                    link(V.tensor_tensor(counts[:, (j + 1) % 2, :], rank[:, 1, j, :], counts[:, j % 2, :], ALU.add))
                V.tensor_scalar(scr_s[:, :], iota, float(S), None, ALU.mult)
                link(V.tensor_copy(scr_c[:, :], place[:, :, :]))
                link(V.tensor_tensor(place[:, :, :], scr_c[:, :], scr_s[:, :].unsqueeze(1).broadcast_to([P, TC, NE]),
                                     ALU.add))
                for k in range(TOPK):
                    ins = V.tensor_tensor(scr_p[:, k], pick[:, k, tiles, :], place[:, :, :], ALU.mult)
                link(ins)
                for k in range(TOPK):
                    ins = V.tensor_reduce(where[:, tiles, k], scr_p[:, k], AX.X, ALU.add)
                link(ins)
                V.tensor_copy(where_i[:, tiles, :], where[:, tiles, :]).then_inc(where_ready, 1)

            for qc in range(NC):
                for k in range(QG + 2):
                    if k < QG:
                        cosines(qc, k // HG, k % HG)
                    if k >= 2:
                        q_low(qc, (k - 2) // HG, (k - 2) % HG)
                    if qc and k == 0:
                        second_norm(qc - 1, TC - 1)
                    if qc and k == 3:
                        xn2_low(qc - 1)
                    if qc and k == 6:
                        choose(qc - 1)
                    if qc and k == 9:
                        places(qc - 1)
                    if qc and k == 12:
                        shares(qc - 1)

                for j in range(units(qc)):
                    maxima(qc, 0, j)
                    if j == units(qc) // 2 + 2:
                        subtrahend(qc, 0, 0)
                subtrahend(qc, 0, 1)
                if qc >= SHIFT_FROM:
                    for h in range(2):
                        widen(qc, 0, h)
                if qc == NC - 1:
                    dve.wait_ge(raw_hi, 1)
                    V.scalar_tensor_tensor(out=WEl[:, NE, :], in0=stage[:, 0, :], scalar=WS, in1=WEh[:, NE, :],
                                           op0=ALU.mult, op1=ALU.subtract).then_inc(raw_lo, 1)
                pair(qc, 0)
                with dve.Fori(1, NP - 1) as p:
                    pair(qc, p, sums=p - 1)
                pair(qc, NP - 1, ahead=False, sums=NP - 2)
                part_sums(qc, NP - 1)
                dve.wait_ge(den_ready, qc + 1)
                link(V.reciprocal(rL[:, :, :].rearrange("p h j -> p (h j)"), ps[:, BK_M, 0:H * TC]))
                normalised(qc, 0)
                normalised(qc, 1)
                for j in range(TC):
                    if j + 2 < TC:
                        normalised(qc, j + 2)
                    first_norm(qc, j)
                    if j + 1 < TC:
                        second_norm(qc, j)
            second_norm(NC - 1, TC - 1)
            xn2_low(NC - 1)
            choose(NC - 1)
            places(NC - 1)

            n_tiles, ends = scr[:, 256:256 + NE], [scr[:, 288 + 16 * i:304 + 16 * i] for i in range(2)]
            end = ends[(NE.bit_length() - 1) % 2]
            which, col = scr[:, 1536:1536 + MT], scr[:, 1600:1600 + MT]

            def list_ends():
                link(V.tensor_scalar(scr_s[:, :], iota, float(P), None, ALU.mult))
                more = scr[:, 0:NE * NT].rearrange("p (e j) -> p e j", e=NE)
                link(V.tensor_tensor(more, counts[:, 0, :].unsqueeze(2).broadcast_to([P, NE, NT]),
                                     scr_s[:, :].unsqueeze(1).broadcast_to([P, NE, NT]), ALU.is_gt))
                link(V.tensor_reduce(n_tiles, more, AX.X, ALU.add))
                link(V.tensor_copy(ends[0], n_tiles))
                a, d = 0, 1
                while d < NE:
                    V.tensor_copy(ends[1 - a][:, 0:d], ends[a][:, 0:d])
                    link(V.tensor_tensor(ends[1 - a][:, d:], ends[a][:, d:], ends[a][:, 0:NE - d], ALU.add))
                    a, d = 1 - a, 2 * d

            def list_of_tile():
                done = scr[:, 512:512 + MT * NE].rearrange("p (m e) -> p m e", e=NE)
                link(V.tensor_tensor(done, end.unsqueeze(1).broadcast_to([P, MT, NE]),
                                     tile_id.unsqueeze(2).broadcast_to([P, MT, NE]), ALU.is_le))
                link(V.tensor_reduce(which, done, AX.X, ALU.add))
                link(V.tensor_tensor(done, done, n_tiles.unsqueeze(1).broadcast_to([P, MT, NE]), ALU.mult))
                link(V.tensor_reduce(col, done, AX.X, ALU.add))

            def list_columns():
                link(V.tensor_tensor(col, tile_id, col, ALU.subtract))
                link(V.scalar_tensor_tensor(out=col, in0=which, scalar=float(NT), in1=col, op0=ALU.mult, op1=ALU.add))
                link(V.tensor_scalar(col, col, float(NE * NT - 1), None, ALU.min))
                V.tensor_scalar(expert_i[:, NT:], which, float(NE - 1), None, ALU.min)
                for k in range(2):
                    ins = V.tensor_scalar(sel_t[:, k, :], col, row_id[:, k:k + 1], None, ALU.is_equal)
                ins.then_inc(sel_ready, 1)

            def result_rows():
                V.tensor_tensor(scr[:, 320:336], end, n_tiles, ALU.subtract)
                link(V.tensor_scalar(scr[:, 336:352], iota, -float(S), float(NT * P), ALU.mult, ALU.add))
                link(V.scalar_tensor_tensor(out=scr[:, 352:368], in0=scr[:, 320:336], scalar=float(P),
                                            in1=scr[:, 336:352], op0=ALU.mult, op1=ALU.add))
                shift = scr[:, 1792:1792 + TOPK * NT * NE].rearrange("p (k t e) -> p k t e", k=TOPK, t=NT)
                for k in range(TOPK):
                    ins = V.tensor_tensor(shift[:, k], pick[:, k], scr[:, 352:368].unsqueeze(1).broadcast_to([P, NT, NE]),
                                          ALU.mult)
                link(ins)
                moved = scr[:, 1700:1700 + NT * TOPK].rearrange("p (t k) -> p t k", k=TOPK)
                for k in range(TOPK):
                    ins = V.tensor_reduce(moved[:, :, k], shift[:, k], AX.X, ALU.add)
                link(ins)
                V.tensor_tensor(res_i[:, :, :], moved, where[:, :, :], ALU.add).then_inc(res_ready, 1)

            def x_low(n, r):
                dve.wait_ge(exh_done, n + 1)
                V.tensor_tensor(xgl[:, r], ps[:, r, 0:E].rearrange("p (k c) -> p k c", k=KE), xgh[:, r],
                                ALU.subtract).then_inc(exl_done, 1)

            def product(n, r):
                dve.wait_ge(silu_done, n + 1)
                dve.wait_ge(ht_ready, n + 1)
                V.scalar_tensor_tensor(out=hx[:, r], in0=ps[:, 2 + r, F:2 * F], scalar=1 / WS, in1=sg[:, r],
                                       op0=ALU.mult, op1=ALU.mult).then_inc(h_ready, 1)

            def h_low(n, r):
                dve.wait_ge(hh_done, n + 1)
                V.tensor_tensor(hl[:, r], ps[:, 4 + r, 0:P], hh[:, r], ALU.subtract).then_inc(hl_done, 1)

            def step(n, r, k=None):
                if k is None or k < GT:
                    x_low(n, r % 2)
                if k is None or 0 <= k - 1 < GT:
                    product(n - 1, (r - 1) % 2)
                if k is None or 0 <= k - 2 < GT:
                    h_low(n - 2, r % 2)

            for k in range(XR):
                step(k, k, k)
                if k > 0:
                    (list_ends, list_of_tile, list_columns)[k - 1]()
            with dve.Fori(1, NT // XR - 1) as a:
                for r in range(XR):
                    step(XR * a + r, r)
            dve.wait_ge(tok_done, 1)
            V.tensor_copy(tok_i[:, :], ps[:, 0, E:E + MT]).then_inc(tok_ready, 1)
            with dve.Fori(NT // XR - 1, NT // XR + 3) as a:
                for r in range(XR):
                    step(XR * a + r, r)
            shares(NC - 1)
            with dve.Fori(NT // XR + 3, NT // XR + 7) as a:
                for r in range(XR):
                    step(XR * a + r, r)
            result_rows()
            with dve.Fori(NT // XR + 7, GT // XR) as a:
                for r in range(XR):
                    step(XR * a + r, r)
            for k in range(GT, GT + 2):
                step(k, k % XR, k)

            def weighted(g, first, n):
                acc = parts_of(g, 0)
                for k in range(TOPK):
                    for j in range(first, n):
                        ins = V.scalar_tensor_tensor(out=acc[:, j], in0=parts_of(g, 2 + k)[:, j],
                                                     scalar=share[:, g * TC + j, k:k + 1], in1=acc[:, j],
                                                     op0=ALU.mult, op1=ALU.add)
                    link(ins)
                t0, t1 = g * TC + first, g * TC + n
                for t in range(t0, t1):
                    ins = V.bn_stats(st6[:, t, :], acc[:, t - g * TC])
                link(ins)
                for t in range(t0, t1):
                    ins = V.bn_aggr(mv[:, t, :], st6[:, t, :])
                link(ins)
                inv_std(t1, LN_EPS, src=mv[:, t0:t1, 1], first=t0)
                V.scalar_tensor_tensor(out=shiftb[:, t0:t1], in0=mv[:, t0:t1, 0], scalar=-1.0, in1=rstd[:, t0:t1],
                                       op0=ALU.mult, op1=ALU.mult).then_inc(shift_ready, 1)

            def residual(k, g, first, n):
                dve.wait_ge(normed, k + 1)
                acc = parts_of(g, 0)
                V.tensor_tensor(acc[:, first:n], acc[:, first:n], parts_of(g, 1)[:, first:n],
                                ALU.add).then_inc(out_ready, 1)

            for k, (g, first, n) in enumerate(OUT_PARTS):
                if first == 0:
                    dve.wait_ge(own_in[g], 32)
                dve.wait_ge(got_in[k], 16 * (n - first) * TOPK)
                weighted(g, first, n)
                if k:
                    residual(k - 1, *OUT_PARTS[k - 1])
            residual(len(OUT_PARTS) - 1, *OUT_PARTS[-1])

        @block.tensor
        def _(pe):
            T = nc.tensor

            def three(dst, ah, al, bh, bl, first=True, last=True):
                T.matmul(dst, ah, bh, start=first, stop=False)
                T.matmul(dst, ah, bl, start=False, stop=False)
                return T.matmul(dst, al, bh, start=False, stop=last)

            pe.wait_ge(in_const, 32)
            pe.wait_ge(small_lo, 1)
            for t in range(NT + 1):
                if t < NT:
                    pe.wait_ge(xn_ready, t + 1)
                    if t >= 2:
                        pe.wait_ge(xl_done, t - 1)
                    for k in range(KE):
                        ins = T.transpose(ps[:, t % 2, k * P:(k + 1) * P], xn[:, t % 2, k * P:(k + 1) * P], ident)
                    ins.then_inc(xt_ready, 1)
                if t > 0:
                    u = t - 1
                    pe.wait_ge(xl_done, u + 1)
                    if u >= 2:
                        pe.wait_ge(kva_done, u - 1)
                    for k in range(KE):
                        tok = slice(u * P, (u + 1) * P)
                        ins = three(ps[:, 2 + u % 2, 0:DK], xnTh[:, k, tok], xnTl[:, k, tok],
                                    wsmh[:, k, 0:DK], wsml[:, k, 0:DK], k == 0, k == KE - 1)
                    ins.then_inc(kva_ready, 1)
            pe.wait_ge(in_wq, 16)
            pe.wait_ge(in_wkvb, 16)
            pe.wait_ge(in_wo, 16)
            for h in range(H + 1):
                if h < H:
                    if h >= 2:
                        pe.wait_ge(wt_done, h - 1)
                    b = 4 + h % 2
                    for k in range(KE):
                        T.transpose(ps[:, b, k * P:(k + 1) * P], wq_raw[:, k, h, 0:NOPE], ident)
                    for v in range(2):
                        ins = T.transpose(ps[:, b, 256 + v * LORA:256 + (v + 1) * LORA],
                                          wkvb_raw[0:LORA, h, v * NOPE:(v + 1) * NOPE], ident[0:LORA, 0:LORA])
                    ins.then_inc(wt_ready, 1)
                if h > 0:
                    g = h - 1
                    pe.wait_ge(wt_done, g + 1)
                    if g >= 2:
                        pe.wait_ge(wfl_done, g - 1)
                    b, w, o = 6 + g % 2, wT[:, g % 2, :], LORA * (g % 2)
                    for k in range(KE):
                        T.matmul(ps[:, b, k * LORA:(k + 1) * LORA], w[:, k * P:(k + 1) * P],
                                 w[:, 256:256 + LORA], start=True, stop=True)
                    T.matmul(ps[o:o + LORA, b, 128:384], w[:, 256 + LORA:384], wo_raw[:, g, :],
                             start=True, stop=True).then_inc(wf_ready, 1)
                    if g == KT_AFTER:
                        pe.wait_ge(kfin_ready, 1)
                        for t in range(NT):
                            ins = T.transpose(ps[:, t // TC, t % TC * P:(t % TC + 1) * P], kv[:, t, :], ident)
                            if t % TC == TC - 1:
                                ins.then_inc(kt_ready, 1)

            def turn_xn2(qc):
                pe.wait_ge(xn2_ready, (qc + 1) * TC)
                for k in range(KE):
                    for j in range(TC):
                        ins = T.transpose(ps[:, 4 + k, j * P:(j + 1) * P], lnt[:, j, k * P:(k + 1) * P], ident)
                    ins.then_inc(xt2_ready, 1)

            def logits(qc):
                pe.wait_ge(x2l_done, (qc + 1) * KE)
                for j in range(TC):
                    for k in range(KE):
                        tok = slice(j * P, (j + 1) * P)
                        ins = three(ps[:, 6, j * NE:(j + 1) * NE], xn2h[:, k, tok], xn2l[:, k, tok],
                                    wsmh[:, k, DK:], wsml[:, k, DK:], k == 0, k == KE - 1)
                ins.then_inc(log_ready, 1)

            def ranks(qc):
                pe.wait_ge(pickb_ready, qc + 1)
                pk = pickb[:, :, :].rearrange("p t e -> p (t e)")
                T.matmul(ps[:, 6, 64:64 + TC * NE], before, pk, start=True, stop=True)
                T.matmul(ps[:, 6, 64 + TC * NE:64 + 2 * TC * NE], onesb, pk, start=True, stop=True).then_inc(rank_ready, 1)

            for qc in range(NC):
                def project(tile, g):
                    n = qc * QG + tile * HG + g
                    pe.wait_ge(q_done, n + 1)
                    tok = bass.ds((qc * TC + tile) * P, P)
                    for k in range(KE):
                        cols = slice(g * 512, (g + 1) * 512)
                        ins = three(ps[:, g % 2, :], xnTh[:, k, tok], xnTl[:, k, tok],
                                    WQh[:, k, cols], WQl[:, k, cols], k == 0, k == KE - 1)
                    ins.then_inc(q_ready, 1)

                def turn(tile, g):
                    n = qc * QG + tile * HG + g
                    pe.wait_ge(rope_done, n + 1)
                    pe.wait_ge(ql_done, n + 1)
                    for h in range(4):
                        ins = T.transpose(ps[:, 2 + g % 2, h * P:(h + 1) * P], qs[:, g, h * P:(h + 1) * P], ident)
                    ins.then_inc(qt_ready, 1)

                if qc == 0:
                    pe.wait_ge(kl_done, NT // TC)
                    pe.wait_ge(pe_lo, 1)
                    pe.wait_ge(wfl_done, H)
                for k in range(QG + 2):
                    if k < QG:
                        project(k // HG, k % HG)
                    if k >= 2:
                        turn((k - 2) // HG, (k - 2) % HG)
                    if qc and k == 2:
                        turn_xn2(qc - 1)
                    if qc and k == 4:
                        logits(qc - 1)
                    if qc and k == 8:
                        ranks(qc - 1)

                KT, U = TC * (qc + 1), units(qc)

                def max_unit(p, j):
                    s, i4, kc = j // (U // 2), j % (U // 2) // (qc + 1), j % (qc + 1)
                    w = CQ if kc < qc else P * (i4 + 1)
                    b = 4 + j % MX_RING
                    pe.wait_ge(mx_free, first_unit(qc) + p * U + j + 1)
                    ins = T.matmul(ps[:, b, 0:w], QTh[:, bass.ds((2 * p + s) * CQ + i4 * P, P)],
                                   KTh[:, kc * CQ:kc * CQ + w], start=True, stop=(kc < qc))
                    if kc == qc:
                        ins = T.matmul(ps[:, b, w - P:w], identb, mask_qk, start=False, stop=True)
                    ins.then_inc(mx_ready, 1)

                def turn_max(p, s):
                    k = (qc * NP + p) * 2 + s
                    pe.wait_ge(m_ready, k + 1)
                    if qc or s or not isinstance(p, int) or p:
                        pe.wait_ge(d_ready, k)
                    T.transpose(ps[0:TC, BK_M, s * P:(s + 1) * P], mrow[:, s, :], ident).then_inc(mt_ready, 1)

                def score_unit(p, i):
                    kt, s = i // 2, i % 2
                    j = kt - TC * qc
                    c0 = max(j, 0) * P
                    dst = ps[:, i % ST_RING, c0:]
                    q = bass.ds((2 * p + s) * CQ + c0, CQ - c0)
                    keys = slice(kt * P, (kt + 1) * P)
                    row = s == 0 or qc < SHIFT_FROM
                    if i < 2 and row:
                        pe.wait_ge(d_ready, (qc * NP + p) * 2 + s + 1)
                    pe.wait_ge(exp_done, first_unit(qc) + p * U + i + 1)
                    ins = three(dst, KTh[:, keys], KTl[:, keys], QTh[:, q], QTl[:, q], True, not row and j < 0)
                    if row:
                        ins = T.matmul(dst, ones4, Dm[:, p % 2, s, c0:], start=False, stop=(j < 0))
                    if j >= 0:
                        ins = T.matmul(ps[:, i % ST_RING, c0:c0 + P], identb, mask_kq, start=False, stop=True)
                    ins.then_inc(st_ready, 1)

                def spread(p, h):
                    pe.wait_ge(d_ready, (qc * NP + p) * 2 + 2)
                    k = spreads(qc, p) + h
                    if not isinstance(k, int) or k:
                        pe.wait_ge(wide_done, k)
                    T.matmul(ps[:, BK_M, CQ // 2:], ones4, Dm[:, p % 2, 1, h * CQ // 2:(h + 1) * CQ // 2],
                             start=True, stop=True).then_inc(wide_ready, 1)

                def values(p, kt):
                    c0 = max(kt - TC * qc, 0) * P
                    if kt == 0:
                        pe.wait_ge(o_free, qc * NP + p + 1)
                    for s in range(2):
                        i = 2 * kt + s
                        pe.wait_ge(exp_done, CR_EXP + first_unit(qc) + p * U + i + 1)
                        T.matmul(ps[LORA * s:LORA * (s + 1), BK_O, c0:], kv[:, kt, 0:LORA],
                                 Pr[:, i % P_RING, c0:], start=(kt == 0), stop=(kt == KT - 1)).then_inc(pv_done, 1)

                def pair(p, ahead):
                    slot = 0

                    def between():
                        nonlocal slot
                        if ahead:
                            if slot < U:
                                max_unit(p + 1, slot)
                            if slot == U // 2 + 2:
                                turn_max(p + 1, 0)
                            if slot == U + 1:
                                turn_max(p + 1, 1)
                            if slot in spread_slots(qc):
                                spread(p + 1, spread_slots(qc).index(slot))
                            slot += 1

                    for kt in range(KT):
                        score_unit(p, 2 * kt)
                        between()
                        score_unit(p, 2 * kt + 1)
                        between()
                        if kt >= LAG:
                            values(p, kt - LAG)
                        between()
                    for kt in range(KT - LAG, KT):
                        values(p, kt)

                pe.wait_ge(ql_done, CR + (qc + 1) * QG)
                if qc:
                    pe.wait_ge(where_ready, qc)
                for j in range(U):
                    max_unit(0, j)
                    if j == U // 2 + 2:
                        turn_max(0, 0)
                turn_max(0, 1)
                if qc >= SHIFT_FROM:
                    for h in range(2):
                        spread(0, h)
                with pe.Fori(0, NP - 1) as p:
                    pair(p, True)
                pair(NP - 1, False)

                pe.wait_ge(l_done, CR_L + (qc + 1) * NP)
                parts = Lp[:, :, :].rearrange("p h (j b) -> p h j b", b=4)
                for b in range(4):
                    ins = T.matmul(ps[:, BK_M, 0:H * TC], selL[:, b, :], parts[:, :, :, b],
                                   start=(b == 0), stop=(b == 3))
                ins.then_inc(den_ready, 1)
                pe.wait_ge(o_free, CR_O + (qc + 1) * NP)

                def turn_out(j):
                    for b in range(2):
                        if j:
                            pe.wait_ge(on_ready, (qc * TC + j - 1) * 2 + b + 1)
                        for n in range(4):
                            o = (4 * b + n) * CQ + j * P
                            ins = T.transpose(ps[:, b, n * P:(n + 1) * P], OT[:, o:o + P], ident)
                        ins.then_inc(t1_ready, 1)

                def turn_on(j):
                    for b in range(2):
                        pe.wait_ge(on_ready, (qc * TC + j) * 2 + b + 1)
                        if qc or j:
                            pe.wait_ge(ont_ready, (qc * TC + j - 1) * 2 + b + 1)
                        for n in range(4):
                            ins = T.transpose(ps[:, 2 + b, n * P:(n + 1) * P],
                                              On[:, j % 2, (4 * b + n) * P:(4 * b + n + 1) * P], ident)
                        ins.then_inc(t2_ready, 1)

                turn_out(0)
                turn_on(0)
                turn_out(1)
                for j in range(TC):
                    if j + 1 < TC:
                        turn_on(j + 1)
                    if j + 2 < TC:
                        turn_out(j + 2)
                    pe.wait_ge(ont_ready, (qc * TC + j + 1) * 2)
                    if j >= 2:
                        pe.wait_ge(ysb_ready, qc * TC + j - 1)
                    for n in range(NP):
                        ins = T.matmul(ps[:, 4 + j % 2, 0:E], OnT[:, j % 2, n, :], WO[:, n, :],
                                       start=(n == 0), stop=(n == NP - 1))
                    ins.then_inc(mo_ready, 1)

            turn_xn2(NC - 1)
            logits(NC - 1)
            ranks(NC - 1)

            def turn_x(n, r, a, gathered):
                if gathered:
                    pe.wait_ge(xg_in[r], 16 * (a + 1 - NT // XR))
                else:
                    pe.wait_ge(row_in[r], 16 * (a + 1))
                pe.wait_ge(exl_done, n + 1)
                for k in range(KE):
                    ins = T.transpose(ps[:, r % 2, k * P:(k + 1) * P], xg[:, r, k * P:(k + 1) * P], ident)
                ins.then_inc(ex_ready, 1)

            def experts_of(a, tiles):
                return nc.values_load_multi_w_load_instructions(
                    expert_i[0:1, bass.ds((a - 1) * XR, tiles)], engines=[mybir.EngineType.PE],
                    min_val=0, max_val=NE,
                    skip_runtime_bounds_check_because="they are made as the least of a count and NE - 1")[1]

            def gate_up(n, r, e):
                pe.wait_ge(exl_done, CR + n + 1)
                pe.wait_ge(h_ready, n + 1)
                for k in range(KE):
                    w = slice(k * 2 * F, (k + 1) * 2 * F)
                    ins = three(ps[:, 2 + r, 0:2 * F], xgh[:, r, k], xgl[:, r, k], WEh[:, e, w], WEl[:, e, w],
                                k == 0, k == KE - 1)
                ins.then_inc(gu_ready, 1)

            def turn_h(n, r):
                pe.wait_ge(h_ready, CR + n + 1)
                pe.wait_ge(hl_done, n + 1)
                T.transpose(ps[:, 4 + r, 0:P], hx[:, r], ident).then_inc(ht_ready, 1)

            def down(n, r, e):
                pe.wait_ge(hl_done, CR + n + 1)
                pe.wait_ge(yo_ready, n + 1)
                w = slice(KE * 2 * F, KE * 2 * F + E)
                three(ps[:, 6 + r, 0:E], hh[:, r], hl[:, r], WEh[:, e, w], WEl[:, e, w]).then_inc(dn_done, 1)

            def step(n, r, a, experts, k=None, gathered=False):
                if k is None or k < GT:
                    turn_x(n, r, a, gathered)
                if k is None or 0 <= k - 1 < GT:
                    gate_up(n - 1, (r - 1) % 2, experts[XR + r - 1])
                if k is None or 0 <= k - 2 < GT:
                    turn_h(n - 2, r % 2)
                if k is None or 0 <= k - 3 < GT:
                    down(n - 3, (r - 3) % 2, experts[XR + r - 3])

            pe.wait_ge(raw_lo, 2 + NX)
            pe.wait_ge(where_ready, NC)
            shared = [NE] * 2 * XR
            for k in range(XR):
                step(k, k, 0, shared, k)
            with pe.Fori(1, NT // XR - 1) as a:
                for r in range(XR):
                    step(XR * a + r, r, a, shared)
            pe.wait_ge(sel_ready, 1)
            pe.wait_ge(exl_done, NT - XR + 1)
            pe.wait_ge(map_back, 16)
            for k in range(2):
                ins = T.matmul(ps[:, 0, E:E + MT], mapf[:, k, :], sel_t[:, k, :], start=(k == 0), stop=(k == 1))
            ins.then_inc(tok_done, 1)
            pe.wait_ge(tok_ready, 1)
            for r in range(XR):
                step(NT - XR + r, r, NT // XR - 1, shared)
            with pe.Fori(NT // (2 * XR), GT // (2 * XR)) as b:
                experts = experts_of(2 * b, 3 * XR)
                for h in range(2):
                    for r in range(XR):
                        step(XR * (2 * b + h) + r, r, 2 * b + h, experts[XR * h:], gathered=True)
            experts = experts_of(GT // XR, XR)
            for k in range(GT, GT + 3):
                step(k, k % XR, GT // XR, experts, k)


def constants():
    import numpy as np

    c = np.zeros((P, C_END), np.float32)
    c[:, C_ID:C_ID + P] = np.eye(P)
    pos = np.arange(S, dtype=np.float32)
    inv = np.float32(1.0) / np.float32(10000.0) ** (np.arange(0, ROPE, 2, dtype=np.float32) / np.float32(ROPE))
    ang = pos[:, None] * inv.astype(np.float32)
    cos, sin = np.cos(ang).astype(np.float32), np.sin(ang).astype(np.float32)
    c[:, C_COS:C_SIN] = cos.reshape(NT, P, ROPE // 2).transpose(1, 0, 2).reshape(P, -1)
    c[:, C_SIN:C_SEL] = np.concatenate([-sin, sin], 1).reshape(NT, P, ROPE).transpose(1, 0, 2).reshape(P, -1)
    sel = np.zeros((P, TC, P), np.float32)
    for b in range(TC):
        for a in range(4):
            sel[32 * a + np.arange(32), b, 32 * b + np.arange(32)] = 1
    c[:, C_SEL:C_BLK] = sel.reshape(P, -1)
    blk = np.zeros((P, TC, P), np.float32)
    for j in range(TC):
        blk[j, j] = -1
    c[:, C_IOTA:C_TOK] = np.arange(NE)
    c[:, C_TOK:C_ROW] = np.arange(P)[:, None] + P * np.arange(NT)
    c[:, C_ROW:C_TILE] = np.arange(P)[:, None] + P * np.arange(2)
    c[:, C_TILE:C_END] = np.arange(MT)
    row, col = np.arange(P)[:, None], np.arange(P)[None]
    ones4 = np.broadcast_to(row < TC, (P, P))
    b16 = np.concatenate([row == col, (col > row) * NEG, (col < row) * NEG, ones4, np.zeros((P, P)), row < col,
                          np.ones((P, P)), blk.reshape(P, -1)], 1)
    return c, (b16.astype(np.float32).view(np.uint32) >> 16).astype(np.uint16)


_INS = ['L0_attn_x', 'L0_attn_wq', 'L0_attn_wkv_a', 'L0_attn_wkv_b', 'L0_attn_wo', 'L0_attn_kv_norm_scale',
        'L0_ffn_gate_w', 'L0_ffn_expert_bias', 'L0_ffn_shared_gate_w', 'L0_ffn_shared_up_w',
        'L0_ffn_shared_down_w', 'L0_ffn_experts_gate_up', 'L0_ffn_experts_down']


def kernel(**inputs):
    import numpy as _np
    import concourse.bacc as _bacc
    from concourse import mybir as _mybir
    from concourse.bass_utils import run_bass_kernel_spmd as _run

    nc = _bacc.Bacc("TRN2", target_bir_lowering=False, num_devices=1)
    arrays, args = {}, []
    given = {name: _np.ascontiguousarray(inputs[name]) for name in _INS}
    given["table_f32"], given["table_bf16"] = constants()
    for name, a in given.items():
        arrays[f"in_{name}"] = a
        args.append(nc.dram_tensor(f"in_{name}", a.shape, _mybir.dt.from_np(a.dtype), kind="ExternalInput").ap())
    args.append(nc.dram_tensor("out_0", (1, S, E), F32, kind="ExternalOutput").ap())
    attention_moe(nc, *args)
    r = _run(nc, [arrays], core_ids=[0])
    return r.results[0]["out_0"]
```
